# Optimizing a Trainium2 kernel written in Bass

```python
import numpy as np
import jax
import jax.numpy as jnp

def _softmax(x, axis=-1):
    return jax.nn.softmax(x, axis=axis)

def _gelu(x):
    return jax.nn.gelu(x, approximate=True)

def _silu(x):
    return jax.nn.silu(x)

def _sigmoid(x):
    return jax.nn.sigmoid(x)

def _layernorm(x, axis=-1, eps=1e-05):
    m = jnp.mean(x, axis=axis, keepdims=True)
    v = jnp.var(x, axis=axis, keepdims=True)
    return (x - m) / jnp.sqrt(v + eps)

def _scatter_add(tgt, idx, src, axis=0):
    return tgt.at[idx].add(src)

def _segment_sum(src, seg, n):
    return jax.ops.segment_sum(src, seg, n)
kernel_name = 'mk_seq_postln_d4_jaxref_r8_6eb67b'

def setup_inputs(seed: int=0):
    np.random.seed(seed)
    _w = jnp.asarray

    def _L0_attn_setup():
        import jax, jax.numpy as jnp
        import numpy as np
        INDIM = 128
        NHEADS = 16
        DK = INDIM // NHEADS
        DV = INDIM // NHEADS
        B, S = (4, 256)
        key = jax.random.key(seed)
        ks = jax.random.split(key, 5)
        x = jax.random.normal(ks[0], (B, S, INDIM), dtype=jnp.float32)
        std_qk = np.sqrt(2.0 / (INDIM + DK)).astype(np.float32)
        std_v = np.sqrt(2.0 / (INDIM + DV)).astype(np.float32)
        Wq = jax.random.normal(ks[1], (NHEADS * DK, INDIM), dtype=jnp.float32) * std_qk
        Wk = jax.random.normal(ks[2], (NHEADS * DK, INDIM), dtype=jnp.float32) * std_qk
        Wv = jax.random.normal(ks[3], (NHEADS * DV, INDIM), dtype=jnp.float32) * std_v
        std_o = np.sqrt(2.0 / (NHEADS * DV + INDIM)).astype(np.float32)
        Wo = jax.random.normal(ks[4], (INDIM, NHEADS * DV), dtype=jnp.float32) * std_o
        bq = jnp.zeros((NHEADS * DK,), jnp.float32)
        bk = jnp.zeros((NHEADS * DK,), jnp.float32)
        bv = jnp.zeros((NHEADS * DV,), jnp.float32)
        bo = jnp.zeros((INDIM,), jnp.float32)
        return {'x': x, 'Wq': Wq, 'bq': bq, 'Wk': Wk, 'bk': bk, 'Wv': Wv, 'bv': bv, 'Wo': Wo, 'bo': bo}
    _L0_attn_in = _L0_attn_setup()

    def _L0_ffn_setup():
        import jax, jax.numpy as jnp
        import numpy as np
        B, S, D = (4, 256, 128)
        E, F, K = (8, 512, 2)

        def _moe(x, router_w, w1, b1, w2, b2):
            logits = jnp.einsum('bsd,de->bse', x, router_w)
            top_logits, indices = jax.lax.top_k(logits, K)
            weights = jax.nn.softmax(top_logits, axis=-1)
            h = jnp.einsum('bsd,edf->ebsf', x, w1) + b1[:, None, None, :]
            h = jax.nn.gelu(h)
            stacked = jnp.einsum('ebsf,efd->ebsd', h, w2) + b2[:, None, None, :]
            per_token = jnp.moveaxis(stacked, 0, 2)
            selected = jnp.take_along_axis(per_token, indices[..., None], axis=2)
            return jnp.einsum('bskf,bsk->bsf', selected, weights)
        key = jax.random.key(seed)
        ks = jax.random.split(key, 4)
        scale_in = 1.0 / np.sqrt(D)
        scale_hid = 1.0 / np.sqrt(F)
        return {'x': jax.random.normal(ks[0], (B, S, D), dtype=jnp.float32), 'router_w': jax.random.normal(ks[1], (D, E), dtype=jnp.float32) * scale_in, 'w1': jax.random.normal(ks[2], (E, D, F), dtype=jnp.float32) * scale_in, 'b1': jnp.zeros((E, F), dtype=jnp.float32), 'w2': jax.random.normal(ks[3], (E, F, D), dtype=jnp.float32) * scale_hid, 'b2': jnp.zeros((E, D), dtype=jnp.float32)}
    _L0_ffn_in = _L0_ffn_setup()

    def _L1_attn_setup():
        import jax, jax.numpy as jnp
        import numpy as np
        B, S, D = (8, 256, 128)
        key = jax.random.key(seed)
        kx, kw, kb = jax.random.split(key, 3)
        x = jax.random.normal(kx, (B, S, D), dtype=jnp.float32)
        W = jax.random.normal(kw, (3 * D, D), dtype=jnp.float32) * (1.0 / np.sqrt(D))
        b = jax.random.normal(kb, (3 * D,), dtype=jnp.float32) * 0.01
        return {'x': x, 'W': W, 'b': b}
    _L1_attn_in = _L1_attn_setup()

    def _L1_ffn_setup():
        import jax, jax.numpy as jnp
        import numpy as np
        DIM = 128

        def _reference_tuple_inner(x, W_r, W_k, W_v, mu_r, mu_k):
            B, T, C = x.shape
            x_prev = jnp.concatenate([jnp.zeros((B, 1, C), x.dtype), x[:, :-1, :]], axis=1)
            xr = mu_r * x + (1.0 - mu_r) * x_prev
            xk = mu_k * x + (1.0 - mu_k) * x_prev
            r = jax.nn.sigmoid(jnp.einsum('btc,dc->btd', xr, W_r))
            k = jnp.einsum('btc,dc->btd', xk, W_k)
            k_act = jnp.square(jax.nn.relu(k))
            out = r * jnp.einsum('btc,dc->btd', k_act, W_v)
            new_state = x[:, -1, :]
            return (out, new_state)
        key = jax.random.key(seed)
        ks = jax.random.split(key, 6)
        B, T, C = (8, 256, DIM)
        x = jax.random.normal(ks[0], (B, T, C), dtype=jnp.float32)
        s = 1.0 / np.sqrt(C)
        W_r = jax.random.uniform(ks[1], (C, C), jnp.float32, -s, s)
        W_k = jax.random.uniform(ks[2], (C, C), jnp.float32, -s, s)
        W_v = jax.random.uniform(ks[3], (C, C), jnp.float32, -s, s)
        mu_r = jax.random.uniform(ks[4], (C,), jnp.float32)
        mu_k = jax.random.uniform(ks[5], (C,), jnp.float32)
        return {'x': x, 'W_r': W_r, 'W_k': W_k, 'W_v': W_v, 'mu_r': mu_r, 'mu_k': mu_k}
    _L1_ffn_in = _L1_ffn_setup()

    def _L2_attn_setup():
        import jax, jax.numpy as jnp
        import numpy as np
        D_MODEL = 128
        N_HEADS = 16
        D_HEAD = D_MODEL // N_HEADS
        BLOCK = 128
        B, T = (2, 256)

        def _flash_attention(Q, K, V, block_size, scale):
            Bb, H, Tt, d = Q.shape
            n_blocks = Tt // block_size
            Kb = K.reshape(Bb, H, n_blocks, block_size, d).transpose(2, 0, 1, 3, 4)
            Vb = V.reshape(Bb, H, n_blocks, block_size, d).transpose(2, 0, 1, 3, 4)
            starts = jnp.arange(n_blocks) * block_size
            q_pos = jnp.arange(Tt)

            def step(carry, xs):
                m, l, acc = carry
                kb, vb, st = xs
                scores = scale * jnp.einsum('bhtd,bhsd->bhts', Q, kb)
                kv_pos = st + jnp.arange(block_size)
                future = kv_pos[None, :] > q_pos[:, None]
                scores = jnp.where(future[None, None], -jnp.inf, scores)
                m_new = jnp.maximum(m, jnp.max(scores, axis=-1, keepdims=True))
                p = jnp.exp(scores - m_new)
                corr = jnp.exp(m - m_new)
                l = corr * l + jnp.sum(p, axis=-1, keepdims=True)
                acc = corr * acc + jnp.einsum('bhts,bhsd->bhtd', p, vb)
                return ((m_new, l, acc), None)
            m0 = jnp.full((Bb, H, Tt, 1), -jnp.inf, dtype=jnp.float32)
            l0 = jnp.zeros((Bb, H, Tt, 1), dtype=jnp.float32)
            a0 = jnp.zeros((Bb, H, Tt, d), dtype=jnp.float32)
            (m, l, acc), _ = jax.lax.scan(step, (m0, l0, a0), (Kb, Vb, starts))
            return acc / jnp.maximum(l, 1e-12)
        key = jax.random.key(seed)
        ks = jax.random.split(key, 5)
        x = jax.random.normal(ks[0], (B, T, D_MODEL), dtype=jnp.float32)

        def init_w(k):
            return jax.random.normal(k, (D_MODEL, D_MODEL), dtype=jnp.float32) / np.sqrt(D_MODEL).astype(np.float32)
        return {'x': x, 'Wq': init_w(ks[1]), 'Wk': init_w(ks[2]), 'Wv': init_w(ks[3]), 'Wo': init_w(ks[4])}
    _L2_attn_in = _L2_attn_setup()

    def _L2_ffn_setup():
        import jax, jax.numpy as jnp
        import numpy as np
        DIM = 128

        def _reference_tuple_inner(x, W_r, W_k, W_v, mu_r, mu_k):
            B, T, C = x.shape
            x_prev = jnp.concatenate([jnp.zeros((B, 1, C), x.dtype), x[:, :-1, :]], axis=1)
            xr = mu_r * x + (1.0 - mu_r) * x_prev
            xk = mu_k * x + (1.0 - mu_k) * x_prev
            r = jax.nn.sigmoid(jnp.einsum('btc,dc->btd', xr, W_r))
            k = jnp.einsum('btc,dc->btd', xk, W_k)
            k_act = jnp.square(jax.nn.relu(k))
            out = r * jnp.einsum('btc,dc->btd', k_act, W_v)
            new_state = x[:, -1, :]
            return (out, new_state)
        key = jax.random.key(seed)
        ks = jax.random.split(key, 6)
        B, T, C = (8, 256, DIM)
        x = jax.random.normal(ks[0], (B, T, C), dtype=jnp.float32)
        s = 1.0 / np.sqrt(C)
        W_r = jax.random.uniform(ks[1], (C, C), jnp.float32, -s, s)
        W_k = jax.random.uniform(ks[2], (C, C), jnp.float32, -s, s)
        W_v = jax.random.uniform(ks[3], (C, C), jnp.float32, -s, s)
        mu_r = jax.random.uniform(ks[4], (C,), jnp.float32)
        mu_k = jax.random.uniform(ks[5], (C,), jnp.float32)
        return {'x': x, 'W_r': W_r, 'W_k': W_k, 'W_v': W_v, 'mu_r': mu_r, 'mu_k': mu_k}
    _L2_ffn_in = _L2_ffn_setup()

    def _L3_attn_setup():
        import jax, jax.numpy as jnp
        import numpy as np
        from jax import lax

        def _phi(x):
            return jax.nn.elu(x) + 1.0
        key = jax.random.key(seed)
        ks = jax.random.split(key, 5)
        B, T, D, H = (8, 512, 128, 64)
        x = jax.random.normal(ks[0], (B, T, D), dtype=jnp.float32)
        W_q = jax.random.normal(ks[1], (D, H), dtype=jnp.float32) * (1.0 / np.sqrt(D))
        W_k = jax.random.normal(ks[2], (D, H), dtype=jnp.float32) * (1.0 / np.sqrt(D))
        W_v = jax.random.normal(ks[3], (D, H), dtype=jnp.float32) * (1.0 / np.sqrt(D))
        W_o = jax.random.normal(ks[4], (H, D), dtype=jnp.float32) * (1.0 / np.sqrt(H))
        return {'x': x, 'W_q': W_q, 'W_k': W_k, 'W_v': W_v, 'W_o': W_o}
    _L3_attn_in = _L3_attn_setup()

    def _L3_ffn_setup():
        import jax, jax.numpy as jnp
        import numpy as np
        import math
        D_MODEL = 128
        N_EXPERTS = 16
        D_FF = 512
        CAP_FACTOR = 1.25
        MIN_CAPACITY = 4

        def _capacity(num_tokens, num_experts):
            cap = math.floor(CAP_FACTOR * num_tokens / num_experts)
            cap += cap % 2
            return max(cap, MIN_CAPACITY)

        def _top1_router(gate_logits, capacity):
            s, e = gate_logits.shape
            probs = jax.nn.softmax(gate_logits, axis=-1)
            top1 = jnp.argmax(gate_logits, axis=-1)
            mask = jax.nn.one_hot(top1, e, dtype=jnp.int32)
            ranks = jnp.cumsum(mask, axis=0) - 1
            mask = mask * (ranks < capacity).astype(jnp.int32)
            rank1 = jnp.sum(mask * ranks, axis=-1)
            ranks_oh = jax.nn.one_hot(rank1, capacity, dtype=probs.dtype)
            weight = mask.astype(probs.dtype) * probs
            combine_weights = weight[:, :, None] * ranks_oh[:, None, :]
            sec_mask = combine_weights > 0
            return (combine_weights, sec_mask)
        key = jax.random.key(seed)
        k1, k2, k3, k4 = jax.random.split(key, 4)
        x = jax.random.normal(k1, (4, 256, D_MODEL), dtype=jnp.float32)
        gate_w = jax.random.normal(k2, (N_EXPERTS, D_MODEL), dtype=jnp.float32) * math.sqrt(0.1 / D_MODEL)
        w1 = jax.random.normal(k3, (N_EXPERTS, D_MODEL, D_FF), dtype=jnp.float32) * (1.0 / math.sqrt(D_MODEL))
        w2 = jax.random.normal(k4, (N_EXPERTS, D_FF, D_MODEL), dtype=jnp.float32) * (1.0 / math.sqrt(D_FF))
        return {'x': x, 'gate_w': gate_w, 'w1': w1, 'w2': w2}
    _L3_ffn_in = _L3_ffn_setup()
    _d = {'L0_attn_x': _L0_attn_in['x'], 'L0_attn_Wq': _L0_attn_in['Wq'], 'L0_attn_bq': _L0_attn_in['bq'], 'L0_attn_Wk': _L0_attn_in['Wk'], 'L0_attn_bk': _L0_attn_in['bk'], 'L0_attn_Wv': _L0_attn_in['Wv'], 'L0_attn_bv': _L0_attn_in['bv'], 'L0_attn_Wo': _L0_attn_in['Wo'], 'L0_attn_bo': _L0_attn_in['bo'], 'L0_ffn_router_w': _L0_ffn_in['router_w'], 'L0_ffn_w1': _L0_ffn_in['w1'], 'L0_ffn_b1': _L0_ffn_in['b1'], 'L0_ffn_w2': _L0_ffn_in['w2'], 'L0_ffn_b2': _L0_ffn_in['b2'], 'L1_attn_W': _L1_attn_in['W'], 'L1_attn_b': _L1_attn_in['b'], 'L1_ffn_W_r': _L1_ffn_in['W_r'], 'L1_ffn_W_k': _L1_ffn_in['W_k'], 'L1_ffn_W_v': _L1_ffn_in['W_v'], 'L1_ffn_mu_r': _L1_ffn_in['mu_r'], 'L1_ffn_mu_k': _L1_ffn_in['mu_k'], 'L2_attn_Wq': _L2_attn_in['Wq'], 'L2_attn_Wk': _L2_attn_in['Wk'], 'L2_attn_Wv': _L2_attn_in['Wv'], 'L2_attn_Wo': _L2_attn_in['Wo'], 'L2_ffn_W_r': _L2_ffn_in['W_r'], 'L2_ffn_W_k': _L2_ffn_in['W_k'], 'L2_ffn_W_v': _L2_ffn_in['W_v'], 'L2_ffn_mu_r': _L2_ffn_in['mu_r'], 'L2_ffn_mu_k': _L2_ffn_in['mu_k'], 'L3_attn_W_q': _L3_attn_in['W_q'], 'L3_attn_W_k': _L3_attn_in['W_k'], 'L3_attn_W_v': _L3_attn_in['W_v'], 'L3_attn_W_o': _L3_attn_in['W_o'], 'L3_ffn_gate_w': _L3_ffn_in['gate_w'], 'L3_ffn_w1': _L3_ffn_in['w1'], 'L3_ffn_w2': _L3_ffn_in['w2']}
    _x0 = _d['L0_attn_x']
    _d['L0_attn_x'] = jax.random.normal(jax.random.fold_in(jax.random.key(seed), 1), (16, 256, 128), dtype=_x0.dtype)
    del _x0
    return _d

def reference(L0_attn_x, L0_attn_Wq, L0_attn_bq, L0_attn_Wk, L0_attn_bk, L0_attn_Wv, L0_attn_bv, L0_attn_Wo, L0_attn_bo, L0_ffn_router_w, L0_ffn_w1, L0_ffn_b1, L0_ffn_w2, L0_ffn_b2, L1_attn_W, L1_attn_b, L1_ffn_W_r, L1_ffn_W_k, L1_ffn_W_v, L1_ffn_mu_r, L1_ffn_mu_k, L2_attn_Wq, L2_attn_Wk, L2_attn_Wv, L2_attn_Wo, L2_ffn_W_r, L2_ffn_W_k, L2_ffn_W_v, L2_ffn_mu_r, L2_ffn_mu_k, L3_attn_W_q, L3_attn_W_k, L3_attn_W_v, L3_attn_W_o, L3_ffn_gate_w, L3_ffn_w1, L3_ffn_w2):

    def _L0_attn_ref(x, Wq, bq, Wk, bk, Wv, bv, Wo, bo):
        import jax, jax.numpy as jnp
        import numpy as np
        INDIM = 128
        NHEADS = 16
        DK = INDIM // NHEADS
        DV = INDIM // NHEADS
        B, S = (4, 256)
        b, s, _ = x.shape
        q = (x @ Wq.T + bq).reshape(b, s, NHEADS, DK)
        k = (x @ Wk.T + bk).reshape(b, s, NHEADS, DK)
        v = (x @ Wv.T + bv).reshape(b, s, NHEADS, DV)
        w = jnp.einsum('bshd,bzhd->bhsz', q, k)
        w = w / jnp.sqrt(jnp.float32(DV))
        w = jax.nn.softmax(w, axis=-1)
        vw = jnp.einsum('bhsz,bzhd->bshd', w, v)
        vw = vw.reshape(b, s, NHEADS * DV)
        out = vw @ Wo.T + bo
        return out

    def _L0_ffn_ref(x, router_w, w1, b1, w2, b2):
        import jax, jax.numpy as jnp
        import numpy as np
        B, S, D = (4, 256, 128)
        E, F, K = (8, 512, 2)

        def _moe(x, router_w, w1, b1, w2, b2):
            logits = jnp.einsum('bsd,de->bse', x, router_w)
            top_logits, indices = jax.lax.top_k(logits, K)
            weights = jax.nn.softmax(top_logits, axis=-1)
            h = jnp.einsum('bsd,edf->ebsf', x, w1) + b1[:, None, None, :]
            h = jax.nn.gelu(h)
            stacked = jnp.einsum('ebsf,efd->ebsd', h, w2) + b2[:, None, None, :]
            per_token = jnp.moveaxis(stacked, 0, 2)
            selected = jnp.take_along_axis(per_token, indices[..., None], axis=2)
            return jnp.einsum('bskf,bsk->bsf', selected, weights)
        return _moe(x, router_w, w1, b1, w2, b2)

    def _L1_attn_ref(x, W, b):
        import jax, jax.numpy as jnp
        import numpy as np
        B, S, D = (8, 256, 128)
        qkv = jnp.einsum('bsd,fd->bsf', x, W) + b
        q, k, v = jnp.split(qkv, 3, axis=-1)
        attn = jnp.einsum('bik,bjk->bij', q, k) / k.shape[-1]
        attn = jax.nn.softmax(attn, axis=1)
        out = jnp.einsum('bij,bjk->bik', attn, v)
        return out

    def _L1_ffn_ref(x, W_r, W_k, W_v, mu_r, mu_k):
        import jax, jax.numpy as jnp
        import numpy as np
        DIM = 128

        def _reference_tuple_inner(x, W_r, W_k, W_v, mu_r, mu_k):
            B, T, C = x.shape
            x_prev = jnp.concatenate([jnp.zeros((B, 1, C), x.dtype), x[:, :-1, :]], axis=1)
            xr = mu_r * x + (1.0 - mu_r) * x_prev
            xk = mu_k * x + (1.0 - mu_k) * x_prev
            r = jax.nn.sigmoid(jnp.einsum('btc,dc->btd', xr, W_r))
            k = jnp.einsum('btc,dc->btd', xk, W_k)
            k_act = jnp.square(jax.nn.relu(k))
            out = r * jnp.einsum('btc,dc->btd', k_act, W_v)
            new_state = x[:, -1, :]
            return (out, new_state)
        return _reference_tuple_inner(x, W_r, W_k, W_v, mu_r, mu_k)[0]

    def _L2_attn_ref(x, Wq, Wk, Wv, Wo):
        import jax, jax.numpy as jnp
        import numpy as np
        D_MODEL = 128
        N_HEADS = 16
        D_HEAD = D_MODEL // N_HEADS
        BLOCK = 128
        B, T = (2, 256)

        def _flash_attention(Q, K, V, block_size, scale):
            Bb, H, Tt, d = Q.shape
            n_blocks = Tt // block_size
            Kb = K.reshape(Bb, H, n_blocks, block_size, d).transpose(2, 0, 1, 3, 4)
            Vb = V.reshape(Bb, H, n_blocks, block_size, d).transpose(2, 0, 1, 3, 4)
            starts = jnp.arange(n_blocks) * block_size
            q_pos = jnp.arange(Tt)

            def step(carry, xs):
                m, l, acc = carry
                kb, vb, st = xs
                scores = scale * jnp.einsum('bhtd,bhsd->bhts', Q, kb)
                kv_pos = st + jnp.arange(block_size)
                future = kv_pos[None, :] > q_pos[:, None]
                scores = jnp.where(future[None, None], -jnp.inf, scores)
                m_new = jnp.maximum(m, jnp.max(scores, axis=-1, keepdims=True))
                p = jnp.exp(scores - m_new)
                corr = jnp.exp(m - m_new)
                l = corr * l + jnp.sum(p, axis=-1, keepdims=True)
                acc = corr * acc + jnp.einsum('bhts,bhsd->bhtd', p, vb)
                return ((m_new, l, acc), None)
            m0 = jnp.full((Bb, H, Tt, 1), -jnp.inf, dtype=jnp.float32)
            l0 = jnp.zeros((Bb, H, Tt, 1), dtype=jnp.float32)
            a0 = jnp.zeros((Bb, H, Tt, d), dtype=jnp.float32)
            (m, l, acc), _ = jax.lax.scan(step, (m0, l0, a0), (Kb, Vb, starts))
            return acc / jnp.maximum(l, 1e-12)
        Bx, Tx, _ = x.shape
        scale = 1.0 / np.sqrt(D_HEAD).astype(np.float32)

        def proj(W):
            y = jnp.einsum('btm,nm->btn', x, W)
            return y.reshape(Bx, Tx, N_HEADS, D_HEAD).transpose(0, 2, 1, 3)
        Q, K, V = (proj(Wq), proj(Wk), proj(Wv))
        O = _flash_attention(Q.astype(jnp.float32), K.astype(jnp.float32), V.astype(jnp.float32), BLOCK, scale)
        O = O.astype(x.dtype).transpose(0, 2, 1, 3).reshape(Bx, Tx, D_MODEL)
        return jnp.einsum('btm,nm->btn', O, Wo)

    def _L2_ffn_ref(x, W_r, W_k, W_v, mu_r, mu_k):
        import jax, jax.numpy as jnp
        import numpy as np
        DIM = 128

        def _reference_tuple_inner(x, W_r, W_k, W_v, mu_r, mu_k):
            B, T, C = x.shape
            x_prev = jnp.concatenate([jnp.zeros((B, 1, C), x.dtype), x[:, :-1, :]], axis=1)
            xr = mu_r * x + (1.0 - mu_r) * x_prev
            xk = mu_k * x + (1.0 - mu_k) * x_prev
            r = jax.nn.sigmoid(jnp.einsum('btc,dc->btd', xr, W_r))
            k = jnp.einsum('btc,dc->btd', xk, W_k)
            k_act = jnp.square(jax.nn.relu(k))
            out = r * jnp.einsum('btc,dc->btd', k_act, W_v)
            new_state = x[:, -1, :]
            return (out, new_state)
        return _reference_tuple_inner(x, W_r, W_k, W_v, mu_r, mu_k)[0]

    def _L3_attn_ref(x, W_q, W_k, W_v, W_o):
        import jax, jax.numpy as jnp
        import numpy as np
        from jax import lax

        def _phi(x):
            return jax.nn.elu(x) + 1.0
        B, T, D = x.shape
        H = W_q.shape[1]
        q = _phi(jnp.einsum('btd,dh->bth', x, W_q))
        k = _phi(jnp.einsum('btd,dh->bth', x, W_k))
        v = jnp.einsum('btd,dh->bth', x, W_v)
        qT = jnp.swapaxes(q, 0, 1)
        kT = jnp.swapaxes(k, 0, 1)
        vT = jnp.swapaxes(v, 0, 1)
        S0 = jnp.zeros((B, H, H), dtype=x.dtype)
        z0 = jnp.zeros((B, H), dtype=x.dtype)

        def step(carry, inp):
            S, z = carry
            q_t, k_t, v_t = inp
            S = S + k_t[:, :, None] * v_t[:, None, :]
            z = z + k_t
            o_t = jnp.einsum('bij,bj->bi', S, q_t)
            denom = jnp.maximum(jnp.sum(z * q_t, axis=-1, keepdims=True), 1e-06)
            return ((S, z), o_t / denom)
        (_, _), oT = lax.scan(step, (S0, z0), (qT, kT, vT))
        o = jnp.swapaxes(oT, 0, 1)
        return jnp.einsum('bth,hd->btd', o, W_o)

    def _L3_ffn_ref(x, gate_w, w1, w2):
        import jax, jax.numpy as jnp
        import numpy as np
        import math
        D_MODEL = 128
        N_EXPERTS = 16
        D_FF = 512
        CAP_FACTOR = 1.25
        MIN_CAPACITY = 4

        def _capacity(num_tokens, num_experts):
            cap = math.floor(CAP_FACTOR * num_tokens / num_experts)
            cap += cap % 2
            return max(cap, MIN_CAPACITY)

        def _top1_router(gate_logits, capacity):
            s, e = gate_logits.shape
            probs = jax.nn.softmax(gate_logits, axis=-1)
            top1 = jnp.argmax(gate_logits, axis=-1)
            mask = jax.nn.one_hot(top1, e, dtype=jnp.int32)
            ranks = jnp.cumsum(mask, axis=0) - 1
            mask = mask * (ranks < capacity).astype(jnp.int32)
            rank1 = jnp.sum(mask * ranks, axis=-1)
            ranks_oh = jax.nn.one_hot(rank1, capacity, dtype=probs.dtype)
            weight = mask.astype(probs.dtype) * probs
            combine_weights = weight[:, :, None] * ranks_oh[:, None, :]
            sec_mask = combine_weights > 0
            return (combine_weights, sec_mask)
        tokens = x.reshape(-1, D_MODEL)
        s = tokens.shape[0]
        capacity = _capacity(s, N_EXPERTS)
        gate_logits = tokens.astype(jnp.float32) @ gate_w.T
        combine_weights, sec_mask = _top1_router(gate_logits, capacity)
        dispatch = jnp.einsum('sec,sd->ecd', sec_mask.astype(tokens.dtype), tokens)
        h = jax.nn.gelu(jnp.einsum('ecd,edf->ecf', dispatch, w1))
        expert_out = jnp.einsum('ecf,efd->ecd', h, w2)
        out = jnp.einsum('sec,ecd->sd', combine_weights.astype(tokens.dtype), expert_out)
        return out.reshape(x.shape)
    x = L0_attn_x
    x = _layernorm(x + _L0_attn_ref(x, L0_attn_Wq, L0_attn_bq, L0_attn_Wk, L0_attn_bk, L0_attn_Wv, L0_attn_bv, L0_attn_Wo, L0_attn_bo), axis=-1)
    x = _layernorm(x + _L0_ffn_ref(x, L0_ffn_router_w, L0_ffn_w1, L0_ffn_b1, L0_ffn_w2, L0_ffn_b2), axis=-1)
    x = _layernorm(x + _L1_attn_ref(x, L1_attn_W, L1_attn_b), axis=-1)
    x = _layernorm(x + _L1_ffn_ref(x, L1_ffn_W_r, L1_ffn_W_k, L1_ffn_W_v, L1_ffn_mu_r, L1_ffn_mu_k), axis=-1)
    x = _layernorm(x + _L2_attn_ref(x, L2_attn_Wq, L2_attn_Wk, L2_attn_Wv, L2_attn_Wo), axis=-1)
    x = _layernorm(x + _L2_ffn_ref(x, L2_ffn_W_r, L2_ffn_W_k, L2_ffn_W_v, L2_ffn_mu_r, L2_ffn_mu_k), axis=-1)
    x = _layernorm(x + _L3_attn_ref(x, L3_attn_W_q, L3_attn_W_k, L3_attn_W_v, L3_attn_W_o), axis=-1)
    x = _layernorm(x + _L3_ffn_ref(x, L3_ffn_gate_w, L3_ffn_w1, L3_ffn_w2), axis=-1)
    return x

_drawn_inputs = setup_inputs


def setup_inputs(seed=0):
    import zlib

    import numpy as np

    out = dict(_drawn_inputs(seed))
    spreads = {'L0_attn_bq': (0.0, 0.1),
     'L0_attn_bk': (0.0, 0.8),
     'L0_attn_bv': (0.0, 0.1),
     'L0_attn_bo': (0.0, 0.1),
     'L0_ffn_b1': (0.0, 0.1),
     'L0_ffn_b2': (0.0, 0.1)}
    factors = {'L1_attn_b': 3.049,
     'L1_ffn_W_r': 2.829,
     'L1_ffn_mu_r': 5.451,
     'L2_ffn_W_r': 2.709,
     'L2_ffn_mu_r': 5.449}
    for name, (base, spread) in spreads.items():
        noise = np.random.default_rng([zlib.crc32(name.encode()), seed]).standard_normal(out[name].shape)
        drawn = base * np.exp(spread * noise) if base else spread * noise
        out[name] = jnp.asarray(drawn.astype(out[name].dtype))
    for name, factor in factors.items():
        out[name] = (out[name] * factor).astype(out[name].dtype)
    return out
```

```python
from contextlib import ExitStack

import numpy as np

import concourse.bass as bass
from concourse import mybir

P = 128
D = 128
SEQS = 16
S = 256
TILES = SEQS * S // P
HEADS = 16
DH = D // HEADS
SLOTS = 4
EPS = 1e-5

E0 = 8
F = 512
FC = F // P
CAP0 = SEQS * S
ROOM0 = CAP0 + S
GROUPS0 = 2 * SEQS + E0 - 1
E3 = 16
CAP3 = 320
HIDE = -1e30

F32 = mybir.dt.float32
BF16 = mybir.dt.bfloat16
I32 = mybir.dt.int32
U32 = mybir.dt.uint32
ALU = mybir.AluOpType
ACT = mybir.ActivationFunctionType
AX = mybir.AxisListType

MATS = ["q0", "k0", "v0", "o0", "q1", "k1", "v1", "r1", "m1", "w1", "q2", "k2", "v2", "o2",
        "r2", "m2", "w2"]
COLS = ["bq0", "bk0", "bq1", "bk1", "mr1", "mk1", "mr2", "mk2"]
ROWS = ["bv0", "bo0", "bv1"]


class Seq:

    def __init__(self, n, slot, least, turn):
        self.n, self.slot, self.least, self.turn = n, slot, least, turn

    def back(self, k):
        return self.n - (k if isinstance(self.n, int) else min(k, self.least))


def sweep(eng, lags, step, n=SEQS, lead=0):
    def peeled(s):
        step(lambda k: Seq(s - k, (s - k) % SLOTS, s - k, (s - k) // SLOTS) if 0 <= s - k < n else None)

    first = lags - 1 + lead
    full = n - first
    for s in range(first):
        peeled(s)
    with eng.Fori(0, full // SLOTS) as i:
        for c in range(SLOTS):
            s0 = first + c
            step(lambda k: Seq(SLOTS * i + (s0 - k), (s0 - k) % SLOTS, s0 - k,
                               i + (s0 - k) // SLOTS))
    for s in range(first + full // SLOTS * SLOTS, n + lags - 1):
        peeled(s)


def wait(eng, sem, n):
    if isinstance(n, int) and n <= 0:
        return
    eng.wait_ge(sem, n)


def wait_apart(eng, sem, n, passed):
    wait(eng, sem, n)
    eng.sem_inc(passed, 1)


def post_norm_stack(nc, x, mats, cols, rows, router0, w1_0, b1_0, w2_0, b2_0,
                    w_l3, wo_l3, gate, w1_3, w2_3, out):
    with ExitStack() as ctx:
        def sb(name, shape, dt=F32, at=ctx):
            return at.enter_context(nc.sbuf_tensor(name, shape, dt))

        def sem(name):
            return ctx.enter_context(nc.semaphore(name))

        xg = sb("xg", [P, TILES, D])
        wm = sb("wm", [P, len(MATS), D])
        cv = sb("cv", [P, len(COLS)])
        row1 = sb("row1", [1, len(ROWS) * D])
        rowb = sb("rowb", [P, len(ROWS), D])
        ident = sb("ident", [P, P])
        ident16 = sb("ident16", [P, P], BF16)
        ones = sb("ones", [P, P])
        upto = sb("upto", [P, 2, P])
        hide_k = sb("hide_k", [P, P], BF16)
        hide_q = sb("hide_q", [P, P], BF16)
        half = sb("half", [P, 2])
        omu = sb("omu", [P, 4])
        xs = [sb(f"xs{i}", [P, 2, D]) for i in range(SLOTS)]
        xt = [sb(f"xt{i}", [P, 1 + S]) for i in range(SLOTS)]
        res = [sb(f"res{i}", [P, 2, D]) for i in range(SLOTS)]
        st = [sb(f"st{i}", [P, 2, 6]) for i in range(SLOTS)]
        mv = [sb(f"mv{i}", [P, 2, 2]) for i in range(SLOTS)]
        ve = [sb(f"ve{i}", [P, 2, 1]) for i in range(SLOTS)]
        rstd = [sb(f"rstd{i}", [P, 2, 1]) for i in range(SLOTS)]
        zero_col = sb("zero_col", [P, 1])

        EM = max(E0, E3)
        NG = GROUPS0 + 1
        LD = 64
        rw0 = sb("rw0", [P, E0])
        rw3 = sb("rw3", [P, E3])
        wl = sb("wl", [P, 3, LD])
        wo = sb("wo", [P, D])
        iota_e = sb("iota_e", [P, EM])
        iota_g = sb("iota_g", [P, NG])
        base0 = sb("base0", [P, 2, E0])
        base3 = sb("base3", [P, 2, E3])
        dump = sb("dump", [P, TILES])
        upto16 = sb("upto16", [P, P], BF16)
        ones16 = sb("ones16", [P, P], BF16)
        zt = sb("zt", [P, CAP3])
        ks = [sb(f"ks{i}", [51, HEADS, S], BF16) for i in range(SLOTS)]
        va = [sb(f"va{i}", [P, 2, HEADS, 32]) for i in range(SLOTS)]

        with ExitStack() as mem:
            qs = [sb(f"qs{i}", [51, HEADS, S], BF16, mem) for i in range(SLOTS)]
            ex = [sb(f"ex{i}", [P, 4, S], F32, mem) for i in range(2)]
            qk = [sb(f"qk{i}", [P, 2, S], F32, mem) for i in range(2)]
            rem = [sb(f"rem{i}", [P, 2, S], F32, mem) for i in range(2)]
            parts = [sb(f"parts{i}", [P, 3, 2, S], BF16, mem) for i in range(2)]
            mx = [sb(f"mx{i}", [P, 2, HEADS], F32, mem) for i in range(2)]
            mr = [sb(f"mr{i}", [P, 2, HEADS], F32, mem) for i in range(2)]
            mp = [sb(f"mp{i}", [P, 2, 3, HEADS], BF16, mem) for i in range(2)]
            mt = [sb(f"mt{i}", [96, P], BF16, mem) for i in range(2)]
            ob = sb("ob", [P, 4, S], F32, mem)
            rc = [sb(f"rc{i}", [P, 2, HEADS], F32, mem) for i in range(2)]
            on = [sb(f"on{i}", [P, 2, D], F32, mem) for i in range(2)]
            ont = [sb(f"ont{i}", [P, S], F32, mem) for i in range(2)]
            xb = [sb(f"xb{i}", [P, 2, D], F32, mem) for i in range(SLOTS)]

        scr = nc.dram_tensor("scr", (SLOTS, 2, 3, P, S), BF16).ap()

        def psum(name, shape, dt=F32):
            return ctx.enter_context(nc.psum_tensor(name, shape, dt))

        p0 = psum("p0", [P, 512])
        p1 = psum("p1", [P, 512])
        pt = psum("pt", [P, 2, 512])
        pm = psum("pm", [P, 2, 512])
        po = psum("po", [P, 2, 512])

        passed = sem("passed")
        consts = sem("consts")
        consts_v = sem("consts_v")
        w_in = sem("w_in")
        x_in = sem("x_in")
        rows_ps = sem("rows_ps")
        rows_sb = sem("rows_sb")
        x_loaded = [sem(f"x_loaded{i}") for i in range(SLOTS)]
        xt_ps = sem("xt_ps")
        xt_sb = sem("xt_sb")
        res_sb = sem("res_sb")
        ln_st = sem("ln_st")
        ln_mv = sem("ln_mv")
        ln_ve = sem("ln_ve")
        ln_rs = sem("ln_rs")
        ln_x = sem("ln_x")
        out_done = sem("out_done")
        qk_ps = sem("qk_ps")
        v_ps = sem("v_ps")
        qk_sb = sem("qk_sb")
        v_sb = sem("v_sb")
        part1 = sem("part1")
        rest1 = sem("rest1")
        part2 = sem("part2")
        part3 = sem("part3")
        to_scr = sem("to_scr")
        stacked = [sem(f"stacked{i}") for i in range(SLOTS)]
        ms_ps = sem("ms_ps")
        ms_max = sem("ms_max")
        m_parts = sem("m_parts")
        mt_ps = sem("mt_ps")
        mt_sb = sem("mt_sb")
        mrows = [sem(f"mrows{i}") for i in range(SLOTS)]
        ts_ps = sem("ts_ps")
        e_sb = sem("e_sb")
        pv_ps = sem("pv_ps")
        o_sb = sem("o_sb")
        ot_ps = sem("ot_ps")
        o_rc = sem("o_rc")
        o_rc2 = sem("o_rc2")
        o_nrm = sem("o_nrm")
        ont_ps = sem("ont_ps")
        ont_sb = sem("ont_sb")
        y_ps = sem("y_ps")
        xb_sb = sem("xb_sb")

        W_IN = 16 * 8
        CONSTS = 11
        cleared = sem("cleared")
        SPLITS = 16 * 9

        def mat(name):
            return wm[:, MATS.index(name), :]

        def col(name):
            return cv[:, COLS.index(name):COLS.index(name) + 1]

        def row(name):
            return rowb[:, ROWS.index(name), :]

        def load_x(sp, q, done, normed):
            sp.wait_ge(ln_x, 2 * normed) if normed else sp.wait_ge(x_in, 16)
            wait_apart(sp, xt_ps, done + q.back(3), passed)
            sp.dma_start(xs[q.slot][:, :, :], xg[:, bass.ds(2 * q.n, 2), :]).then_inc(x_loaded[q.slot], 16)

        def transpose_x(pe, q, done):
            pe.wait_ge(x_loaded[q.slot], 16 * (done // SLOTS + q.turn + 1))
            pe.transpose(p0[:, 0:P], xs[q.slot][:, 0, :], ident[:, :])
            pe.transpose(p0[:, P:S], xs[q.slot][:, 1, :], ident[:, :]).then_inc(xt_ps, 1)

        def copy_xt(act, q, done):
            act.wait_ge(xt_ps, done + q.n + 1)
            nc.scalar.copy(xt[q.slot][:, 1:1 + S], p0[:, 0:S]).then_inc(xt_sb, 1)

        def norm_stats(dve, q, done):
            dve.wait_ge(res_sb, done + q.n + 1)
            for t in range(2):
                nc.vector.bn_stats(st[q.slot][:, t, :], res[q.slot][:, t, :]).then_inc(ln_st, 1)
            for t in range(2):
                wait_apart(dve, ln_st, 2 * (done + q.n) + 1 + t, passed)
                nc.vector.bn_aggr(mv[q.slot][:, t, :], st[q.slot][:, t, :]).then_inc(ln_mv, 1)

        def norm_rstd(pool, q, done):
            wait_apart(pool, ln_mv, 2 * (done + q.n + 1), passed)
            nc.gpsimd.tensor_scalar(ve[q.slot][:, :, :], mv[q.slot][:, :, 1:2], EPS, None,
                                    ALU.add).then_inc(ln_ve, 1)
            pool.wait_ge(ln_ve, done + q.n + 1)
            nc.gpsimd.tensor_tensor(rstd[q.slot][:, :, :], ve[q.slot][:, :, :],
                                    half[:, :].unsqueeze(2), ALU.pow).then_inc(ln_rs, 1)

        def norm_apply(dve, q, done):
            dve.wait_ge(ln_rs, done + q.n + 1)
            for t in range(2):
                nc.vector.tensor_scalar(xg[:, bass.ds(2 * q.n + t, 1), :], res[q.slot][:, t:t + 1, :],
                                        mv[q.slot][:, t, 0:1], rstd[q.slot][:, t, :],
                                        ALU.subtract, ALU.mult).then_inc(ln_x, 1)

        def heads_sync(sp, a, g, n):
            def step(at):
                if (q := at(0)):
                    load_x(sp, q, g, n)
                if (q := at(2)):
                    sp.wait_ge(mt_sb, a + q.n + 1)
                    for t in range(2):
                        sp.dma_start(qs[q.slot][48:51, :, t * P:t * P + P],
                                     mt[q.slot % 2][48 * t:48 * t + 48, :]).then_inc(mrows[q.slot], 16)
                if (q := at(0)):
                    sp.wait_ge(part3, a + q.n + 1)
                    for i in range(2):
                        sp.dma_start(scr[q.slot, i].rearrange("t p k -> p t k"),
                                     parts[q.slot % 2][:, :, i, :]).then_inc(to_scr, 16)
                    wait_apart(sp, to_scr, 32 * (a + q.n + 1), passed)
                    wait_apart(sp, ts_ps, 8 * (a + q.back(3)), passed)
                    for i, stack, lists in ((0, qs, ((0, 3), (0, 2), (0, 1))),
                                            (1, ks, ((0, 1), (0, 1), (0, 1), (1, 2), (1, 2), (2, 3)))):
                        at_row = 0
                        for lo, hi in lists:
                            src = scr[q.slot, i, lo:hi].rearrange("t (d h) k -> (t d) h k", h=HEADS)
                            sp.dma_start(stack[q.slot][at_row:at_row + 8 * (hi - lo), :, :],
                                         src).then_inc(stacked[q.slot], 16)
                            at_row += 8 * (hi - lo)
            sweep(sp, 5, step)

        def heads_tensor(pe, a, g, causal, layer):
            def scores_t(q, j):
                b, kt = j // 2, j % 2
                pe.wait_ge(stacked[q.slot], SPLITS * (a // SLOTS + q.turn + 1))
                pe.wait_ge(mrows[q.slot], 32 * (a // SLOTS + q.turn + 1))
                wait(pe, e_sb, 8 * (a + q.n) + j)
                for i in range(4):
                    h = 4 * b + i
                    dst = pt[:, i // 2, (i % 2) * S:(i % 2) * S + S]
                    lhs = ks[q.slot][:, h, kt * P:kt * P + P]
                    rhs = qs[q.slot][:, h, :]
                    if not causal:
                        last = pe.matmul(dst, lhs, rhs, start=True, stop=True)
                        continue
                    d0 = kt * P
                    pe.matmul(dst[:, d0:d0 + P], ident16[:, :], hide_k[:, :], start=True, stop=False)
                    last = pe.matmul(dst[:, d0:d0 + P], lhs, rhs[:, d0:d0 + P], start=False, stop=True)
                    if kt == 0:
                        last = pe.matmul(dst[:, P:S], lhs, rhs[:, P:S], start=True, stop=True)
                last.then_inc(ts_ps, 1)

            def scores_m(q, j):
                b, qt = j // 2, j % 2
                if j == 0:
                    pe.wait_ge(stacked[q.slot], SPLITS * (a // SLOTS + q.turn + 1))
                wait(pe, ms_max, 8 * (a + q.n) + j)
                for i in range(4):
                    h = 4 * b + i
                    dst = pm[:, i // 2, (i % 2) * S:(i % 2) * S + S]
                    lhs = qs[q.slot][0:48, h, qt * P:qt * P + P]
                    rhs = ks[q.slot][0:48, h, :]
                    if not causal:
                        last = pe.matmul(dst, lhs, rhs, start=True, stop=True)
                        continue
                    d0 = qt * P
                    if qt == 1:
                        pe.matmul(dst[:, 0:P], lhs, rhs[:, 0:P], start=True, stop=True)
                    pe.matmul(dst[:, d0:d0 + P], ident16[:, :], hide_q[:, :], start=True, stop=False)
                    last = pe.matmul(dst[:, d0:d0 + P], lhs, rhs[:, d0:d0 + P], start=False, stop=True)
                last.then_inc(ms_ps, 1)

            def times_v(q, j):
                b, kt = j // 2, j % 2
                pe.wait_ge(e_sb, 8 * (a + q.n) + j + 1)
                pe.wait_ge(v_sb, 2 * (a + q.n + 1))
                if j == 0:
                    wait(pe, o_sb, a + q.n)
                lo = kt * P if causal else 0
                for i in range(4):
                    c0 = (b % 2) * S
                    last = pe.matmul(po[32 * i:32 * i + 32, b // 2, c0 + lo:c0 + S],
                                     va[q.slot][:, kt, 4 * b + i, :], ex[j % 2][:, i, lo:S],
                                     start=(kt == 0), stop=(kt == 1))
                last.then_inc(pv_ps, 1)

            def step(at):
                for j in range(8):
                    if (q := at(2) if j >= 2 else at(3)):
                        scores_t(q, (j - 2) % 8)
                    if (q := at(1)):
                        scores_m(q, j)
                    if (q := at(2) if j >= 3 else at(3)):
                        times_v(q, (j - 3) % 8)
                    if j == 0:
                        if (q := at(0)):
                            wait(pe, v_sb, 2 * (a + q.n))
                            wait(pe, ont_sb, a + q.back(3))
                            transpose_x(pe, q, g)
                        if (q := at(2)):
                            wait(pe, res_sb, n_of(layer) + q.back(1))
                            if at(1):
                                pe.wait_ge(qk_sb, 2 * (a + at(1).n + 1))
                            wait_apart(pe, m_parts, 4 * (a + q.n + 1), passed)
                            pe.transpose(p1[0:96, :].bitcast(BF16)[:, 0:P],
                                         mp[q.slot % 2][:, :, :, :].rearrange("p t c h -> p (t c h)"),
                                         ident16[:, :]).then_inc(mt_ps, 1)
                    if j == 1 and (q := at(0)):
                        pe.wait_ge(xt_sb, g + q.n + 1)
                        xq = xt[q.slot][:, 1:1 + S]
                        if at(2):
                            pe.wait_ge(mt_sb, a + at(2).n + 1)
                        else:
                            wait(pe, qk_sb, 2 * (a + q.n))
                        wait(pe, res_sb, n_of(layer) + q.back(3))
                        pe.matmul(p1[:, 0:S], mat(f"q{layer}"), xq, start=True, stop=True)
                        pe.matmul(p1[:, S:2 * S], mat(f"k{layer}"), xq, start=True, stop=True).then_inc(qk_ps, 1)
                        for t in range(2):
                            last = pe.matmul(p0[:, t * P:t * P + P], xq[:, t * P:t * P + P],
                                             mat(f"v{layer}"), start=True, stop=True)
                        last.then_inc(v_ps, 1)
                    if (q := at(3)):
                        if j == 4:
                            pe.wait_ge(o_sb, a + q.n + 1)
                            if at(4):
                                pe.wait_ge(res_sb, n_of(layer) + at(4).n + 1)
                            if at(0):
                                pe.wait_ge(v_sb, 2 * (a + at(0).n + 1))
                                pe.wait_ge(qk_sb, 2 * (a + at(0).n + 1))
                            for t, bank in ((0, p0), (1, p1)):
                                for b in range(4):
                                    last = pe.transpose(bank[:, b * P:b * P + P],
                                                        ob[:, b, t * P:t * P + P], ident[:, :])
                            last.then_inc(ot_ps, 1)
                        if j == 5:
                            pe.wait_ge(o_nrm, 2 * (a + q.n + 1))
                            for t in range(2):
                                last = pe.transpose(p0[:, t * P:t * P + P], on[q.slot % 2][:, t, :],
                                                    ident[:, :])
                            last.then_inc(ont_ps, 1)
                        if j == 7:
                            pe.wait_ge(ont_sb, a + q.n + 1)
                            for t in range(2):
                                last = pe.matmul(p1[:, t * P:t * P + P], ont[q.slot % 2][:, t * P:t * P + P],
                                                 mat(f"o{layer}"), start=True, stop=True)
                            last.then_inc(y_ps, 1)
            sweep(pe, 5, step)

        def n_of(layer):
            return 0 if layer == 0 else 4 * SEQS

        def heads_scalar(act, a, g, causal):
            def exps(q, j):
                act.wait_ge(ts_ps, 8 * (a + q.n) + j + 1)
                wait(act, pv_ps, 8 * (a + q.n) + j - 1)
                lo = P if causal and j % 2 else 0
                nc.scalar.activation(ex[j % 2][:, :, lo:S],
                                     pt[:, :, :].rearrange("p a (b k) -> p (a b) k", k=S)[:, :, lo:S],
                                     ACT.Exp).then_inc(e_sb, 1)

            def step(at):
                for j in range(8):
                    if j == 3 and (q := at(3)):
                        act.wait_ge(pv_ps, 8 * (a + q.n + 1))
                        wait(act, ot_ps, a + q.n)
                        nc.scalar.copy(ob[:, :, :], po[:, :, :].rearrange("p a (b k) -> p (a b) k", k=S)
                                       ).then_inc(o_sb, 1)
                    if (q := at(2) if j >= 2 else at(3)):
                        exps(q, (j - 2) % 8)
                    if j == 0 and (q := at(0)):
                        copy_xt(act, q, g)
                    if j == 0 and (q := at(2)):
                        act.wait_ge(mt_ps, a + q.n + 1)
                        wait(act, ts_ps, 8 * (a + q.back(1)))
                        nc.scalar.copy(mt[q.slot % 2][:, :], p1[0:96, :].bitcast(BF16)[:, 0:P]).then_inc(mt_sb, 1)
                    if j == 2 and (q := at(0)):
                        act.wait_ge(qk_sb, 2 * (a + q.n + 1))
                        wait(act, to_scr, 32 * (a + q.back(1)))
                        nc.scalar.copy(parts[q.slot % 2][:, 0, :, :], qk[q.slot % 2][:, :, :]).then_inc(part1, 1)
                    if j == 3 and (q := at(0)):
                        act.wait_ge(rest1, a + q.n + 1)
                        nc.scalar.copy(parts[q.slot % 2][:, 1, :, :], rem[q.slot % 2][:, :, :]).then_inc(part2, 1)
                    if j == 6 and (q := at(3)):
                        act.wait_ge(ont_ps, a + q.n + 1)
                        wait(act, y_ps, a + q.back(1))
                        nc.scalar.copy(ont[q.slot % 2][:, :], p0[:, 0:S]).then_inc(ont_sb, 1)
            sweep(act, 5, step)

        def heads_vector(dve, a, n, causal, layer):
            def row_max(q, j):
                b, qt = j // 2, j % 2
                dve.wait_ge(ms_ps, 8 * (a + q.n) + j + 1)
                if j == 0:
                    wait(dve, m_parts, 4 * (a + q.back(1)))
                hi = P if causal and qt == 0 else S
                nc.vector.tensor_reduce(mx[q.slot % 2][:, qt, 4 * b:4 * b + 4],
                                        pm[:, :, :].rearrange("p a (b k) -> p (a b) k", k=S)[:, :, 0:hi],
                                        AX.X, ALU.max).then_inc(ms_max, 1)

            def step(at):
                for j in range(8):
                    if (q := at(1)):
                        row_max(q, j)
                    if j == 0 and (q := at(4)):
                        dve.wait_ge(y_ps, a + q.n + 1)
                        wait(dve, ln_x, 2 * (n + q.back(3)))
                        y = p1[:, 0:S].rearrange("p (t d) -> p t d", t=2)
                        if layer == 0:
                            dve.wait_ge(xb_sb, q.n + 1)
                            nc.vector.tensor_tensor(res[q.slot][:, :, :], y, xb[q.slot][:, :, :],
                                                    ALU.add).then_inc(res_sb, 1)
                        else:
                            nc.vector.tensor_tensor(res[q.slot][:, :, :], y,
                                                    xg[:, bass.ds(2 * q.n, 2), :], ALU.add).then_inc(res_sb, 1)
                        norm_stats(dve, q, n)
                    if j == 1 and (q := at(0)):
                        dve.wait_ge(qk_ps, a + q.n + 1)
                        wait(dve, part3, a + q.back(1))
                        c = float(DH) ** -0.5
                        if layer == 0:
                            nc.vector.tensor_scalar(qk[q.slot % 2][:, 0, :], p1[:, 0:S], col("bq0"), c,
                                                    ALU.add, ALU.mult).then_inc(qk_sb, 1)
                            nc.vector.tensor_scalar(qk[q.slot % 2][:, 1, :], p1[:, S:2 * S], col("bk0"), None,
                                                    ALU.add).then_inc(qk_sb, 1)
                        else:
                            nc.vector.tensor_scalar(qk[q.slot % 2][:, 0, :], p1[:, 0:S], c, None,
                                                    ALU.mult).then_inc(qk_sb, 1)
                            nc.vector.tensor_copy(qk[q.slot % 2][:, 1, :], p1[:, S:2 * S]).then_inc(qk_sb, 1)
                        dve.wait_ge(v_ps, a + q.n + 1)
                        for t in range(2):
                            v = p0[:, t * P:t * P + P].rearrange("p (h d) -> p h d", h=HEADS)
                            dst = va[q.slot][:, t, :, 0:DH]
                            if layer == 0:
                                nc.vector.tensor_tensor(dst, v, row("bv0").rearrange("p (h d) -> p h d", h=HEADS),
                                                        ALU.add).then_inc(v_sb, 1)
                            else:
                                nc.vector.tensor_copy(dst, v).then_inc(v_sb, 1)
                    if j == 2 and (q := at(4)):
                        norm_apply(dve, q, n)
                    if j == 4 and (q := at(3)):
                        dve.wait_ge(ot_ps, a + q.n + 1)
                        for t, bank in ((0, p0), (1, p1)):
                            o = bank[:, :].rearrange("p (h d) -> p h d", d=32)
                            r = rc[q.slot % 2][:, t, :]
                            if layer == 2:
                                nc.vector.tensor_scalar(r.unsqueeze(2), o[:, :, DH:DH + 1], 1e-12, None,
                                                        ALU.max).then_inc(o_rc, 1)
                                dve.wait_ge(o_rc, 2 * q.n + t + 1)
                                nc.vector.reciprocal(r, r).then_inc(o_rc2, 1)
                            else:
                                nc.vector.reciprocal(r.unsqueeze(2), o[:, :, DH:DH + 1]).then_inc(o_rc2, 1)
                        for t, bank in ((0, p0), (1, p1)):
                            dve.wait_ge(o_rc2, 2 * (a + q.n) + t + 1)
                            o = bank[:, :].rearrange("p (h d) -> p h d", d=32)
                            nc.vector.tensor_tensor(on[q.slot % 2][:, t, :].rearrange("p (h d) -> p h d", h=HEADS),
                                                    o[:, :, 0:DH],
                                                    rc[q.slot % 2][:, t, :].unsqueeze(2).to_broadcast([P, HEADS, DH]),
                                                    ALU.mult).then_inc(o_nrm, 1)
                if (q := at(1)):
                    s = q.slot % 2
                    k = 4 * (a + q.n)
                    dve.wait_ge(ms_max, 8 * (a + q.n + 1))
                    wait(dve, mt_ps, a + q.back(1))
                    nc.vector.tensor_scalar(mp[s][:, :, 0, :], mx[s][:, :, :], -1.0, None,
                                            ALU.mult).then_inc(m_parts, 1)
                    dve.wait_ge(m_parts, k + 1)
                    nc.vector.scalar_tensor_tensor(mr[s][:, :, :], mx[s][:, :, :], -1.0, mp[s][:, :, 0, :],
                                                   ALU.mult, ALU.subtract).then_inc(m_parts, 1)
                    dve.wait_ge(m_parts, k + 2)
                    nc.vector.tensor_copy(mp[s][:, :, 1, :], mr[s][:, :, :]).then_inc(m_parts, 1)
                    dve.wait_ge(m_parts, k + 3)
                    nc.vector.tensor_tensor(mp[s][:, :, 2, :], mr[s][:, :, :], mp[s][:, :, 1, :],
                                            ALU.subtract).then_inc(m_parts, 1)
            sweep(dve, 5, step)

        def heads_pool(pool, a, n, layer):
            def step(at):
                if (q := at(4)):
                    norm_rstd(pool, q, n)
                if (q := at(0)):
                    s = q.slot % 2
                    pool.wait_ge(part1, a + q.n + 1)
                    nc.gpsimd.tensor_tensor(rem[s][:, :, :], qk[s][:, :, :], parts[s][:, 0, :, :],
                                            ALU.subtract).then_inc(rest1, 1)
                    pool.wait_ge(part2, a + q.n + 1)
                    nc.gpsimd.tensor_tensor(parts[s][:, 2, :, :], rem[s][:, :, :], parts[s][:, 1, :, :],
                                            ALU.subtract).then_inc(part3, 1)
                if layer == 0 and (q := at(3)):
                    pool.wait_ge(x_in, 16)
                    pool.wait_ge(rows_sb, len(ROWS))
                    wait(pool, res_sb, q.back(3))
                    for t in range(2):
                        ins = nc.gpsimd.tensor_tensor(xb[q.slot][:, t:t + 1, :], xg[:, bass.ds(2 * q.n + t, 1), :],
                                                      row("bo0").unsqueeze(1), ALU.add)
                    ins.then_inc(xb_sb, 1)
            sweep(pool, 5, step)

        pt0, pt1, pm0, pm1, po0, po1 = (b[:, i, :] for b in (pt, pm, po) for i in range(2))
        with ExitStack() as mem:
            kq = [sb(f"kq{i}", [P, 2, S], F32, mem) for i in range(2)]
            v1 = [sb(f"v1_{i}", [P, 2, D], F32, mem) for i in range(2)]
            vn = [sb(f"vn{i}", [P, 2, D], F32, mem) for i in range(2)]
            e1 = [sb(f"e1_{i}", [P, 2, S], F32, mem) for i in range(2)]
            m1 = [sb(f"m1_{i}", [P, 2], F32, mem) for i in range(2)]
            nb1 = [sb(f"nb1_{i}", [P, 2], F32, mem) for i in range(2)]
            sum1 = [sb(f"sum1_{i}", [P, 2], F32, mem) for i in range(2)]
            inv1 = [sb(f"inv1_{i}", [P, 2], F32, mem) for i in range(2)]
        kq_ps, kq_sb, v1_ps, v1_sb = sem("kq_ps"), sem("kq_sb"), sem("v1_ps"), sem("v1_sb")
        s1_ps, s1_max, s1_nb, e1_sb = sem("s1_ps"), sem("s1_max"), sem("s1_nb"), sem("e1_sb")
        inv1_sb, vn_sb, y1_ps = sem("inv1_sb"), sem("vn_sb"), sem("y1_ps")

        def single_tensor(pe, g, n):
            def step(at):
                if (q := at(1)):
                    s = q.slot % 2
                    pe.wait_ge(kq_sb, 2 * (q.n + 1))
                    wait(pe, e1_sb, 2 * q.n)
                    for t in range(2):
                        last = pe.matmul(pt1[:, t * S:t * S + S], kq[s][:, 1, t * P:t * P + P], kq[s][:, 0, :],
                                         start=True, stop=True)
                    last.then_inc(s1_ps, 1)
                if (q := at(0)):
                    wait(pe, xt_sb, g + q.n)
                    transpose_x(pe, q, g)
                if (q := at(2)):
                    s = q.slot % 2
                    pe.wait_ge(vn_sb, 2 * (q.n + 1))
                    wait(pe, res_sb, n + q.n)
                    for i in range(2):
                        for t in range(2):
                            last = pe.matmul(po0[:, i * P:i * P + P], e1[s][:, t, i * P:i * P + P],
                                             vn[s][:, t, :], start=(t == 0), stop=(t == 1))
                    last.then_inc(y1_ps, 1)
                if (q := at(0)):
                    pe.wait_ge(xt_sb, g + q.n + 1)
                    wait(pe, kq_sb, 2 * q.n)
                    xq = xt[q.slot][:, 1:1 + S]
                    pe.matmul(p1[:, 0:S], mat("q1"), xq, start=True, stop=True)
                    pe.matmul(p1[:, S:2 * S], mat("k1"), xq, start=True, stop=True).then_inc(kq_ps, 1)
                    wait(pe, v1_sb, q.n)
                    for t in range(2):
                        last = pe.matmul(pt0[:, t * P:t * P + P], xq[:, t * P:t * P + P], mat("v1"),
                                         start=True, stop=True)
                    last.then_inc(v1_ps, 1)
            sweep(pe, 4, step)

        def single_scalar(act, g):
            def step(at):
                if (q := at(0)):
                    copy_xt(act, q, g)
                if (q := at(1)):
                    s = q.slot % 2
                    act.wait_ge(s1_nb, q.n + 1)
                    wait(act, y1_ps, q.back(1))
                    for t in range(2):
                        nc.scalar.activation(e1[s][:, t, :], pt1[:, t * S:t * S + S], ACT.Exp,
                                             bias=nb1[s][:, t:t + 1], scale=1.0 / D,
                                             accum_out=sum1[s][:, t:t + 1]).then_inc(e1_sb, 1)
            sweep(act, 4, step)

        def single_vector(dve, n):
            def step(at):
                if (q := at(3)):
                    norm_apply(dve, q, n)
                if (q := at(1)):
                    s = q.slot % 2
                    dve.wait_ge(s1_ps, q.n + 1)
                    nc.vector.tensor_reduce(m1[s][:, :], pt1[:, :].rearrange("p (t k) -> p t k", t=2), AX.X,
                                            ALU.max).then_inc(s1_max, 1)
                    dve.wait_ge(s1_max, q.n + 1)
                    nc.vector.tensor_scalar(nb1[s][:, :], m1[s][:, :], -1.0 / D, None,
                                            ALU.mult).then_inc(s1_nb, 1)
                if (q := at(0)):
                    s = q.slot % 2
                    dve.wait_ge(kq_ps, q.n + 1)
                    nc.vector.tensor_scalar(kq[s][:, 0, :], p1[:, 0:S], col("bq1"), None, ALU.add).then_inc(kq_sb, 1)
                    nc.vector.tensor_scalar(kq[s][:, 1, :], p1[:, S:2 * S], col("bk1"), None, ALU.add).then_inc(kq_sb, 1)
                    dve.wait_ge(v1_ps, q.n + 1)
                    wait(dve, vn_sb, 2 * (q.back(1)))
                    nc.vector.tensor_tensor(v1[s][:, :, :], pt0[:, 0:S].rearrange("p (t d) -> p t d", t=2),
                                            row("bv1").unsqueeze(1).to_broadcast([P, 2, D]), ALU.add).then_inc(v1_sb, 1)
                if (q := at(2)):
                    dve.wait_ge(y1_ps, q.n + 1)
                    add_x(dve, q, po0)
                    norm_stats(dve, q, n)
                if (q := at(1)):
                    s = q.slot % 2
                    dve.wait_ge(e1_sb, 2 * (q.n + 1))
                    nc.vector.reciprocal(inv1[s][:, :], sum1[s][:, :]).then_inc(inv1_sb, 1)
                    dve.wait_ge(inv1_sb, q.n + 1)
                    dve.wait_ge(v1_sb, q.n + 1)
                    for t in range(2):
                        nc.vector.tensor_scalar(vn[s][:, t, :], v1[s][:, t, :], inv1[s][:, t:t + 1], None,
                                                ALU.mult).then_inc(vn_sb, 1)
            sweep(dve, 4, step)

        def add_x(dve, q, bank):
            nc.vector.tensor_tensor(res[q.slot][:, :, :], bank[:, 0:S].rearrange("p (t d) -> p t d", t=2),
                                    xg[:, bass.ds(2 * q.n, 2), :], ALU.add).then_inc(res_sb, 1)

        with ExitStack() as mem:
            mix = [sb(f"mix{i}", [P, 2, S], F32, mem) for i in range(2)]
            before = [sb(f"before{i}", [P, 2, S], F32, mem) for i in range(2)]
            rs = [sb(f"rs{i}", [P, 2, D], F32, mem) for i in range(SLOTS)]
            kr = [sb(f"kr{i}", [P, S], F32, mem) for i in range(2)]
            ka = [sb(f"ka{i}", [P, S], F32, mem) for i in range(2)]
            gv = [sb(f"gv{i}", [P, 2, D], F32, mem) for i in range(2)]
        before_sb, mix_sb, r_ps, k_ps = sem("before_sb"), sem("mix_sb"), sem("r_ps"), sem("k_ps")
        r_sb, kr_sb, ka_sb, vf_ps, gv_sb = sem("r_sb"), sem("kr_sb"), sem("ka_sb"), sem("vf_ps"), sem("gv_sb")

        def mixing_tensor(pe, a, g, layer):
            def step(at):
                if (q := at(1)):
                    s = q.slot % 2
                    pe.wait_ge(mix_sb, 2 * (a + q.n + 1))
                    wait(pe, r_sb, a + q.n)
                    for t in range(2):
                        last = pe.matmul(p1[:, t * P:t * P + P], mix[s][:, 0, t * P:t * P + P], mat(f"r{layer}"),
                                         start=True, stop=True)
                    last.then_inc(r_ps, 1)
                    wait(pe, kr_sb, a + q.n)
                    pe.matmul(pt0[:, 0:S], mat(f"m{layer}"), mix[s][:, 1, :], start=True, stop=True).then_inc(k_ps, 1)
                if (q := at(0)):
                    wait(pe, xt_sb, g + q.n)
                    transpose_x(pe, q, g)
                if (q := at(2)):
                    pe.wait_ge(ka_sb, a + q.n + 1)
                    wait(pe, gv_sb, a + q.n)
                    for t in range(2):
                        last = pe.matmul(pt1[:, t * P:t * P + P], ka[q.slot % 2][:, t * P:t * P + P],
                                         mat(f"w{layer}"), start=True, stop=True)
                    last.then_inc(vf_ps, 1)
            sweep(pe, 4, step)

        def mixing_scalar(act, a, g):
            def step(at):
                if (q := at(0)):
                    copy_xt(act, q, g)
                if (q := at(1)):
                    act.wait_ge(r_ps, a + q.n + 1)
                    nc.scalar.activation(rs[q.slot][:, :, :], p1[:, 0:S].rearrange("p (t d) -> p t d", t=2),
                                         ACT.Sigmoid).then_inc(r_sb, 1)
                    act.wait_ge(k_ps, a + q.n + 1)
                    wait(act, ka_sb, a + q.back(1))
                    nc.scalar.activation(kr[q.slot % 2][:, :], pt0[:, 0:S], ACT.Relu).then_inc(kr_sb, 1)
            sweep(act, 4, step)

        def mixing_vector(dve, a, g, n, layer):
            def step(at):
                if (q := at(3)):
                    norm_apply(dve, q, n)
                if (q := at(0)):
                    s = q.slot % 2
                    dve.wait_ge(xt_sb, g + q.n + 1)
                    wait(dve, k_ps, a + q.back(1))
                    for c in range(2):
                        nc.vector.tensor_scalar(before[s][:, c, :], xt[q.slot][:, 0:S],
                                                omu[:, 2 * layer - 2 + c:2 * layer - 1 + c], None,
                                                ALU.mult).then_inc(before_sb, 1)
                    for c, mu in ((0, "mr"), (1, "mk")):
                        dve.wait_ge(before_sb, 2 * (a + q.n) + 1 + c)
                        nc.vector.scalar_tensor_tensor(mix[s][:, c, :], xt[q.slot][:, 1:1 + S],
                                                       col(f"{mu}{layer}"), before[s][:, c, :],
                                                       ALU.mult, ALU.add).then_inc(mix_sb, 1)
                if (q := at(2)):
                    s = q.slot % 2
                    dve.wait_ge(vf_ps, a + q.n + 1)
                    nc.vector.tensor_tensor(gv[s][:, :, :], pt1[:, 0:S].rearrange("p (t d) -> p t d", t=2),
                                            rs[q.slot][:, :, :], ALU.mult).then_inc(gv_sb, 1)
                    dve.wait_ge(gv_sb, a + q.n + 1)
                    nc.vector.tensor_tensor(res[q.slot][:, :, :], gv[s][:, :, :], xg[:, bass.ds(2 * q.n, 2), :],
                                            ALU.add).then_inc(res_sb, 1)
                    norm_stats(dve, q, n)
            sweep(dve, 4, step)

        def mixing_pool(pool, a, n):
            def step(at):
                if (q := at(1)):
                    s = q.slot % 2
                    pool.wait_ge(kr_sb, a + q.n + 1)
                    wait(pool, vf_ps, a + q.back(1))
                    nc.gpsimd.tensor_tensor(ka[s][:, :], kr[s][:, :], kr[s][:, :], ALU.mult).then_inc(ka_sb, 1)
                if (q := at(2)):
                    norm_rstd(pool, q, n)
            sweep(pool, 4, step)

        def norm_pool(pool, n, lags, lag):
            def step(at):
                if (q := at(lag)):
                    norm_rstd(pool, q, n)
            sweep(pool, lags, step)

        with ExitStack() as mem:
            qt3 = [sb(f"qt3_{i}", [LD, S], F32, mem) for i in range(2)]
            vt3 = [sb(f"vt3_{i}", [LD, S], F32, mem) for i in range(2)]
            lowt = [sb(f"lowt{i}", [LD, S], F32, mem) for i in range(2)]
            low = [sb(f"low{i}", [P, S], F32, mem) for i in range(2)]
            elt = [sb(f"elt{i}", [LD, S], F32, mem) for i in range(2)]
            el = [sb(f"el{i}", [P, S], F32, mem) for i in range(2)]
            tok = [sb(f"tok{i}", [P, 2, 2, LD], F32, mem) for i in range(SLOTS)]
            am = [sb(f"am{i}", [P, 3, P], F32, mem) for i in range(2)]
            zq = [sb(f"zq{i}", [P, 2, LD], F32, mem) for i in range(2)]
            den = [sb(f"den{i}", [P, 2], F32, mem) for i in range(2)]
            den2 = [sb(f"den2_{i}", [P, 2], F32, mem) for i in range(2)]
            inv3 = [sb(f"inv3_{i}", [P, 2], F32, mem) for i in range(SLOTS)]
            o3 = [sb(f"o3_{i}", [P, 2, LD], F32, mem) for i in range(2)]
            ot3 = [sb(f"ot3_{i}", [P, P], F32, mem) for i in range(2)]
        t3_ps, tok_ps, low_sb, el_sb, qt3_sb, vt3_sb, tok_sb = (sem(s) for s in (
            "t3_ps", "tok_ps", "low_sb", "el_sb", "qt3_sb", "vt3_sb", "tok_sb"))
        a3_ps, z3_ps, am_sb, zq_sb, den_sb, den2_sb, inv3_sb = (sem(s) for s in (
            "a3_ps", "z3_ps", "am_sb", "zq_sb", "den_sb", "den2_sb", "inv3_sb"))
        o3_ps, o3_sb, ot3_ps, ot3_sb, y3_ps = (sem(s) for s in ("o3_ps", "o3_sb", "ot3_ps", "ot3_sb", "y3_ps"))

        def linear_tensor(pe, g, n):
            def step(at):
                if (q := at(2)):
                    s = q.slot % 2
                    pe.wait_ge(am_sb, 2 * (q.n + 1))
                    wait(pe, o3_sb, q.n)
                    k0, k1 = tok[q.slot][:, 0, 1, :], tok[q.slot][:, 1, 1, :]
                    pe.matmul(po0[:, 0:LD], am[s][:, 0, :], k0, start=True, stop=True)
                    pe.matmul(po0[:, LD:2 * LD], am[s][:, 1, :], k0, start=True, stop=False)
                    pe.matmul(po0[:, LD:2 * LD], am[s][:, 2, :], k1, start=False, stop=True).then_inc(o3_ps, 1)
                if (q := at(1)):
                    s = q.slot % 2
                    pe.wait_ge(qt3_sb, q.n + 1)
                    pe.wait_ge(vt3_sb, q.n + 1)
                    wait(pe, am_sb, 2 * q.n)
                    pe.matmul(pt1[:, 0:S], vt3[s][:, 0:P], qt3[s][:, :], start=True, stop=True)
                    pe.matmul(pt1[:, S:S + P], vt3[s][:, P:S], qt3[s][:, P:S], start=True, stop=True).then_inc(a3_ps, 1)
                    pe.wait_ge(tok_sb, q.n + 1)
                    wait(pe, zq_sb, q.n)
                    k0, k1 = tok[q.slot][:, 0, 1, :], tok[q.slot][:, 1, 1, :]
                    pe.matmul(pm0[:, 0:LD], upto[:, 0, :], k0, start=True, stop=True)
                    pe.matmul(pm0[:, LD:2 * LD], upto[:, 1, :], k0, start=True, stop=False)
                    pe.matmul(pm0[:, LD:2 * LD], upto[:, 0, :], k1, start=False, stop=True).then_inc(z3_ps, 1)
                if (q := at(0)):
                    wait(pe, xt_sb, g + q.n)
                    wait(pe, vt3_sb, q.n)
                    transpose_x(pe, q, g)
                if (q := at(2)):
                    pe.wait_ge(o3_sb, q.n + 1)
                    wait(pe, ot3_sb, q.n)
                    wait(pe, res_sb, n + q.n)
                    pe.transpose(po1[:, 0:P], o3[q.slot % 2][:, :, :].rearrange("p t d -> p (t d)"),
                                 ident[:, :]).then_inc(ot3_ps, 1)
                if (q := at(0)):
                    xq = xt[q.slot][:, 1:1 + S]
                    pe.wait_ge(xt_sb, g + q.n + 1)
                    wait(pe, qt3_sb, q.n)
                    pe.matmul(p1[0:LD, 0:S], wl[:, 0, :], xq, start=True, stop=True)
                    pe.matmul(p0[0:LD, S:2 * S], wl[:, 2, :], xq, start=True, stop=True).then_inc(t3_ps, 1)
                    wait(pe, tok_sb, q.n)
                    for t in range(2):
                        last = pe.matmul(pt0[:, t * P:t * P + P], xq[:, t * P:t * P + P],
                                         wl[:, 0:2, :].rearrange("p a b -> p (a b)"), start=True, stop=True)
                    last.then_inc(tok_ps, 1)
                if (q := at(2)):
                    pe.wait_ge(ot3_sb, q.n + 1)
                    wait(pe, res_sb, n + q.n)
                    for t in range(2):
                        last = pe.matmul((pm1, po1)[t][:, t * P:t * P + P], ot3[q.slot % 2][t * LD:t * LD + LD, :],
                                         wo[t * LD:t * LD + LD, :],
                                         start=True, stop=True)
                    last.then_inc(y3_ps, 1)
            sweep(pe, 4, step)

        def linear_scalar(act, g):
            def step(at):
                if (q := at(0)):
                    copy_xt(act, q, g)
                if (q := at(2)):
                    act.wait_ge(ot3_ps, q.n + 1)
                    wait(act, y3_ps, q.back(1))
                    nc.scalar.copy(ot3[q.slot % 2][:, :], po1[:, 0:P]).then_inc(ot3_sb, 1)
                if (q := at(0)):
                    s = q.slot % 2
                    act.wait_ge(t3_ps, q.n + 1)
                    wait(act, a3_ps, q.back(1))
                    nc.scalar.copy(vt3[s][:, :], p0[0:LD, S:2 * S]).then_inc(vt3_sb, 1)
                    act.wait_ge(low_sb, 2 * q.n + 1)
                    wait(act, tok_sb, q.back(1))
                    nc.scalar.activation(elt[s][:, :], lowt[s][:, :], ACT.Exp).then_inc(el_sb, 1)
                    act.wait_ge(low_sb, 2 * q.n + 2)
                    nc.scalar.activation(el[s][:, :], low[s][:, :], ACT.Exp).then_inc(el_sb, 1)
            sweep(act, 4, step)

        def linear_vector(dve, n):
            def step(at):
                if (q := at(3)):
                    norm_apply(dve, q, n)
                if (q := at(2)):
                    s = q.slot % 2
                    dve.wait_ge(o3_ps, q.n + 1)
                    nc.vector.tensor_tensor(o3[s][:, :, :], po0[:, 0:2 * LD].rearrange("p (t d) -> p t d", t=2),
                                            inv3[q.slot][:, :].unsqueeze(2).to_broadcast([P, 2, LD]),
                                            ALU.mult).then_inc(o3_sb, 1)
                if (q := at(1)):
                    s = q.slot % 2
                    dve.wait_ge(a3_ps, q.n + 1)
                    nc.vector.tensor_tensor(am[s][:, 0:2, :], pt1[:, 0:S].rearrange("p (a b) -> p a b", a=2),
                                            upto[:, :, :], ALU.mult).then_inc(am_sb, 1)
                    nc.vector.tensor_tensor(am[s][:, 2, :], pt1[:, S:S + P], upto[:, 0, :], ALU.mult).then_inc(am_sb, 1)
                    dve.wait_ge(z3_ps, q.n + 1)
                    nc.vector.tensor_tensor(zq[s][:, :, :], pm0[:, 0:2 * LD].rearrange("p (t d) -> p t d", t=2),
                                            tok[q.slot][:, :, 0, :], ALU.mult).then_inc(zq_sb, 1)
                    dve.wait_ge(zq_sb, q.n + 1)
                    nc.vector.tensor_reduce(den[s][:, :], zq[s][:, :, :], AX.X, ALU.add).then_inc(den_sb, 1)
                    dve.wait_ge(den_sb, q.n + 1)
                    nc.vector.tensor_scalar(den2[s][:, :], den[s][:, :], 1e-6, None, ALU.max).then_inc(den2_sb, 1)
                    dve.wait_ge(den2_sb, q.n + 1)
                    nc.vector.reciprocal(inv3[q.slot][:, :], den2[s][:, :]).then_inc(inv3_sb, 1)
                    dve.wait_ge(inv3_sb, q.n + 1)
                if (q := at(0)):
                    s = q.slot % 2
                    dve.wait_ge(t3_ps, q.n + 1)
                    wait(dve, el_sb, 2 * (q.back(1)))
                    nc.vector.tensor_scalar(lowt[s][:, :], p1[0:LD, 0:S], 0.0, None, ALU.min).then_inc(low_sb, 1)
                    dve.wait_ge(tok_ps, q.n + 1)
                    nc.vector.tensor_scalar(low[s][:, :], pt0[:, 0:S], 0.0, None, ALU.min).then_inc(low_sb, 1)
                    dve.wait_ge(el_sb, 2 * q.n + 1)
                    nc.vector.scalar_tensor_tensor(qt3[s][:, :], p1[0:LD, 0:S], 0.0, elt[s][:, :], ALU.max,
                                                   ALU.add).then_inc(qt3_sb, 1)
                    dve.wait_ge(el_sb, 2 * q.n + 2)
                    nc.vector.scalar_tensor_tensor(tok[q.slot][:, :, :, :].rearrange("p a b c -> p (a b c)"),
                                                   pt0[:, 0:S], 0.0, el[s][:, :], ALU.max, ALU.add).then_inc(tok_sb, 1)
                if (q := at(2)):
                    dve.wait_ge(y3_ps, q.n + 1)
                    for t, bank in ((0, pm1), (1, po1)):
                        last = nc.vector.tensor_tensor(res[q.slot][:, t:t + 1, :],
                                                       bank[:, t * P:t * P + P].unsqueeze(1),
                                                       xg[:, bass.ds(2 * q.n + t, 1), :], ALU.add)
                    last.then_inc(res_sb, 1)
                    norm_stats(dve, q, n)
            sweep(dve, 4, step)

        def load_x_routed(sp, g, n, before, each):
            def step(at):
                if (q := at(0)):
                    wait_apart(sp, scattered[q.slot], before // SLOTS + each * q.turn, passed)
                    load_x(sp, q, g, n)
            sweep(sp, 3, step)

        def load_x_only(sp, lags, g, n):
            def step(at):
                if (q := at(0)):
                    load_x(sp, q, g, n)
            sweep(sp, lags, step)

        lg = [sb(f"lg{i}", [P, 2, EM]) for i in range(2)]
        top = [sb(f"top{i}", [P, 2, 8]) for i in range(2)]
        topi = [sb(f"topi{i}", [P, 2, 8], U32) for i in range(2)]
        topf = [sb(f"topf{i}", [P, 2, 8]) for i in range(2)]
        oh = [sb(f"oh{i}", [P, 2, 2, EM]) for i in range(2)]
        sel = [sb(f"sel{i}", [P, 2, EM], BF16) for i in range(SLOTS)]
        seen = [sb(f"seen{i}", [P, EM], BF16) for i in range(SLOTS)]
        rank = [sb(f"rank{i}", [P, 2, EM]) for i in range(2)]
        pick = [sb(f"pick{i}", [P, 2, 2, EM]) for i in range(2)]
        pl = [sb(f"pl{i}", [P, 4, 2]) for i in range(2)]
        gap = [sb(f"gap{i}", [P, 2, EM]) for i in range(2)]
        eg = [sb(f"eg{i}", [P, 2, EM]) for i in range(2)]
        place = [sb(f"place{i}", [P, 2, 2], U32) for i in range(SLOTS)]
        places = sb("places", [P, TILES, 2], U32)
        weight = sb("weight", [P, TILES, 2])
        xs0 = nc.dram_tensor("sorted0", (E0 * ROOM0 + 8 * S, D), F32).ap()
        ys0 = nc.dram_tensor("result0", (NG * S, D), F32).ap()
        xs3 = nc.dram_tensor("sorted3", (E3 * CAP3 + SEQS * S, D), F32).ap()
        ys3 = nc.dram_tensor("result3", (E3 * CAP3, D), F32).ap()
        DUMP = E3 * CAP3

        lg_ps, lg_sb, seen_sb, top_sb, topi_sb, topf_sb = (sem(s) for s in (
            "lg_ps", "lg_sb", "seen_sb", "top_sb", "topi_sb", "topf_sb"))
        oh_sb, sel_sb, rank_ps, rank_sb, pick_sb, pl_sb = (sem(s) for s in (
            "oh_sb", "sel_sb", "rank_ps", "rank_sb", "pick_sb", "pl_sb"))
        gap_sb, eg_sb, wt_sb, place_sb, zeroed = (sem(s) for s in (
            "gap_sb", "eg_sb", "wt_sb", "place_sb", "zeroed"))
        scattered = [sem(f"scattered{i}") for i in range(SLOTS)]

        def route_tensor(pe, a, g, E, rw):
            def step(at):
                if (q := at(0)):
                    wait(pe, xt_sb, g + q.n)
                    transpose_x(pe, q, g)
                if (q := at(1)):
                    pe.wait_ge(sel_sb, a + q.n + 1)
                    pe.wait_ge(seen_sb, a // SEQS + a + q.n + 1)
                    wait(pe, rank_sb, a + q.n)
                    s = sel[q.slot]
                    pe.matmul(pt0[:, 0:E], upto16[:, :], s[:, 0, 0:E], start=True, stop=False)
                    pe.matmul(pt0[:, 0:E], ones16[:, :], seen[q.slot][:, 0:E], start=False, stop=True)
                    pe.matmul(pt0[:, E:2 * E], upto16[:, :], s[:, 1, 0:E], start=True, stop=False)
                    pe.matmul(pt0[:, E:2 * E], ones16[:, :], s[:, 0, 0:E], start=False, stop=False)
                    pe.matmul(pt0[:, E:2 * E], ones16[:, :], seen[q.slot][:, 0:E], start=False,
                              stop=True).then_inc(rank_ps, 1)
                if (q := at(0)):
                    pe.wait_ge(xt_sb, g + q.n + 1)
                    wait(pe, lg_sb, a + q.n)
                    for t in range(2):
                        last = pe.matmul(p1[:, t * E:t * E + E], xt[q.slot][:, 1 + t * P:1 + t * P + P], rw[:, :],
                                         start=True, stop=True)
                    last.then_inc(lg_ps, 1)
            sweep(pe, 3, step)

        def route_scalar(act, a, g, E):
            def step(at):
                if (q := at(0)):
                    copy_xt(act, q, g)
                if (q := at(1)):
                    s = q.slot % 2
                    act.wait_ge(gap_sb, 2 * (a + q.n + 1))
                    nc.scalar.activation(eg[s][:, :, 0:E], gap[s][:, :, 0:E], ACT.Exp).then_inc(eg_sb, 1)
            sweep(act, 3, step)

        def route_vector(dve, a, E, choices, base):
            nc.vector.memset(seen[0][:, :], 0.0).then_inc(seen_sb, 1)

            def step(at):
                if (q := at(0)):
                    s, k = q.slot % 2, a + q.n
                    dve.wait_ge(lg_ps, k + 1)
                    nc.vector.tensor_copy(lg[s][:, :, 0:E], p1[:, 0:2 * E].rearrange("p (t e) -> p t e", t=2)
                                          ).then_inc(lg_sb, 1)
                    wait_apart(dve, lg_sb, k + 1, passed)
                    for t in range(2):
                        nc.vector.max(top[s][:, t, :], lg[s][:, t, 0:E]).then_inc(top_sb, 1)
                    for t in range(2):
                        wait_apart(dve, top_sb, 2 * k + 1 + t, passed)
                        nc.vector.max_index(topi[s][:, t, :], top[s][:, t, :], lg[s][:, t, 0:E]).then_inc(topi_sb, 1)
                    dve.wait_ge(topi_sb, 2 * (k + 1))
                    nc.vector.tensor_copy(topf[s][:, :, :], topi[s][:, :, :]).then_inc(topf_sb, 1)
                    dve.wait_ge(topf_sb, k + 1)
                    for i in range(2):
                        for t in range(2):
                            nc.vector.tensor_scalar(oh[s][:, i, t, 0:E], iota_e[:, 0:E], topf[s][:, t, i:i + 1],
                                                    None, ALU.is_equal).then_inc(oh_sb, 1)
                    dve.wait_ge(oh_sb, 4 * (k + 1))
                    if choices == 2:
                        nc.vector.tensor_tensor(sel[q.slot][:, :, 0:E], oh[s][:, 0, :, 0:E], oh[s][:, 1, :, 0:E],
                                                ALU.add).then_inc(sel_sb, 1)
                    else:
                        nc.vector.tensor_copy(sel[q.slot][:, :, 0:E], oh[s][:, 0, :, 0:E]).then_inc(sel_sb, 1)
                    wait(dve, eg_sb, k - 1)
                    for t in range(2):
                        nc.vector.tensor_scalar(gap[s][:, t, 0:E], lg[s][:, t, 0:E], top[s][:, t, 0:1], None,
                                                ALU.subtract).then_inc(gap_sb, 1)
                    dve.wait_ge(gap_sb, 2 * (k + 1))
                if (q := at(1)):
                    s, k = q.slot % 2, a + q.n
                    sd = a // SEQS + k
                    nxt = (q.slot + 1) % SLOTS
                    dve.wait_ge(seen_sb, sd + 1)
                    nc.vector.tensor_tensor(rank[s][:, 0, 0:E], seen[q.slot][:, 0:E], sel[q.slot][:, 0, 0:E],
                                            ALU.add).then_inc(sel2_sb, 1)
                    dve.wait_ge(sel2_sb, k + 1)
                    nc.vector.tensor_tensor(seen[nxt][:, 0:E], rank[s][:, 0, 0:E], sel[q.slot][:, 1, 0:E],
                                            ALU.add).then_inc(seen_sb, 1)
                    dve.wait_ge(seen_sb, sd + 2)
                    dve.wait_ge(rank_ps, k + 1)
                    r = pt0[:, 0:2 * E].rearrange("p (t e) -> p t e", t=2)
                    if choices == 2:
                        nc.vector.tensor_tensor(rank[s][:, :, 0:E], r, base[:, :, :], ALU.add).then_inc(rank_sb, 1)
                        dve.wait_ge(rank_sb, k + 1)
                        for i in range(2):
                            nc.vector.tensor_tensor(pick[s][:, i, :, 0:E], oh[s][:, i, :, 0:E], rank[s][:, :, 0:E],
                                                    ALU.mult).then_inc(pick_sb, 1)
                        dve.wait_ge(pick_sb, 2 * (k + 1))
                        nc.vector.tensor_reduce(pl[s][:, 0:2, :].rearrange("p a b -> p (a b)"),
                                                pick[s][:, :, :, 0:E], AX.X, ALU.add).then_inc(pl_sb, 1)
                        dve.wait_ge(pl_sb, k + 1)
                        wait(dve, scattered[q.slot], 64 * q.turn)
                        nc.vector.tensor_copy(place[q.slot][:, :, :], pl[s][:, 0:2, :]).then_inc(place_sb, 1)
                        nc.vector.tensor_copy(places[:, bass.ds(2 * q.n, 2), :].rearrange("p t c -> p c t"),
                                              pl[s][:, 0:2, :]).then_inc(places_sb, 1)
                        dve.wait_ge(eg_sb, k + 1)
                        e2 = sm[s][:, 0, :]
                        nc.vector.tensor_tensor(gs[s][:, :, 0:E], eg[s][:, :, 0:E], oh[s][:, 1, :, 0:E],
                                                ALU.mult).then_inc(wt_sb, 1)
                        dve.wait_ge(wt_sb, 5 * q.n + 1)
                        nc.vector.tensor_reduce(e2, gs[s][:, :, 0:E], AX.X, ALU.add).then_inc(wt_sb, 1)
                        dve.wait_ge(wt_sb, 5 * q.n + 2)
                        nc.vector.tensor_scalar(sm[s][:, 1, :], e2, 1.0, None, ALU.add).then_inc(wt_sb, 1)
                        dve.wait_ge(wt_sb, 5 * q.n + 3)
                        nc.vector.reciprocal(weight[:, bass.ds(2 * q.n, 2), 0:1],
                                             sm[s][:, 1, :].unsqueeze(2)).then_inc(wt_sb, 1)
                        dve.wait_ge(wt_sb, 5 * q.n + 4)
                        nc.vector.tensor_tensor(weight[:, bass.ds(2 * q.n, 2), 1:2], e2.unsqueeze(2),
                                                weight[:, bass.ds(2 * q.n, 2), 0:1], ALU.mult).then_inc(wt_sb, 1)
                    else:
                        w0 = 5 * SEQS + 7 * q.n
                        nc.vector.tensor_tensor(pick[s][:, 0, :, 0:E], oh[s][:, 0, :, 0:E], r,
                                                ALU.mult).then_inc(rank_sb, 1)
                        nc.vector.tensor_tensor(pick[s][:, 1, :, 0:E], oh[s][:, 0, :, 0:E], base[:, :, :],
                                                ALU.mult).then_inc(pick_sb, 1)
                        dve.wait_ge(rank_sb, k + 1)
                        dve.wait_ge(pick_sb, 2 * SEQS + q.n + 1)
                        nc.vector.tensor_reduce(pl[s][:, 0:2, :].rearrange("p a b -> p (a b)"),
                                                pick[s][:, :, :, 0:E], AX.X, ALU.add).then_inc(pl_sb, 1)
                        dve.wait_ge(pl_sb, k + 1)
                        keep, lost = sm[s][:, 0, :], sm[s][:, 1, :]
                        nc.vector.tensor_scalar(keep, pl[s][:, 0, :], float(CAP3), None, ALU.is_le).then_inc(wt_sb, 1)
                        nc.vector.scalar_tensor_tensor(pl[s][:, 2, :], pl[s][:, 0, :], float(CAP3), pl[s][:, 1, :],
                                                       ALU.min, ALU.add).then_inc(wt_sb, 1)
                        dve.wait_ge(wt_sb, w0 + 2)
                        nc.vector.tensor_copy(places[:, bass.ds(2 * q.n, 2), 0:1],
                                              pl[s][:, 2, :].unsqueeze(2)).then_inc(places_sb, 1)
                        nc.vector.tensor_tensor(lost, pl[s][:, 2, :], dump[:, bass.ds(2 * q.n, 2)],
                                                ALU.subtract).then_inc(wt_sb, 1)
                        dve.wait_ge(wt_sb, w0 + 3)
                        nc.vector.tensor_tensor(pl[s][:, 3, :], lost, keep, ALU.mult).then_inc(wt_sb, 1)
                        dve.wait_ge(wt_sb, w0 + 4)
                        dve.wait_ge(scattered[q.slot], 64 * (SEQS // SLOTS) + 32 * q.turn)
                        nc.vector.tensor_tensor(place[q.slot][:, 0, :], pl[s][:, 3, :], dump[:, bass.ds(2 * q.n, 2)],
                                                ALU.add).then_inc(place_sb, 1)
                        dve.wait_ge(eg_sb, k + 1)
                        nc.vector.tensor_reduce(sm[s][:, 2, :], eg[s][:, :, 0:E], AX.X, ALU.add).then_inc(wt_sb, 1)
                        dve.wait_ge(wt_sb, w0 + 5)
                        nc.vector.reciprocal(sm[s][:, 3, :], sm[s][:, 2, :]).then_inc(wt_sb, 1)
                        dve.wait_ge(wt_sb, w0 + 6)
                        nc.vector.tensor_tensor(weight[:, bass.ds(2 * q.n, 2), 0:1], sm[s][:, 3, :].unsqueeze(2),
                                                keep.unsqueeze(2), ALU.mult).then_inc(wt_sb, 1)
            sweep(dve, 3, step)

        sm = [sb(f"sm{i}", [P, 4, 2]) for i in range(2)]
        gs = [sb(f"gs{i}", [P, 2, EM]) for i in range(2)]
        sel2_sb, places_sb = sem("sel2_sb"), sem("places_sb")

        def route_pool(pool, a, choices, rows):
            def step(at):
                if (q := at(2)):
                    wait_apart(pool, place_sb, a + q.n + 1, passed)
                    for i in range(choices):
                        for t in range(2):
                            pool.indirect_dma_start(
                                out=rows, out_offset=bass.IndirectOffsetOnAxis(ap=place[q.slot][:, i, t:t + 1], axis=0),
                                in_=xs[q.slot][:, t, :], in_offset=None).then_inc(scattered[q.slot], 16)
            sweep(pool, 3, step)

        count_f = sb("count_f", [P, E0])
        count_i = sb("count_i", [P, E0], I32)
        up_i = sb("up_i", [P, E0], I32)
        grp_i = sb("grp_i", [P, E0], I32)
        grp = sb("grp", [P, E0])
        cum = sb("cum", [P, E0])
        past = sb("past", [P, NG, E0])
        spent = sb("spent", [P, NG, E0])
        g_e = sb("g_e", [P, NG])
        g_b = sb("g_b", [P, NG])
        g_j = sb("g_j", [P, NG])
        g_o = sb("g_o", [P, NG])
        g_exp = sb("g_exp", [P, NG], I32)
        g_off = sb("g_off", [P, NG], I32)
        delta = sb("delta", [P, E0])
        ends = sb("ends", [P, E0])
        place_f = sb("place_f", [P, 2 * TILES])
        shift = sb("shift", [P, 2 * TILES, E0])
        moved = sb("moved", [P, 2 * TILES])
        count_ps, list_sb = sem("count_ps"), sem("list_sb")
        tails = sem("tails")
        LIST = 16

        def list_tensor(pe):
            pe.wait_ge(seen_sb, SEQS + 1)
            pe.wait_ge(lg_sb, SEQS)
            pe.matmul(p1[:, 0:E0], ones16[:, :], seen[0][:, 0:E0], start=True, stop=True).then_inc(count_ps, 1)

        def list_vector(dve):
            done = [0]

            def chain(ins):
                done[0] += 1
                ins.then_inc(list_sb, 1)
                dve.wait_ge(list_sb, done[0])

            v = nc.vector
            dve.wait_ge(count_ps, 1)
            chain(v.tensor_copy(count_i[:, :], p1[:, 0:E0]))
            chain(v.tensor_scalar(count_f[:, :], p1[:, 0:E0], float(S - 1), None, ALU.add))
            chain(v.tensor_copy(up_i[:, :], count_f[:, :]))
            chain(v.tensor_scalar(grp_i[:, :], up_i[:, :], S.bit_length() - 1, None, ALU.logical_shift_right))
            chain(v.tensor_copy(grp[:, :], grp_i[:, :]))
            chain(v.tensor_tensor_scan(cum[:, :], ones[:, 0:E0], grp[:, :], 0.0, ALU.mult, ALU.add))
            chain(v.tensor_tensor(past[:, :, :], cum[:, :].unsqueeze(1).to_broadcast([P, NG, E0]),
                                  iota_g[:, :].unsqueeze(2).to_broadcast([P, NG, E0]), ALU.is_le))
            chain(v.tensor_reduce(g_e[:, :], past[:, :, :], AX.X, ALU.add))
            chain(v.tensor_tensor(spent[:, :, :], past[:, :, :], grp[:, :].unsqueeze(1).to_broadcast([P, NG, E0]),
                                  ALU.mult))
            chain(v.tensor_reduce(g_b[:, :], spent[:, :, :], AX.X, ALU.add))
            chain(v.tensor_tensor(g_j[:, :], iota_g[:, :], g_b[:, :], ALU.subtract))
            chain(v.tensor_scalar(g_o[:, :], g_j[:, :], float(S), None, ALU.mult))
            chain(v.scalar_tensor_tensor(g_b[:, :], g_e[:, :], float(ROOM0), g_o[:, :], ALU.mult, ALU.add))
            chain(v.tensor_copy(g_off[:, :], g_b[:, :]))
            chain(v.tensor_scalar(g_j[:, :], g_e[:, :], float(E0 - 1), None, ALU.min))
            chain(v.tensor_copy(g_exp[:, :], g_j[:, :]))
            assert done[0] == LIST
            chain(v.tensor_scalar(delta[:, :], grp[:, :], float(S), -float(ROOM0), ALU.mult, ALU.add))
            chain(v.tensor_scalar(ends[:, :], iota_e[:, 0:E0], float(ROOM0), float(ROOM0), ALU.mult, ALU.add))
            flat = places[:, :, :].rearrange("p t c -> p (t c)")
            wide = [P, 2 * TILES, E0]
            chain(v.tensor_copy(place_f[:, :], flat))
            chain(v.tensor_tensor(shift[:, :, :], ends[:, :].unsqueeze(1).to_broadcast(wide),
                                  place_f[:, :].unsqueeze(2).to_broadcast(wide), ALU.is_le))
            chain(v.tensor_tensor(shift[:, :, :], shift[:, :, :], delta[:, :].unsqueeze(1).to_broadcast(wide), ALU.mult))
            chain(v.tensor_reduce(moved[:, :], shift[:, :, :], AX.X, ALU.add))
            chain(v.tensor_tensor(flat, place_f[:, :], moved[:, :], ALU.add))

        def list_sync(sp):
            sp.wait_ge(list_sb, LIST)
            for s in scattered:
                sp.wait_ge(s, 64 * SEQS // SLOTS)
            for e in range(E0):
                c = sp.value_load(count_i[0:1, e:e + 1], min_val=0, max_val=CAP0)
                sp.dma_start(xs0[bass.ds(c + e * ROOM0, S), :].rearrange("(p r) d -> p (r d)", p=P),
                             zt[:, 0:2 * D]).then_inc(tails, 16)

        we1 = [sb(f"we1_{i}", [P, F]) for i in range(SLOTS)]
        we2 = [sb(f"we2_{i}", [P, FC, D]) for i in range(SLOTS)]
        be1 = [sb(f"be1_{i}", [P, FC]) for i in range(SLOTS)]
        be2 = [sb(f"be2_{i}", [P, 1]) for i in range(SLOTS)]
        xe = [sb(f"xe{i}", [P, 3, D]) for i in range(SLOTS)]
        xet = [sb(f"xet{i}", [P, CAP3]) for i in range(2)]
        he = [sb(f"he{i}", [P, FC, CAP3]) for i in range(2)]
        yt = [sb(f"yt{i}", [P, CAP3]) for i in range(2)]
        ye = [sb(f"ye{i}", [P, 3, D]) for i in range(SLOTS)]
        xet_ps, xet_sb, he_ps, he_sb, yt_ps, yt_sb, ye_ps, ye_sb = (sem(s) for s in (
            "xet_ps", "xet_sb", "he_ps", "he_sb", "yt_ps", "yt_sb", "ye_ps", "ye_sb"))
        grp_in = [sem(f"grp_in{i}") for i in range(SLOTS)]
        grp_out = [sem(f"grp_out{i}") for i in range(SLOTS)]

        def pieces(T):
            return [(i, min(P, T - i * P)) for i in range(-(-T // P))]

        IN0 = 16 * 5
        IN3 = 16 * 4

        def experts_sync(sp, a, first):
            if first:
                sp.wait_ge(tails, 16 * E0)
                sp.wait_ge(zeroed, 32)
            else:
                for s in scattered:
                    sp.wait_ge(s, (64 + 32) * SEQS // SLOTS)
                sp.wait_ge(zeroed, 32)
            offs = {}

            def step(at):
                if (q := at(0)):
                    wait_apart(sp, yt_ps, a + q.back(3), passed)
                    if first:
                        e = sp.value_load(g_exp[0:1, bass.ds(q.n, 1)], min_val=0, max_val=E0 - 1)
                        r = sp.value_load(g_off[0:1, bass.ds(q.n, 1)], min_val=0, max_val=E0 * ROOM0 + 7 * S)
                        sp.dma_start(xe[q.slot][:, 0:2, :], xs0[bass.ds(r, S), :].rearrange("(t p) d -> p t d", p=P)
                                     ).then_inc(grp_in[q.slot], 16)
                        sp.dma_start(we1[q.slot][:, :], w1_0[bass.ds(e, 1)].rearrange("e d f -> d (e f)")
                                     ).then_inc(grp_in[q.slot], 16)
                        sp.dma_start(we2[q.slot][:, :, :], w2_0[bass.ds(e, 1)].rearrange("e (c f) d -> f (e c) d", c=FC)
                                     ).then_inc(grp_in[q.slot], 16)
                        sp.dma_start(be1[q.slot][:, :], b1_0[bass.ds(e, 1)].rearrange("e f c -> f (e c)")
                                     ).then_inc(grp_in[q.slot], 16)
                        sp.dma_start(be2[q.slot][:, :], b2_0[bass.ds(e, 1)].rearrange("e d o -> d (e o)")
                                     ).then_inc(grp_in[q.slot], 16)
                    else:
                        src = xs3[bass.ds(q.n * CAP3, CAP3), :]
                        sp.dma_start(xe[q.slot][:, 0:2, :], src[0:2 * P, :].rearrange("(t p) d -> p t d", p=P)
                                     ).then_inc(grp_in[q.slot], 16)
                        sp.dma_start(xe[q.slot][0:CAP3 - 2 * P, 2, :], src[2 * P:CAP3, :]).then_inc(grp_in[q.slot], 16)
                        sp.dma_start(we1[q.slot][:, :], w1_3[bass.ds(q.n, 1)].rearrange("e d f -> d (e f)")
                                     ).then_inc(grp_in[q.slot], 16)
                        sp.dma_start(we2[q.slot][:, :, :], w2_3[bass.ds(q.n, 1)].rearrange("e (c f) d -> f (e c) d", c=FC)
                                     ).then_inc(grp_in[q.slot], 16)
                if (q := at(3)):
                    wait_apart(sp, ye_sb, a + q.n + 1, passed)
                    if first:
                        sp.dma_start(ys0[bass.ds(q.n * S, S), :].rearrange("(t p) d -> p t d", p=P), ye[q.slot][:, 0:2, :]
                                     ).then_inc(grp_out[q.slot], 16)
                    else:
                        dst = ys3[bass.ds(q.n * CAP3, CAP3), :]
                        sp.dma_start(dst[0:2 * P, :].rearrange("(t p) d -> p t d", p=P), ye[q.slot][:, 0:2, :]
                                     ).then_inc(grp_out[q.slot], 16)
                        sp.dma_start(dst[2 * P:CAP3, :], ye[q.slot][0:CAP3 - 2 * P, 2, :]).then_inc(grp_out[q.slot], 16)
            sweep(sp, 4, step, NG if first else E3)

        def experts_tensor(pe, a, T, n, loads, loaded):
            hb = [pt0, pt1, pm0, pm1]

            def step(at):
                if (q := at(0)):
                    wait(pe, xet_sb, a + q.n)
                    pe.wait_ge(grp_in[q.slot], loaded // SLOTS + loads * (q.turn + 1))
                    for i, m in pieces(T):
                        last = pe.transpose(p0[:, i * P:i * P + m], xe[q.slot][0:m, i, :], ident[0:m, 0:m])
                    last.then_inc(xet_ps, 1)
                if (q := at(1)):
                    pe.wait_ge(xet_sb, a + q.n + 1)
                    for c in range(FC):
                        wait(pe, he_sb, 4 * (a + q.back(1)) + c + 1)
                        pe.matmul(hb[c][:, 0:T], we1[q.slot][:, c * P:c * P + P], xet[q.slot % 2][:, 0:T],
                                  start=True, stop=True).then_inc(he_ps, 1)
                if (q := at(2)):
                    wait(pe, yt_sb, a + q.n)
                    pe.wait_ge(he_sb, 4 * (a + q.n + 1))
                    for c in range(FC):
                        last = pe.matmul(po0[:, 0:T], we2[q.slot][:, c, :], he[q.slot % 2][:, c, 0:T],
                                         start=(c == 0), stop=(c == FC - 1))
                    last.then_inc(yt_ps, 1)
                if (q := at(3)):
                    pe.wait_ge(yt_sb, a + q.n + 1)
                    wait(pe, ye_sb, a + q.n)
                    for i, m in pieces(T):
                        last = pe.transpose(po1[0:m, i * P:i * P + P], yt[q.slot % 2][:, i * P:i * P + m], ident[:, :])
                    last.then_inc(ye_ps, 1)
            sweep(pe, 4, step, n)

        def experts_scalar(act, a, T, n, biased):
            hb = [pt0, pt1, pm0, pm1]

            def step(at):
                if (q := at(1)):
                    wait(act, yt_ps, a + q.back(1))
                    for c in range(FC):
                        act.wait_ge(he_ps, 4 * (a + q.n) + c + 1)
                        nc.scalar.activation(he[q.slot % 2][:, c, 0:T], hb[c][:, 0:T], ACT.Gelu_apprx_tanh,
                                             bias=be1[q.slot][:, c:c + 1] if biased else zero_col[:, :]
                                             ).then_inc(he_sb, 1)
            sweep(act, 4, step, n)

        def experts_vector(dve, a, T, n, biased, outs, out0):
            def step(at):
                if (q := at(0)):
                    dve.wait_ge(xet_ps, a + q.n + 1)
                    wait(dve, he_ps, 4 * (a + q.back(1)))
                    nc.vector.tensor_copy(xet[q.slot % 2][:, 0:T], p0[:, 0:T]).then_inc(xet_sb, 1)
                if (q := at(2)):
                    dve.wait_ge(yt_ps, a + q.n + 1)
                    wait(dve, ye_ps, a + q.back(1))
                    if biased:
                        nc.vector.tensor_scalar(yt[q.slot % 2][:, 0:T], po0[:, 0:T], be2[q.slot][:, :], None,
                                                ALU.add).then_inc(yt_sb, 1)
                    else:
                        nc.vector.tensor_copy(yt[q.slot % 2][:, 0:T], po0[:, 0:T]).then_inc(yt_sb, 1)
                if (q := at(3)):
                    dve.wait_ge(ye_ps, a + q.n + 1)
                    wait(dve, grp_out[q.slot], out0 // SLOTS + outs * q.turn)
                    whole = T // P
                    nc.vector.tensor_copy(ye[q.slot][:, 0:whole, :],
                                          po1[:, 0:whole * P].rearrange("p (t d) -> p t d", t=whole)
                                          ).then_inc(ye_most if T % P else ye_sb, 1)
                    if T % P:
                        dve.wait_ge(ye_most, q.n + 1)
                        nc.vector.tensor_copy(ye[q.slot][0:T % P, whole, :],
                                              po1[0:T % P, whole * P:whole * P + P]).then_inc(ye_sb, 1)
            sweep(dve, 4, step, n)

        ye_most = sem("ye_most")

        at_row = [sb(f"at_row{i}", [P, 2, 2], U32) for i in range(SLOTS)]
        wrow = [sb(f"wrow{i}", [P, 2, 2]) for i in range(SLOTS)]
        yr = [sb(f"yr{i}", [P, 2, 2, D]) for i in range(SLOTS)]
        part = [sb(f"part{i}", [P, 2, D]) for i in range(2)]
        row_at, wrow_sb, part_sb = (sem(s) for s in ("row_at", "wrow_sb", "part_sb"))
        gathered = [sem(f"gathered{i}") for i in range(SLOTS)]

        def gather_pool(pool, a, n, choices, rows, outs_done, got):
            for s in grp_out:
                pool.wait_ge(s, outs_done // SLOTS)

            def step(at):
                if (q := at(3)):
                    norm_rstd(pool, q, n)
                if (q := at(1)):
                    pool.wait_ge(row_at, a + q.n + 1)
                    wait_apart(pool, res_sb, n + q.back(3), passed)
                    for t in range(2):
                        for i in range(choices):
                            pool.indirect_dma_start(
                                out=yr[q.slot][:, t, i, :], out_offset=None, in_=rows,
                                in_offset=bass.IndirectOffsetOnAxis(ap=at_row[q.slot][:, t, i:i + 1], axis=0)
                            ).then_inc(gathered[q.slot], 16)
            sweep(pool, 5, step)

        def gather_vector(dve, a, n, choices, got):
            def step(at):
                if (q := at(4)):
                    norm_apply(dve, q, n)
                if (q := at(0)):
                    wait(dve, gathered[q.slot], got // SLOTS + 32 * choices * q.turn)
                    nc.vector.tensor_copy(at_row[q.slot][:, :, 0:choices],
                                          places[:, bass.ds(2 * q.n, 2), 0:choices]).then_inc(row_at, 1)
                    nc.vector.tensor_copy(wrow[q.slot][:, :, 0:choices],
                                          weight[:, bass.ds(2 * q.n, 2), 0:choices]).then_inc(wrow_sb, 1)
                if (q := at(2)):
                    dve.wait_ge(wrow_sb, a + q.n + 1)
                    dve.wait_ge(gathered[q.slot], got // SLOTS + 32 * choices * (q.turn + 1))
                    src = xg[:, bass.ds(2 * q.n, 2), :]
                    if choices == 2:
                        for t in range(2):
                            nc.vector.scalar_tensor_tensor(part[q.slot % 2][:, t:t + 1, :], yr[q.slot][:, t, 0:1, :],
                                                           wrow[q.slot][:, t, 0:1], src[:, t:t + 1, :],
                                                           ALU.mult, ALU.add).then_inc(part_sb, 1)
                        dve.wait_ge(part_sb, 2 * (q.n + 1))
                        src = part[q.slot % 2][:, :, :]
                    for t in range(2):
                        last = nc.vector.scalar_tensor_tensor(res[q.slot][:, t:t + 1, :],
                                                              yr[q.slot][:, t, choices - 1:choices, :],
                                                              wrow[q.slot][:, t, choices - 1:choices],
                                                              src[:, t:t + 1, :], ALU.mult, ALU.add)
                    last.then_inc(res_sb, 1)
                    norm_stats(dve, q, n)
            sweep(dve, 5, step)

        def store_out(sp, n):
            def step(at):
                if (q := at(4)):
                    sp.wait_ge(ln_x, 2 * (n + q.n + 1))
                    sp.dma_start(out[bass.ds(2 * q.n, 2)].rearrange("t p d -> p t d"),
                                 xg[:, bass.ds(2 * q.n, 2), :]).then_inc(out_done, 16)
            sweep(sp, 5, step)
            sp.wait_ge(out_done, 16 * SEQS)

        N = SEQS
        CONSTS_V = 3 * SLOTS + 1
        block = ctx.enter_context(nc.Block())

        @block.sync
        def _(sp):
            sp.dma_start(xg[:, :, :], x.rearrange("t p d -> p t d")).then_inc(x_in, 16)
            sp.dma_start(wm[:, :, :], mats.rearrange("p (m d) -> p m d", d=D)).then_inc(w_in, 16)
            sp.dma_start(cv[:, :], cols).then_inc(w_in, 16)
            sp.dma_start(row1[:, :], rows).then_inc(w_in, 16)
            sp.dma_start(rw0[:, :], router0).then_inc(w_in, 16)
            sp.dma_start(rw3[:, :], gate).then_inc(w_in, 16)
            sp.dma_start(wl[:, :, :], w_l3.rearrange("p (m d) -> p m d", d=LD)).then_inc(w_in, 16)
            for t in range(2):
                sp.dma_start(wo[t * LD:t * LD + LD, :], wo_l3).then_inc(w_in, 16)
            sp.wait_ge(consts, CONSTS)
            sp.dma_start(xs3[0:E3 * CAP3, :].rearrange("n d -> (n d)").rearrange("(e p k) -> p e k", p=P, e=E3),
                         zt[:, :].unsqueeze(1).to_broadcast([P, E3, CAP3])).then_inc(zeroed, 16)
            sp.dma_start(xs0[E0 * ROOM0:E0 * ROOM0 + 8 * S, :].rearrange("(e p r) d -> p e (r d)", p=P, e=8),
                         zt[:, 0:2 * D].unsqueeze(1).to_broadcast([P, 8, 2 * D])).then_inc(zeroed, 16)
            heads_sync(sp, 0, 0, 0)
            load_x_routed(sp, N, N, 0, 64)
            list_sync(sp)
            experts_sync(sp, 0, True)
            load_x_only(sp, 4, 2 * N, 2 * N)
            load_x_only(sp, 4, 3 * N, 3 * N)
            heads_sync(sp, N, 4 * N, 4 * N)
            load_x_only(sp, 4, 5 * N, 5 * N)
            load_x_only(sp, 4, 6 * N, 6 * N)
            load_x_routed(sp, 7 * N, 7 * N, 64 * N, 32)
            experts_sync(sp, NG, False)
            store_out(sp, 7 * N)

        @block.tensor
        def _(pe):
            pe.wait_ge(w_in, W_IN)
            pe.wait_ge(consts, CONSTS)
            pe.wait_ge(consts_v, CONSTS_V)
            pe.matmul(po0[:, 0:3 * D], ones[0:1, :], row1[:, :], start=True, stop=True).then_inc(rows_ps, 1)
            pe.wait_ge(rows_sb, len(ROWS))
            heads_tensor(pe, 0, 0, False, 0)
            route_tensor(pe, 0, N, E0, rw0)
            list_tensor(pe)
            experts_tensor(pe, 0, S, NG, IN0, 0)
            single_tensor(pe, 2 * N, 2 * N)
            mixing_tensor(pe, 0, 3 * N, 1)
            heads_tensor(pe, N, 4 * N, True, 2)
            mixing_tensor(pe, N, 5 * N, 2)
            linear_tensor(pe, 6 * N, 6 * N)
            route_tensor(pe, N, 7 * N, E3, rw3)
            experts_tensor(pe, NG, CAP3, E3, IN3, IN0 * NG)

        @block.scalar
        def _(act):
            heads_scalar(act, 0, 0, False)
            route_scalar(act, 0, N, E0)
            experts_scalar(act, 0, S, NG, True)
            single_scalar(act, 2 * N)
            mixing_scalar(act, 0, 3 * N)
            heads_scalar(act, N, 4 * N, True)
            mixing_scalar(act, N, 5 * N)
            linear_scalar(act, 6 * N)
            route_scalar(act, N, 7 * N, E3)
            experts_scalar(act, NG, CAP3, E3, False)

        @block.vector
        def _(dve):
            for i in range(SLOTS):
                nc.vector.memset(va[i][:, :, :, DH:DH + 1], 1.0).then_inc(consts_v, 1)
                nc.vector.memset(va[i][:, :, :, DH + 1:], 0.0).then_inc(consts_v, 1)
                nc.vector.memset(xt[i][:, 0:1], 0.0).then_inc(consts_v, 1)
            dve.wait_ge(w_in, W_IN)
            nc.vector.tensor_scalar(omu[:, :], cv[:, COLS.index("mr1"):COLS.index("mr1") + 4], -1.0, 1.0,
                                    ALU.mult, ALU.add).then_inc(consts_v, 1)
            dve.wait_ge(rows_ps, 1)
            for i in range(len(ROWS)):
                nc.vector.tensor_copy(rowb[:, i, :], po0[:, i * D:i * D + D]).then_inc(rows_sb, 1)
            dve.wait_ge(rows_sb, len(ROWS))
            dve.wait_ge(consts_v, CONSTS_V)
            dve.wait_ge(x_in, 16)
            heads_vector(dve, 0, 0, False, 0)
            route_vector(dve, 0, E0, 2, base0)
            list_vector(dve)
            experts_vector(dve, 0, S, NG, True, 16, 0)
            gather_vector(dve, 0, N, 2, 0)
            single_vector(dve, 2 * N)
            mixing_vector(dve, 0, 3 * N, 3 * N, 1)
            heads_vector(dve, N, 4 * N, True, 2)
            mixing_vector(dve, N, 5 * N, 5 * N, 2)
            linear_vector(dve, 6 * N)
            dve.wait_ge(wt_sb, 5 * N)
            route_vector(dve, N, E3, 1, base3)
            experts_vector(dve, NG, CAP3, E3, False, 32, 16 * NG)
            gather_vector(dve, N, 7 * N, 1, 64 * N)

        @block.gpsimd
        def _(pool):
            g = nc.gpsimd
            for t, v in ((ident, 0.0), (ones, 1.0), (upto, 1.0), (hide_k, 0.0), (hide_q, 0.0), (half, -0.5),
                         (zt, 0.0), (zero_col, 0.0), (ones16, 1.0), (upto16, 1.0), (ident16, 0.0)):
                g.memset(t[tuple([slice(None)] * len(t.shape))], v).then_inc(cleared, 1)
            for i in range(SLOTS):
                g.memset(ks[i][:, :, :], 1.0).then_inc(cleared, 1)
            pool.wait_ge(cleared, 11 + SLOTS)
            for t in (ident, ident16):
                g.affine_select(out=t[:, :], in_=t[:, :], compare_op=ALU.not_equal, fill=1.0, base=0,
                                pattern=[[-1, P]], channel_multiplier=1).then_inc(consts, 1)
            for t in (upto[:, 0, :], upto16[:, :]):
                g.affine_select(out=t, in_=t, compare_op=ALU.is_ge, fill=0.0, base=0,
                                pattern=[[1, P]], channel_multiplier=-1).then_inc(consts, 1)
            g.affine_select(out=hide_k[:, :], in_=hide_k[:, :], compare_op=ALU.is_ge, fill=HIDE, base=0,
                            pattern=[[1, P]], channel_multiplier=-1).then_inc(consts, 1)
            g.affine_select(out=hide_q[:, :], in_=hide_q[:, :], compare_op=ALU.is_ge, fill=HIDE, base=0,
                            pattern=[[-1, P]], channel_multiplier=1).then_inc(consts, 1)
            ig = {"allow_small_or_imprecise_dtypes": True}
            g.iota(iota_e[:, :], [[1, EM]], base=0, channel_multiplier=0, **ig).then_inc(consts, 1)
            g.iota(iota_g[:, :], [[1, NG]], base=0, channel_multiplier=0, **ig).then_inc(consts, 1)
            g.iota(dump[:, :], [[P, TILES]], base=DUMP, channel_multiplier=1, **ig).then_inc(consts, 1)
            g.iota(base0[:, :, :], [[0, 2], [ROOM0, E0]], base=-1, channel_multiplier=0, **ig).then_inc(consts, 1)
            g.iota(base3[:, :, :], [[0, 2], [CAP3, E3]], base=-1, channel_multiplier=0, **ig).then_inc(consts, 1)
            heads_pool(pool, 0, 0, 0)
            route_pool(pool, 0, 2, xs0)
            gather_pool(pool, 0, N, 2, ys0, 16 * NG, 0)
            norm_pool(pool, 2 * N, 4, 2)
            mixing_pool(pool, 0, 3 * N)
            heads_pool(pool, N, 4 * N, 2)
            mixing_pool(pool, N, 5 * N)
            norm_pool(pool, 6 * N, 4, 2)
            route_pool(pool, N, 1, xs3)
            gather_pool(pool, N, 7 * N, 1, ys3, 16 * NG + 32 * E3, 64 * N)


_INS = ["x", "mats", "cols", "rows", "router0", "w1_0", "b1_0", "w2_0", "b2_0", "w_l3", "wo_l3", "gate",
        "w1_3", "w2_3"]


def kernel(**inputs):
    import numpy as _np
    import concourse.bacc as _bacc
    from concourse import mybir as _mybir
    from concourse.bass_utils import run_bass_kernel_spmd as _run

    a = {k: _np.asarray(v) for k, v in inputs.items()}

    def turned(w):
        return w.T

    def by_dim(w):
        return w.reshape(HEADS, DH, D).transpose(1, 0, 2).reshape(D, D).T

    def col_by_dim(b):
        return b.reshape(HEADS, DH).T.reshape(D)

    w1 = a["L1_attn_W"]
    b1 = a["L1_attn_b"]
    mats = [by_dim(a["L0_attn_Wq"]), by_dim(a["L0_attn_Wk"]), turned(a["L0_attn_Wv"]), turned(a["L0_attn_Wo"]),
            turned(w1[0:D]), turned(w1[D:2 * D]), turned(w1[2 * D:3 * D]),
            turned(a["L1_ffn_W_r"]), turned(a["L1_ffn_W_k"]), turned(a["L1_ffn_W_v"]),
            by_dim(a["L2_attn_Wq"]), by_dim(a["L2_attn_Wk"]), turned(a["L2_attn_Wv"]), turned(a["L2_attn_Wo"]),
            turned(a["L2_ffn_W_r"]), turned(a["L2_ffn_W_k"]), turned(a["L2_ffn_W_v"])]
    cols = [col_by_dim(a["L0_attn_bq"]), col_by_dim(a["L0_attn_bk"]), b1[0:D], b1[D:2 * D],
            a["L1_ffn_mu_r"], a["L1_ffn_mu_k"], a["L2_ffn_mu_r"], a["L2_ffn_mu_k"]]
    laid = {
        "x": a["L0_attn_x"].reshape(TILES, P, D),
        "mats": _np.concatenate(mats, axis=1),
        "cols": _np.stack(cols, axis=1),
        "rows": _np.concatenate([a["L0_attn_bv"], a["L0_attn_bo"], b1[2 * D:3 * D]]).reshape(1, 3 * D),
        "router0": a["L0_ffn_router_w"],
        "w1_0": a["L0_ffn_w1"],
        "b1_0": a["L0_ffn_b1"].reshape(E0, FC, P).transpose(0, 2, 1),
        "w2_0": a["L0_ffn_w2"],
        "b2_0": a["L0_ffn_b2"].reshape(E0, D, 1),
        "w_l3": _np.concatenate([a["L3_attn_W_q"], a["L3_attn_W_k"], a["L3_attn_W_v"]], axis=1),
        "wo_l3": a["L3_attn_W_o"],
        "gate": a["L3_ffn_gate_w"].T,
        "w1_3": a["L3_ffn_w1"],
        "w2_3": a["L3_ffn_w2"],
    }
    nc = _bacc.Bacc("TRN2", target_bir_lowering=False, num_devices=1)
    arrays, args = {}, []
    for name in _INS:
        v = _np.ascontiguousarray(laid[name])
        arrays[f"in_{name}"] = v
        args.append(nc.dram_tensor(f"in_{name}", v.shape, _mybir.dt.from_np(v.dtype), kind="ExternalInput").ap())
    args.append(nc.dram_tensor("out_x", (TILES, P, D), F32, kind="ExternalOutput").ap())
    post_norm_stack(nc, *args)
    r = _run(nc, [arrays], core_ids=[0])
    return r.results[0]["out_x"].reshape(SEQS, S, D)
```

```python
from contextlib import ExitStack

import numpy as np

import concourse.bass as bass
from concourse import mybir

P = 128
D = 128
SEQS = 16
S = 256
TILES = SEQS * S // P
HEADS = 16
DH = D // HEADS
SLOTS = 4
EPS = 1e-5

E0 = 8
F = 512
FC = F // P
CAP0 = SEQS * S
ROOM0 = CAP0 + S
GROUPS0 = 2 * SEQS + E0 - 1
E3 = 16
CAP3 = 320
HIDE = -1e30

F32 = mybir.dt.float32
BF16 = mybir.dt.bfloat16
I32 = mybir.dt.int32
U32 = mybir.dt.uint32
ALU = mybir.AluOpType
ACT = mybir.ActivationFunctionType
AX = mybir.AxisListType

MATS = ["q0", "k0", "v0", "o0", "q1", "k1", "v1", "r1", "m1", "w1", "q2", "k2", "v2", "o2",
        "r2", "m2", "w2"]
COLS = ["bq0", "bk0", "bq1", "bk1", "mr1", "mk1", "mr2", "mk2"]
ROWS = ["bv0", "bo0", "bv1"]


class Seq:

    def __init__(self, n, slot, least, turn):
        self.n, self.slot, self.least, self.turn = n, slot, least, turn

    def back(self, k):
        return self.n - (k if isinstance(self.n, int) else min(k, self.least))


def sweep(eng, lags, step, n=SEQS, lead=0):
    def peeled(s):
        step(lambda k: Seq(s - k, (s - k) % SLOTS, s - k, (s - k) // SLOTS) if 0 <= s - k < n else None)

    first = lags - 1 + lead
    full = n - first
    for s in range(first):
        peeled(s)
    with eng.Fori(0, full // SLOTS) as i:
        for c in range(SLOTS):
            s0 = first + c
            step(lambda k: Seq(SLOTS * i + (s0 - k), (s0 - k) % SLOTS, s0 - k,
                               i + (s0 - k) // SLOTS))
    for s in range(first + full // SLOTS * SLOTS, n + lags - 1):
        peeled(s)


def behind(at, k):
    return lambda i: at(i + k)


def wait(eng, sem, n):
    if isinstance(n, int) and n <= 0:
        return
    eng.wait_ge(sem, n)


def wait_apart(eng, sem, n, passed):
    wait(eng, sem, n)
    eng.sem_inc(passed, 1)


def post_norm_stack(nc, x, mats, cols, rows, router0, pack0,
                    w_l3, wo_l3, gate, pack3, out):
    with ExitStack() as ctx:
        def sb(name, shape, dt=F32, at=ctx):
            return at.enter_context(nc.sbuf_tensor(name, shape, dt))

        def sem(name):
            return ctx.enter_context(nc.semaphore(name))

        xg = sb("xg", [P, TILES, D])
        wm = sb("wm", [P, len(MATS), D])
        cv = sb("cv", [P, len(COLS)])
        row1 = sb("row1", [1, len(ROWS) * D])
        rowb = sb("rowb", [P, len(ROWS), D])
        ident = sb("ident", [P, P])
        ident16 = sb("ident16", [P, P], BF16)
        ones = sb("ones", [P, P])
        upto = sb("upto", [P, 2, P])
        hide_k = sb("hide_k", [P, P], BF16)
        hide_q = sb("hide_q", [P, P], BF16)
        half = sb("half", [P, 2])
        omu = sb("omu", [P, 4])
        xs = [sb(f"xs{i}", [P, 2, D]) for i in range(SLOTS)]
        xt = [sb(f"xt{i}", [P, 1 + S]) for i in range(SLOTS)]
        res = [sb(f"res{i}", [P, 2, D]) for i in range(SLOTS)]
        st = [sb(f"st{i}", [P, 2, 6]) for i in range(SLOTS)]
        mv = [sb(f"mv{i}", [P, 2, 2]) for i in range(SLOTS)]
        ve = [sb(f"ve{i}", [P, 2, 1]) for i in range(SLOTS)]
        rstd = [sb(f"rstd{i}", [P, 2, 1]) for i in range(SLOTS)]
        zero_col = sb("zero_col", [P, 1])

        EM = max(E0, E3)
        NG = GROUPS0 + 1
        LD = 64
        rw0 = sb("rw0", [P, E0])
        rw3 = sb("rw3", [P, E3])
        wl = sb("wl", [P, 3, LD])
        wo = sb("wo", [P, D])
        iota_e = sb("iota_e", [P, EM])
        iota_g = sb("iota_g", [P, NG])
        base0 = sb("base0", [P, 2, E0])
        base3 = sb("base3", [P, 2, E3])
        dump = sb("dump", [P, TILES])
        upto16 = sb("upto16", [P, P], BF16)
        ones16 = sb("ones16", [P, P], BF16)
        zt = sb("zt", [P, CAP3])
        STACK, MAX_AT = 48, 96
        ks = [sb(f"ks{i}", [MAX_AT + 3, HEADS, S], BF16) for i in range(SLOTS)]
        va = [sb(f"va{i}", [P, 2, HEADS, 32]) for i in range(SLOTS)]

        with ExitStack() as mem:
            qs = [sb(f"qs{i}", [MAX_AT + 3, HEADS, S], BF16, mem) for i in range(SLOTS)]
            ex = [sb(f"ex{i}", [P, 4, S], F32, mem) for i in range(2)]
            qk = [sb(f"qk{i}", [P, 2, S], F32, mem) for i in range(2)]
            rem = [sb(f"rem{i}", [P, 2, S], F32, mem) for i in range(2)]
            parts = [sb(f"parts{i}", [P, 3, 2, S], BF16, mem) for i in range(2)]
            mx = [sb(f"mx{i}", [P, 2, HEADS], F32, mem) for i in range(2)]
            mr = [sb(f"mr{i}", [P, 2, HEADS], F32, mem) for i in range(2)]
            mp = [sb(f"mp{i}", [P, 2, 3, HEADS], BF16, mem) for i in range(2)]
            mt = [sb(f"mt{i}", [96, P], BF16, mem) for i in range(2)]
            ob = sb("ob", [P, 4, S], F32, mem)
            rc = [sb(f"rc{i}", [P, 2, HEADS], F32, mem) for i in range(2)]
            on = [sb(f"on{i}", [P, 2, D], F32, mem) for i in range(2)]
            ont = [sb(f"ont{i}", [P, S], F32, mem) for i in range(2)]
            xb = [sb(f"xb{i}", [P, 2, D], F32, mem) for i in range(SLOTS)]

        scr = nc.dram_tensor("scr", (SLOTS, 3, 2, P, S), BF16).ap()

        def psum(name, shape, dt=F32):
            return ctx.enter_context(nc.psum_tensor(name, shape, dt))

        p0 = psum("p0", [P, 512])
        p1 = psum("p1", [P, 512])
        pt = psum("pt", [P, 2, 512])
        pm = psum("pm", [P, 2, 512])
        po = psum("po", [P, 2, 512])

        passed = sem("passed")
        consts = sem("consts")
        consts_v = sem("consts_v")
        w_in = sem("w_in")
        x_in = sem("x_in")
        rows_ps = sem("rows_ps")
        rows_sb = sem("rows_sb")
        x_loaded = [sem(f"x_loaded{i}") for i in range(SLOTS)]
        xt_ps = sem("xt_ps")
        xt_sb = sem("xt_sb")
        res_sb = sem("res_sb")
        ln_st = sem("ln_st")
        ln_mv = sem("ln_mv")
        ln_ve = sem("ln_ve")
        ln_rs = sem("ln_rs")
        ln_x = sem("ln_x")
        out_done = sem("out_done")
        qk_ps = sem("qk_ps")
        v_ps = sem("v_ps")
        qk_sb = sem("qk_sb")
        v_sb = sem("v_sb")
        part1 = sem("part1")
        rest1 = sem("rest1")
        part2 = sem("part2")
        part3 = sem("part3")
        to_scr = sem("to_scr")
        stacked = [sem(f"stacked{i}") for i in range(SLOTS)]
        ms_ps = sem("ms_ps")
        ms_max = sem("ms_max")
        m_parts = sem("m_parts")
        mt_ps = sem("mt_ps")
        mt_sb = sem("mt_sb")
        mrows = [sem(f"mrows{i}") for i in range(SLOTS)]
        ts_ps = sem("ts_ps")
        e_sb = sem("e_sb")
        pv_ps = sem("pv_ps")
        o_sb = sem("o_sb")
        ot_ps = sem("ot_ps")
        o_rc = sem("o_rc")
        o_rc2 = sem("o_rc2")
        o_nrm = sem("o_nrm")
        ont_ps = sem("ont_ps")
        ont_sb = sem("ont_sb")
        y_ps = sem("y_ps")
        xb_sb = sem("xb_sb")

        W_IN = 16 * 8
        CONSTS = 11
        cleared = sem("cleared")
        qs_zero = sem("qs_zero")
        SPLITS = 16 * 6

        def mat(name):
            return wm[:, MATS.index(name), :]

        def col(name):
            return cv[:, COLS.index(name):COLS.index(name) + 1]

        def row(name):
            return rowb[:, ROWS.index(name), :]

        def load_x(sp, q, done, normed):
            sp.wait_ge(ln_x, 2 * normed) if normed else sp.wait_ge(x_in, 16)
            wait_apart(sp, xt_ps, done + q.back(3), passed)
            sp.dma_start(xs[q.slot][:, :, :], xg[:, bass.ds(2 * q.n, 2), :]).then_inc(x_loaded[q.slot], 16)

        def transpose_x(pe, q, done):
            pe.wait_ge(x_loaded[q.slot], 16 * (done // SLOTS + q.turn + 1))
            pe.transpose(p0[:, 0:P], xs[q.slot][:, 0, :], ident[:, :])
            pe.transpose(p0[:, P:S], xs[q.slot][:, 1, :], ident[:, :]).then_inc(xt_ps, 1)

        def copy_xt(act, q, done):
            act.wait_ge(xt_ps, done + q.n + 1)
            nc.scalar.copy(xt[q.slot][:, 1:1 + S], p0[:, 0:S]).then_inc(xt_sb, 1)

        def norm_stats(dve, q, done):
            dve.wait_ge(res_sb, done + q.n + 1)
            for t in range(2):
                nc.vector.bn_stats(st[q.slot][:, t, :], res[q.slot][:, t, :]).then_inc(ln_st, 1)
            for t in range(2):
                wait_apart(dve, ln_st, 2 * (done + q.n) + 1 + t, passed)
                nc.vector.bn_aggr(mv[q.slot][:, t, :], st[q.slot][:, t, :]).then_inc(ln_mv, 1)

        def norm_rstd(pool, q, done):
            wait_apart(pool, ln_mv, 2 * (done + q.n + 1), passed)
            nc.gpsimd.tensor_scalar(ve[q.slot][:, :, :], mv[q.slot][:, :, 1:2], EPS, None,
                                    ALU.add).then_inc(ln_ve, 1)
            pool.wait_ge(ln_ve, done + q.n + 1)
            nc.gpsimd.tensor_tensor(rstd[q.slot][:, :, :], ve[q.slot][:, :, :],
                                    half[:, :].unsqueeze(2), ALU.pow).then_inc(ln_rs, 1)

        def norm_apply(dve, q, done):
            dve.wait_ge(ln_rs, done + q.n + 1)
            for t in range(2):
                nc.vector.tensor_scalar(xg[:, bass.ds(2 * q.n + t, 1), :], res[q.slot][:, t:t + 1, :],
                                        mv[q.slot][:, t, 0:1], rstd[q.slot][:, t, :],
                                        ALU.subtract, ALU.mult).then_inc(ln_x, 1)

        M0 = 1
        T0 = 4
        V0 = T0 + 1

        def heads_sync(sp, a, g, n):
            def step(at):
                if (q := at(0)):
                    load_x(sp, q, g, n)
                if (q := at(3)):
                    sp.wait_ge(mt_sb, a + q.n + 1)
                    for t in range(2):
                        sp.dma_start(qs[q.slot][MAX_AT:MAX_AT + 3, :, t * P:t * P + P],
                                     mt[q.slot % 2][STACK * t:STACK * t + STACK, :]).then_inc(mrows[q.slot], 16)
                if (q := at(1)):
                    sp.wait_ge(part3, a + q.n + 1)
                    sp.dma_start(scr[q.slot].rearrange("t i p k -> p (t i) k"),
                                 parts[q.slot % 2][:, :, :, :].rearrange("p t i k -> p (t i) k")).then_inc(to_scr, 16)
                    wait_apart(sp, to_scr, 16 * (a + q.n + 1), passed)
                    wait_apart(sp, ts_ps, 16 * (a + q.back(3)), passed)
                    sp.wait_ge(qs_zero, SLOTS * (1 if a == 0 else 2))
                    for first, n_rows in ((0, 24), (24, 16), (40, 8)):
                        src = scr[q.slot, 0:n_rows // DH, 0].rearrange("t (d h) k -> t d (h k)", h=HEADS)
                        sp.dma_start(qs[q.slot][first:first + n_rows, :, :].rearrange("r h k -> r (h k)"), src).then_inc(stacked[q.slot], 16)
                        src = scr[q.slot, 3 - n_rows // DH, 1].rearrange("(d h) k -> d (h k)", h=HEADS)
                        sp.dma_start(ks[q.slot][first:first + n_rows, :, :].rearrange("r h k -> r (h k)"),
                                     src.unsqueeze(0).to_broadcast([n_rows // DH, DH, HEADS * S])
                                     ).then_inc(stacked[q.slot], 16)
            sweep(sp, 6, step)

        def heads_tensor(pe, a, g, causal, layer):
            def scores_t(q, j, u):
                b, kt = j // 2, j % 2
                pe.wait_ge(stacked[q.slot], SPLITS * (a // SLOTS + q.turn + 1))
                pe.wait_ge(mrows[q.slot], 32 * (a // SLOTS + q.turn + 1))
                wait(pe, e_sb, 16 * (a + q.n) + 2 * j + u - 1)
                for i in (2 * u, 2 * u + 1):
                    h = 4 * b + i
                    dst = pt[:, i // 2, (i % 2) * S:(i % 2) * S + S]
                    lhs = ks[q.slot][:, h, kt * P:kt * P + P]
                    rhs = qs[q.slot][:, h, :]
                    if not causal:
                        last = pe.matmul(dst, lhs, rhs, start=True, stop=True)
                        continue
                    d0 = kt * P
                    pe.matmul(dst[:, d0:d0 + P], ident16[:, :], hide_k[:, :], start=True, stop=False)
                    last = pe.matmul(dst[:, d0:d0 + P], lhs, rhs[:, d0:d0 + P], start=False, stop=True)
                    if kt == 0:
                        last = pe.matmul(dst[:, P:S], lhs, rhs[:, P:S], start=True, stop=True)
                last.then_inc(ts_ps, 1)

            def scores_m(q, j, u):
                b, qt = j // 2, j % 2
                if j == 0:
                    pe.wait_ge(stacked[q.slot], SPLITS * (a // SLOTS + q.turn + 1))
                wait(pe, ms_max, 16 * (a + q.n) + 2 * j + u - 1)
                for i in (2 * u, 2 * u + 1):
                    h = 4 * b + i
                    dst = pm[:, i // 2, (i % 2) * S:(i % 2) * S + S]
                    lhs = qs[q.slot][0:MAX_AT, h, qt * P:qt * P + P]
                    rhs = ks[q.slot][0:MAX_AT, h, :]
                    if not causal:
                        last = pe.matmul(dst, lhs, rhs, start=True, stop=True)
                        continue
                    d0 = qt * P
                    if qt == 1:
                        pe.matmul(dst[:, 0:P], lhs, rhs[:, 0:P], start=True, stop=True)
                    pe.matmul(dst[:, d0:d0 + P], ident16[:, :], hide_q[:, :], start=True, stop=False)
                    last = pe.matmul(dst[:, d0:d0 + P], lhs, rhs[:, d0:d0 + P], start=False, stop=True)
                last.then_inc(ms_ps, 1)

            def times_v(q, j):
                b, kt = j // 2, j % 2
                pe.wait_ge(e_sb, 16 * (a + q.n) + 2 * j + 2)
                pe.wait_ge(v_sb, 2 * (a + q.n + 1))
                if j == 0:
                    wait(pe, o_sb, a + q.n)
                lo = kt * P if causal else 0
                for i in range(4):
                    c0 = (b % 2) * S
                    last = pe.matmul(po[32 * i:32 * i + 32, b // 2, c0 + lo:c0 + S],
                                     va[q.slot][:, kt, 4 * b + i, :], ex[j % 2][:, i, lo:S],
                                     start=(kt == 0), stop=(kt == 1))
                last.then_inc(pv_ps, 1)

            def between(at, j, u):
                if (j, u) == (0, 0) and (q := at(0)):
                    wait(pe, v_sb, 2 * (a + q.n))
                    wait(pe, ont_sb, a + q.back(3))
                    transpose_x(pe, q, g)
                if (j, u) == (0, 1) and (q := at(4)):
                    pe.wait_ge(ont_sb, a + q.n + 1)
                    for t in range(2):
                        last = pe.matmul(p1[:, t * P:t * P + P], ont[q.slot % 2][:, t * P:t * P + P],
                                         mat(f"o{layer}"), start=True, stop=True)
                    last.then_inc(y_ps, 1)
                if j == 1 and (q := at(0)):
                    xq = xt[q.slot][:, 1:1 + S]
                    if u == 0:
                        pe.wait_ge(xt_sb, g + q.n + 1)
                        wait(pe, qk_sb, 2 * (a + q.n))
                        wait(pe, res_sb, n_of(layer) + q.back(3))
                        pe.matmul(p1[:, 0:S], mat(f"q{layer}"), xq, start=True, stop=True)
                    else:
                        pe.matmul(p1[:, S:2 * S], mat(f"k{layer}"), xq, start=True, stop=True).then_inc(qk_ps, 1)
                if (j, u) == (1, 1) and (q := at(2)):
                    if at(0):
                        pe.wait_ge(xt_sb, g + at(0).n + 1)
                    elif at(1):
                        pe.wait_ge(v_sb, 2 * (a + at(1).n + 1))
                    wait_apart(pe, m_parts, 4 * (a + q.n + 1), passed)
                    pe.transpose(p0[0:96, S:2 * S].bitcast(BF16)[:, 0:P],
                                 mp[q.slot % 2][:, :, :, :].rearrange("p t c h -> p (t c h)"),
                                 ident16[:, :]).then_inc(mt_ps, 1)
                if (j, u) == (2, 0) and (q := at(0)):
                    if at(2):
                        pe.wait_ge(mt_sb, a + at(2).n + 1)
                    for t in range(2):
                        last = pe.matmul(p0[:, t * P:t * P + P], xt[q.slot][:, 1 + t * P:1 + t * P + P],
                                         mat(f"v{layer}"), start=True, stop=True)
                    last.then_inc(v_ps, 1)
                if j == 6 and (q := at(3)):
                    if u == 0:
                        pe.wait_ge(o_sb, a + q.n + 1)
                        if at(2):
                            pe.wait_ge(mt_sb, a + at(2).n + 1)
                        if at(4):
                            pe.wait_ge(res_sb, n_of(layer) + at(4).n + 1)
                        if at(0):
                            pe.wait_ge(v_sb, 2 * (a + at(0).n + 1))
                            pe.wait_ge(qk_sb, 2 * (a + at(0).n + 1))
                    for b in range(4):
                        last = pe.transpose((p0, p1)[u][:, b * P:b * P + P], ob[:, b, u * P:u * P + P], ident[:, :])
                    if u == 1:
                        last.then_inc(ot_ps, 1)
                if (j, u) == (7, 1) and (q := at(3)):
                    pe.wait_ge(o_nrm, 2 * (a + q.n + 1))
                    for t in range(2):
                        last = pe.transpose(p0[:, t * P:t * P + P], on[q.slot % 2][:, t, :], ident[:, :])
                    last.then_inc(ont_ps, 1)

            def step(at):
                for j in range(8):
                    for u in range(2):
                        if (q := at(2) if j >= T0 else at(3)):
                            scores_t(q, (j - T0) % 8, u)
                        if (q := at(1) if j >= M0 else at(2)):
                            scores_m(q, (j - M0) % 8, u)
                        between(at, j, u)
                    if (q := at(2) if j >= V0 else at(3)):
                        times_v(q, (j - V0) % 8)
            sweep(pe, 5, step)

        def n_of(layer):
            return 0 if layer == 0 else 4 * SEQS

        def heads_scalar(act, a, g, causal):
            def exps(q, j):
                wait(act, pv_ps, 8 * (a + q.n) + j - 1)
                lo = P if causal and j % 2 else 0
                for u in range(2):
                    act.wait_ge(ts_ps, 16 * (a + q.n) + 2 * j + u + 1)
                    nc.scalar.activation(ex[j % 2][:, 2 * u:2 * u + 2, lo:S],
                                         pt[:, u, :].rearrange("p (b k) -> p b k", k=S)[:, :, lo:S],
                                         ACT.Exp).then_inc(e_sb, 1)

            def step(at):
                for j in range(8):
                    if j == V0 and (q := at(3)):
                        act.wait_ge(pv_ps, 8 * (a + q.n + 1))
                        wait(act, ot_ps, a + q.n)
                        nc.scalar.copy(ob[:, :, :], po[:, :, :].rearrange("p a (b k) -> p (a b) k", k=S)
                                       ).then_inc(o_sb, 1)
                    if (q := at(2) if j >= T0 else at(3)):
                        exps(q, (j - T0) % 8)
                    if j == 0 and (q := at(0)):
                        copy_xt(act, q, g)
                    if j == 1 and (q := at(2)):
                        act.wait_ge(mt_ps, a + q.n + 1)
                        wait(act, ts_ps, 16 * (a + q.back(1)))
                        nc.scalar.copy(mt[q.slot % 2][:, :], p0[0:96, S:2 * S].bitcast(BF16)[:, 0:P]
                                       ).then_inc(mt_sb, 1)
                    if j == 2 and (q := at(0)):
                        act.wait_ge(qk_sb, 2 * (a + q.n + 1))
                        wait(act, to_scr, 16 * (a + q.back(1)))
                        nc.scalar.copy(parts[q.slot % 2][:, 0, :, :], qk[q.slot % 2][:, :, :]).then_inc(part1, 1)
                    if j == 3 and (q := at(0)):
                        act.wait_ge(rest1, a + q.n + 1)
                        nc.scalar.copy(parts[q.slot % 2][:, 1, :, :], rem[q.slot % 2][:, :, :]).then_inc(part2, 1)
                    if j == 7 and (q := at(3)):
                        act.wait_ge(ont_ps, a + q.n + 1)
                        wait(act, y_ps, a + q.back(1))
                        nc.scalar.copy(ont[q.slot % 2][:, :], p0[:, 0:S]).then_inc(ont_sb, 1)
            sweep(act, 5, step)

        def heads_vector(dve, a, n, causal, layer):
            def row_max(q, j):
                b, qt = j // 2, j % 2
                if j == 0:
                    wait(dve, m_parts, 4 * (a + q.back(1)))
                hi = P if causal and qt == 0 else S
                for u in range(2):
                    dve.wait_ge(ms_ps, 16 * (a + q.n) + 2 * j + u + 1)
                    nc.vector.tensor_reduce(mx[q.slot % 2][:, qt, 4 * b + 2 * u:4 * b + 2 * u + 2],
                                            pm[:, u, :].rearrange("p (b k) -> p b k", k=S)[:, :, 0:hi],
                                            AX.X, ALU.max).then_inc(ms_max, 1)

            def split_max(q):
                s = q.slot % 2
                k = 4 * (a + q.n)
                dve.wait_ge(ms_max, 16 * (a + q.n + 1))
                wait(dve, mt_ps, a + q.back(1))
                nc.vector.tensor_scalar(mp[s][:, :, 0, :], mx[s][:, :, :], -1.0, None,
                                        ALU.mult).then_inc(m_parts, 1)
                dve.wait_ge(m_parts, k + 1)
                nc.vector.scalar_tensor_tensor(mr[s][:, :, :], mx[s][:, :, :], -1.0, mp[s][:, :, 0, :],
                                               ALU.mult, ALU.subtract).then_inc(m_parts, 1)
                dve.wait_ge(m_parts, k + 2)
                nc.vector.tensor_copy(mp[s][:, :, 1, :], mr[s][:, :, :]).then_inc(m_parts, 1)
                dve.wait_ge(m_parts, k + 3)
                nc.vector.tensor_tensor(mp[s][:, :, 2, :], mr[s][:, :, :], mp[s][:, :, 1, :],
                                        ALU.subtract).then_inc(m_parts, 1)

            def step(at):
                for j in range(8):
                    if (q := at(1) if j >= M0 else at(2)):
                        row_max(q, (j - M0) % 8)
                    if j == 0 and (q := at(4)):
                        dve.wait_ge(y_ps, a + q.n + 1)
                        wait(dve, ln_x, 2 * (n + q.back(3)))
                        y = p1[:, 0:S].rearrange("p (t d) -> p t d", t=2)
                        if layer == 0:
                            dve.wait_ge(xb_sb, q.n + 1)
                            nc.vector.tensor_tensor(res[q.slot][:, :, :], y, xb[q.slot][:, :, :],
                                                    ALU.add).then_inc(res_sb, 1)
                        else:
                            nc.vector.tensor_tensor(res[q.slot][:, :, :], y,
                                                    xg[:, bass.ds(2 * q.n, 2), :], ALU.add).then_inc(res_sb, 1)
                    if j == M0 - 1 and (q := at(2)):
                        split_max(q)
                    if j == 0 and (q := at(4)):
                        norm_stats(dve, q, n)
                    if j == 1 and (q := at(0)):
                        dve.wait_ge(qk_ps, a + q.n + 1)
                        wait(dve, part3, a + q.back(1))
                        c = float(DH) ** -0.5
                        if layer == 0:
                            nc.vector.tensor_scalar(qk[q.slot % 2][:, 0, :], p1[:, 0:S], col("bq0"), c,
                                                    ALU.add, ALU.mult).then_inc(qk_sb, 1)
                            nc.vector.tensor_scalar(qk[q.slot % 2][:, 1, :], p1[:, S:2 * S], col("bk0"), None,
                                                    ALU.add).then_inc(qk_sb, 1)
                        else:
                            nc.vector.tensor_scalar(qk[q.slot % 2][:, 0, :], p1[:, 0:S], c, None,
                                                    ALU.mult).then_inc(qk_sb, 1)
                            nc.vector.tensor_copy(qk[q.slot % 2][:, 1, :], p1[:, S:2 * S]).then_inc(qk_sb, 1)
                    if j == 2 and (q := at(0)):
                        dve.wait_ge(v_ps, a + q.n + 1)
                        for t in range(2):
                            v = p0[:, t * P:t * P + P].rearrange("p (h d) -> p h d", h=HEADS)
                            dst = va[q.slot][:, t, :, 0:DH]
                            if layer == 0:
                                nc.vector.tensor_tensor(dst, v, row("bv0").rearrange("p (h d) -> p h d", h=HEADS),
                                                        ALU.add).then_inc(v_sb, 1)
                            else:
                                nc.vector.tensor_copy(dst, v).then_inc(v_sb, 1)
                    if j == 2 and (q := at(4)):
                        norm_apply(dve, q, n)
                    if j == 6 and (q := at(3)):
                        dve.wait_ge(ot_ps, a + q.n + 1)
                        for t, bank in ((0, p0), (1, p1)):
                            o = bank[:, :].rearrange("p (h d) -> p h d", d=32)
                            r = rc[q.slot % 2][:, t, :]
                            if layer == 2:
                                nc.vector.tensor_scalar(r.unsqueeze(2), o[:, :, DH:DH + 1], 1e-12, None,
                                                        ALU.max).then_inc(o_rc, 1)
                                dve.wait_ge(o_rc, 2 * q.n + t + 1)
                                nc.vector.reciprocal(r, r).then_inc(o_rc2, 1)
                            else:
                                nc.vector.reciprocal(r.unsqueeze(2), o[:, :, DH:DH + 1]).then_inc(o_rc2, 1)
                        for t, bank in ((0, p0), (1, p1)):
                            dve.wait_ge(o_rc2, 2 * (a + q.n) + t + 1)
                            o = bank[:, :].rearrange("p (h d) -> p h d", d=32)
                            nc.vector.tensor_tensor(on[q.slot % 2][:, t, :].rearrange("p (h d) -> p h d", h=HEADS),
                                                    o[:, :, 0:DH],
                                                    rc[q.slot % 2][:, t, :].unsqueeze(2).to_broadcast([P, HEADS, DH]),
                                                    ALU.mult).then_inc(o_nrm, 1)
            sweep(dve, 5, step)

        def heads_pool(pool, a, n, layer):
            for i in range(SLOTS):
                nc.gpsimd.memset(qs[i][0:MAX_AT, :, :], 0.0).then_inc(qs_zero, 1)

            def step(at):
                if (q := at(4)):
                    norm_rstd(pool, q, n)
                if (q := at(0)):
                    s = q.slot % 2
                    pool.wait_ge(part1, a + q.n + 1)
                    nc.gpsimd.tensor_tensor(rem[s][:, :, :], qk[s][:, :, :], parts[s][:, 0, :, :],
                                            ALU.subtract).then_inc(rest1, 1)
                    pool.wait_ge(part2, a + q.n + 1)
                    nc.gpsimd.tensor_tensor(parts[s][:, 2, :, :], rem[s][:, :, :], parts[s][:, 1, :, :],
                                            ALU.subtract).then_inc(part3, 1)
                if layer == 0 and (q := at(3)):
                    pool.wait_ge(x_in, 16)
                    pool.wait_ge(rows_sb, len(ROWS))
                    wait(pool, res_sb, q.back(3))
                    for t in range(2):
                        ins = nc.gpsimd.tensor_tensor(xb[q.slot][:, t:t + 1, :], xg[:, bass.ds(2 * q.n + t, 1), :],
                                                      row("bo0").unsqueeze(1), ALU.add)
                    ins.then_inc(xb_sb, 1)
            sweep(pool, 5, step)

        pt0, pt1, pm0, pm1, po0, po1 = (b[:, i, :] for b in (pt, pm, po) for i in range(2))
        with ExitStack() as mem:
            kq = [sb(f"kq{i}", [P, 2, S], F32, mem) for i in range(2)]
            v1 = [sb(f"v1_{i}", [P, 2, D], F32, mem) for i in range(2)]
            vn = [sb(f"vn{i}", [P, 2, D], F32, mem) for i in range(2)]
            e1 = [sb(f"e1_{i}", [P, 2, S], F32, mem) for i in range(2)]
            m1 = [sb(f"m1_{i}", [P, 2], F32, mem) for i in range(2)]
            nb1 = [sb(f"nb1_{i}", [P, 2], F32, mem) for i in range(2)]
            sum1 = [sb(f"sum1_{i}", [P, 2], F32, mem) for i in range(2)]
            inv1 = [sb(f"inv1_{i}", [P, 2], F32, mem) for i in range(2)]
        kq_ps, kq_sb, v1_ps, v1_sb = sem("kq_ps"), sem("kq_sb"), sem("v1_ps"), sem("v1_sb")
        s1_ps, s1_max, s1_nb, e1_sb = sem("s1_ps"), sem("s1_max"), sem("s1_nb"), sem("e1_sb")
        inv1_sb, vn_sb, y1_ps = sem("inv1_sb"), sem("vn_sb"), sem("y1_ps")

        def single_tensor(pe, g, n):
            def step(at):
                if (q := at(0)):
                    wait(pe, xt_sb, g + q.n)
                    transpose_x(pe, q, g)
                at = behind(at, 1)
                if (q := at(3)):
                    s = q.slot % 2
                    pe.wait_ge(vn_sb, 2 * (q.n + 1))
                    wait(pe, res_sb, n + q.back(1))
                    for i in range(2):
                        for t in range(2):
                            last = pe.matmul((po0, po1)[s][:, i * P:i * P + P], e1[s][:, t, i * P:i * P + P],
                                             vn[s][:, t, :], start=(t == 0), stop=(t == 1))
                    last.then_inc(y1_ps, 1)
                if (q := at(1)):
                    s = q.slot % 2
                    pe.wait_ge(kq_sb, 2 * (q.n + 1))
                    wait(pe, e1_sb, 2 * q.back(1))
                    for t in range(2):
                        last = pe.matmul((pt1, pm1)[s][:, t * S:t * S + S], kq[s][:, 1, t * P:t * P + P], kq[s][:, 0, :],
                                         start=True, stop=True)
                    last.then_inc(s1_ps, 1)
                if (q := at(0)):
                    pe.wait_ge(xt_sb, g + q.n + 1)
                    wait(pe, kq_sb, 2 * q.n)
                    xq = xt[q.slot][:, 1:1 + S]
                    pe.matmul(p1[:, 0:S], mat("q1"), xq, start=True, stop=True)
                    pe.matmul(p1[:, S:2 * S], mat("k1"), xq, start=True, stop=True).then_inc(kq_ps, 1)
                    wait(pe, v1_sb, q.n)
                    for t in range(2):
                        last = pe.matmul(pt0[:, t * P:t * P + P], xq[:, t * P:t * P + P], mat("v1"),
                                         start=True, stop=True)
                    last.then_inc(v1_ps, 1)
            sweep(pe, 6, step)

        def single_scalar(act, g):
            def step(at):
                if (q := at(0)):
                    copy_xt(act, q, g)
                at = behind(at, 1)
                if (q := at(1)):
                    s = q.slot % 2
                    act.wait_ge(s1_nb, q.n + 1)
                    wait(act, y1_ps, q.back(1))
                    for t in range(2):
                        nc.scalar.activation(e1[s][:, t, :], (pt1, pm1)[s][:, t * S:t * S + S], ACT.Exp,
                                             bias=nb1[s][:, t:t + 1], scale=1.0 / D,
                                             accum_out=sum1[s][:, t:t + 1]).then_inc(e1_sb, 1)
                if (q := at(0)):
                    act.wait_ge(kq_ps, q.n + 1)
                    wait(act, s1_ps, q.back(1))
                    for i, b in enumerate(("bq1", "bk1")):
                        nc.scalar.activation(kq[q.slot % 2][:, i, :], p1[:, i * S:i * S + S], ACT.Identity,
                                             bias=col(b)).then_inc(kq_sb, 1)
            sweep(act, 6, step)

        def single_vector(dve, n):
            def step(at):
                at = behind(at, 1)
                if (q := at(2)):
                    s = q.slot % 2
                    dve.wait_ge(e1_sb, 2 * (q.n + 1))
                    nc.vector.reciprocal(inv1[s][:, :], sum1[s][:, :]).then_inc(inv1_sb, 1)
                    dve.wait_ge(inv1_sb, q.n + 1)
                    dve.wait_ge(v1_sb, q.n + 1)
                    for t in range(2):
                        nc.vector.tensor_scalar(vn[s][:, t, :], v1[s][:, t, :], inv1[s][:, t:t + 1], None,
                                                ALU.mult).then_inc(vn_sb, 1)
                if (q := at(1)):
                    s = q.slot % 2
                    dve.wait_ge(s1_ps, q.n + 1)
                    nc.vector.tensor_reduce(m1[s][:, :], (pt1, pm1)[s][:, :].rearrange("p (t k) -> p t k", t=2), AX.X,
                                            ALU.max).then_inc(s1_max, 1)
                    dve.wait_ge(s1_max, q.n + 1)
                    nc.vector.tensor_scalar(nb1[s][:, :], m1[s][:, :], -1.0 / D, None,
                                            ALU.mult).then_inc(s1_nb, 1)
                if (q := at(0)):
                    s = q.slot % 2
                    dve.wait_ge(v1_ps, q.n + 1)
                    wait(dve, vn_sb, 2 * (q.back(1)))
                    nc.vector.tensor_tensor(v1[s][:, :, :], pt0[:, 0:S].rearrange("p (t d) -> p t d", t=2),
                                            row("bv1").unsqueeze(1).to_broadcast([P, 2, D]), ALU.add).then_inc(v1_sb, 1)
                if (q := at(4)):
                    norm_apply(dve, q, n)
                if (q := at(3)):
                    dve.wait_ge(y1_ps, q.n + 1)
                    add_x(dve, q, (po0, po1)[q.slot % 2])
                    norm_stats(dve, q, n)
            sweep(dve, 6, step)

        def add_x(dve, q, bank):
            nc.vector.tensor_tensor(res[q.slot][:, :, :], bank[:, 0:S].rearrange("p (t d) -> p t d", t=2),
                                    xg[:, bass.ds(2 * q.n, 2), :], ALU.add).then_inc(res_sb, 1)

        with ExitStack() as mem:
            mix = [sb(f"mix{i}", [P, 2, S], F32, mem) for i in range(2)]
            before = [sb(f"before{i}", [P, 2, S], F32, mem) for i in range(2)]
            rs = [sb(f"rs{i}", [P, 2, D], F32, mem) for i in range(SLOTS)]
            kr = [sb(f"kr{i}", [P, S], F32, mem) for i in range(2)]
            ka = [sb(f"ka{i}", [P, S], F32, mem) for i in range(2)]
            gv = [sb(f"gv{i}", [P, 2, D], F32, mem) for i in range(2)]
        before_sb, mix_sb, r_ps, k_ps = sem("before_sb"), sem("mix_sb"), sem("r_ps"), sem("k_ps")
        r_sb, kr_sb, ka_sb, vf_ps, gv_sb = sem("r_sb"), sem("kr_sb"), sem("ka_sb"), sem("vf_ps"), sem("gv_sb")

        def mixing_tensor(pe, a, g, layer):
            def step(at):
                if (q := at(0)):
                    wait(pe, xt_sb, g + q.n)
                    transpose_x(pe, q, g)
                at = behind(at, 1)
                if (q := at(1)):
                    s = q.slot % 2
                    pe.wait_ge(mix_sb, 2 * (a + q.n + 1))
                    wait(pe, r_sb, a + q.n)
                    for t in range(2):
                        last = pe.matmul(p1[:, t * P:t * P + P], mix[s][:, 0, t * P:t * P + P], mat(f"r{layer}"),
                                         start=True, stop=True)
                    last.then_inc(r_ps, 1)
                    wait(pe, kr_sb, a + q.n)
                    pe.matmul(pt0[:, 0:S], mat(f"m{layer}"), mix[s][:, 1, :], start=True, stop=True).then_inc(k_ps, 1)
                if (q := at(2)):
                    pe.wait_ge(ka_sb, a + q.n + 1)
                    wait(pe, gv_sb, a + q.n)
                    for t in range(2):
                        last = pe.matmul(pt1[:, t * P:t * P + P], ka[q.slot % 2][:, t * P:t * P + P],
                                         mat(f"w{layer}"), start=True, stop=True)
                    last.then_inc(vf_ps, 1)
            sweep(pe, 5, step)

        def mixing_scalar(act, a, g, layer):
            def step(at):
                if (q := at(0)):
                    copy_xt(act, q, g)
                    act.wait_ge(xt_sb, g + q.n + 1)
                    wait(act, mix_sb, 2 * (a + q.back(1)))
                    for c in range(2):
                        nc.scalar.mul(before[q.slot % 2][:, c, :], xt[q.slot][:, 0:S],
                                      omu[:, 2 * layer - 2 + c:2 * layer - 1 + c]).then_inc(before_sb, 1)
                at = behind(at, 1)
                if (q := at(1)):
                    act.wait_ge(r_ps, a + q.n + 1)
                    nc.scalar.activation(rs[q.slot][:, :, :], p1[:, 0:S].rearrange("p (t d) -> p t d", t=2),
                                         ACT.Sigmoid).then_inc(r_sb, 1)
                    act.wait_ge(k_ps, a + q.n + 1)
                    wait(act, ka_sb, a + q.back(1))
                    nc.scalar.activation(kr[q.slot % 2][:, :], pt0[:, 0:S], ACT.Relu).then_inc(kr_sb, 1)
            sweep(act, 5, step)

        def mixing_vector(dve, a, g, n, layer):
            def step(at):
                at = behind(at, 1)
                if (q := at(0)):
                    s = q.slot % 2
                    wait(dve, k_ps, a + q.back(1))
                    for c, mu in ((0, "mr"), (1, "mk")):
                        dve.wait_ge(before_sb, 2 * (a + q.n) + 1 + c)
                        nc.vector.scalar_tensor_tensor(mix[s][:, c, :], xt[q.slot][:, 1:1 + S],
                                                       col(f"{mu}{layer}"), before[s][:, c, :],
                                                       ALU.mult, ALU.add).then_inc(mix_sb, 1)
                if (q := at(3)):
                    norm_apply(dve, q, n)
                if (q := at(2)):
                    s = q.slot % 2
                    dve.wait_ge(vf_ps, a + q.n + 1)
                    nc.vector.tensor_tensor(gv[s][:, :, :], pt1[:, 0:S].rearrange("p (t d) -> p t d", t=2),
                                            rs[q.slot][:, :, :], ALU.mult).then_inc(gv_sb, 1)
                    dve.wait_ge(gv_sb, a + q.n + 1)
                    nc.vector.tensor_tensor(res[q.slot][:, :, :], gv[s][:, :, :], xg[:, bass.ds(2 * q.n, 2), :],
                                            ALU.add).then_inc(res_sb, 1)
                    norm_stats(dve, q, n)
            sweep(dve, 5, step)

        def mixing_pool(pool, a, n):
            def step(at):
                at = behind(at, 1)
                if (q := at(1)):
                    s = q.slot % 2
                    pool.wait_ge(kr_sb, a + q.n + 1)
                    wait(pool, vf_ps, a + q.back(1))
                    nc.gpsimd.tensor_tensor(ka[s][:, :], kr[s][:, :], kr[s][:, :], ALU.mult).then_inc(ka_sb, 1)
                if (q := at(2)):
                    norm_rstd(pool, q, n)
            sweep(pool, 5, step)

        def norm_pool(pool, n, lags, lag):
            def step(at):
                if (q := at(lag)):
                    norm_rstd(pool, q, n)
            sweep(pool, lags, step)

        with ExitStack() as mem:
            qt3 = [sb(f"qt3_{i}", [LD, S], F32, mem) for i in range(2)]
            vt3 = [sb(f"vt3_{i}", [LD, S], F32, mem) for i in range(2)]
            lowt = [sb(f"lowt{i}", [LD, S], F32, mem) for i in range(2)]
            low = [sb(f"low{i}", [P, S], F32, mem) for i in range(2)]
            elt = [sb(f"elt{i}", [LD, S], F32, mem) for i in range(2)]
            el = [sb(f"el{i}", [P, S], F32, mem) for i in range(2)]
            tok = [sb(f"tok{i}", [P, 2, 2, LD], F32, mem) for i in range(SLOTS)]
            am = [sb(f"am{i}", [P, 3, P], F32, mem) for i in range(2)]
            zq = [sb(f"zq{i}", [P, 2, LD], F32, mem) for i in range(2)]
            den = [sb(f"den{i}", [P, 2], F32, mem) for i in range(2)]
            den2 = [sb(f"den2_{i}", [P, 2], F32, mem) for i in range(2)]
            inv3 = [sb(f"inv3_{i}", [P, 2], F32, mem) for i in range(SLOTS)]
            o3 = [sb(f"o3_{i}", [P, 2, LD], F32, mem) for i in range(2)]
            ot3 = [sb(f"ot3_{i}", [P, P], F32, mem) for i in range(2)]
        t3_ps, tok_ps, low_sb, el_sb, qt3_sb, vt3_sb, tok_sb = (sem(s) for s in (
            "t3_ps", "tok_ps", "low_sb", "el_sb", "qt3_sb", "vt3_sb", "tok_sb"))
        a3_ps, z3_ps, am_sb, zq_sb, den_sb, den2_sb, inv3_sb = (sem(s) for s in (
            "a3_ps", "z3_ps", "am_sb", "zq_sb", "den_sb", "den2_sb", "inv3_sb"))
        o3_ps, o3_sb, ot3_ps, ot3_sb, y3_ps = (sem(s) for s in ("o3_ps", "o3_sb", "ot3_ps", "ot3_sb", "y3_ps"))

        def linear_tensor(pe, g, n):
            def step(at):
                if (q := at(0)):
                    wait(pe, xt_sb, g + q.n)
                    wait(pe, vt3_sb, q.back(1))
                    transpose_x(pe, q, g)
                ahead = at(0)
                at = behind(at, 1)
                if (q := at(2)):
                    s = q.slot % 2
                    pe.wait_ge(am_sb, 2 * (q.n + 1))
                    wait(pe, o3_sb, q.n)
                    k0, k1 = tok[q.slot][:, 0, 1, :], tok[q.slot][:, 1, 1, :]
                    pe.matmul(po0[:, 0:LD], am[s][:, 0, :], k0, start=True, stop=True)
                    pe.matmul(po0[:, LD:2 * LD], am[s][:, 1, :], k0, start=True, stop=False)
                    pe.matmul(po0[:, LD:2 * LD], am[s][:, 2, :], k1, start=False, stop=True).then_inc(o3_ps, 1)
                if (q := at(1)):
                    s = q.slot % 2
                    pe.wait_ge(qt3_sb, q.n + 1)
                    pe.wait_ge(vt3_sb, q.n + 1)
                    wait(pe, am_sb, 2 * q.n)
                    pe.matmul(pt1[:, 0:S], vt3[s][:, 0:P], qt3[s][:, :], start=True, stop=True)
                    pe.matmul(pt1[:, S:S + P], vt3[s][:, P:S], qt3[s][:, P:S], start=True, stop=True).then_inc(a3_ps, 1)
                    pe.wait_ge(tok_sb, q.n + 1)
                    wait(pe, zq_sb, q.n)
                    k0, k1 = tok[q.slot][:, 0, 1, :], tok[q.slot][:, 1, 1, :]
                    pe.matmul(pm0[:, 0:LD], upto[:, 0, :], k0, start=True, stop=True)
                    pe.matmul(pm0[:, LD:2 * LD], upto[:, 1, :], k0, start=True, stop=False)
                    pe.matmul(pm0[:, LD:2 * LD], upto[:, 0, :], k1, start=False, stop=True).then_inc(z3_ps, 1)
                if (q := at(2)):
                    pe.wait_ge(o3_sb, q.n + 1)
                    wait(pe, ot3_sb, q.n)
                    wait(pe, res_sb, n + q.n)
                    pe.transpose(po1[:, 0:P], o3[q.slot % 2][:, :, :].rearrange("p t d -> p (t d)"),
                                 ident[:, :]).then_inc(ot3_ps, 1)
                if (q := at(0)):
                    xq = xt[q.slot][:, 1:1 + S]
                    pe.wait_ge(xt_sb, g + q.n + 1)
                    wait(pe, qt3_sb, q.n)
                    pe.matmul(p1[0:LD, 0:S], wl[:, 0, :], xq, start=True, stop=True)
                    if ahead:
                        pe.wait_ge(xt_sb, g + ahead.n + 1)
                    pe.matmul(p0[0:LD, S:2 * S], wl[:, 2, :], xq, start=True, stop=True).then_inc(t3_ps, 1)
                    wait(pe, tok_sb, q.n)
                    for t in range(2):
                        last = pe.matmul(pt0[:, t * P:t * P + P], xq[:, t * P:t * P + P],
                                         wl[:, 0:2, :].rearrange("p a b -> p (a b)"), start=True, stop=True)
                    last.then_inc(tok_ps, 1)
                if (q := at(2)):
                    pe.wait_ge(ot3_sb, q.n + 1)
                    wait(pe, res_sb, n + q.n)
                    for t in range(2):
                        last = pe.matmul((pm1, po1)[t][:, t * P:t * P + P], ot3[q.slot % 2][t * LD:t * LD + LD, :],
                                         wo[t * LD:t * LD + LD, :],
                                         start=True, stop=True)
                    last.then_inc(y3_ps, 1)
            sweep(pe, 5, step)

        def linear_scalar(act, g):
            def step(at):
                if (q := at(0)):
                    copy_xt(act, q, g)
                at = behind(at, 1)
                if (q := at(2)):
                    act.wait_ge(ot3_ps, q.n + 1)
                    wait(act, y3_ps, q.back(1))
                    nc.scalar.copy(ot3[q.slot % 2][:, :], po1[:, 0:P]).then_inc(ot3_sb, 1)
                if (q := at(0)):
                    s = q.slot % 2
                    act.wait_ge(t3_ps, q.n + 1)
                    wait(act, a3_ps, q.back(1))
                    nc.scalar.copy(vt3[s][:, :], p0[0:LD, S:2 * S]).then_inc(vt3_sb, 1)
                    act.wait_ge(low_sb, 2 * q.n + 1)
                    wait(act, tok_sb, q.back(1))
                    nc.scalar.activation(elt[s][:, :], lowt[s][:, :], ACT.Exp).then_inc(el_sb, 1)
                    act.wait_ge(low_sb, 2 * q.n + 2)
                    nc.scalar.activation(el[s][:, :], low[s][:, :], ACT.Exp).then_inc(el_sb, 1)
            sweep(act, 5, step)

        def linear_vector(dve, n):
            def step(at):
                at = behind(at, 1)
                if (q := at(2)):
                    s = q.slot % 2
                    dve.wait_ge(o3_ps, q.n + 1)
                    nc.vector.tensor_tensor(o3[s][:, :, :], po0[:, 0:2 * LD].rearrange("p (t d) -> p t d", t=2),
                                            inv3[q.slot][:, :].unsqueeze(2).to_broadcast([P, 2, LD]),
                                            ALU.mult).then_inc(o3_sb, 1)
                if (q := at(1)):
                    s = q.slot % 2
                    dve.wait_ge(a3_ps, q.n + 1)
                    nc.vector.tensor_tensor(am[s][:, 0:2, :], pt1[:, 0:S].rearrange("p (a b) -> p a b", a=2),
                                            upto[:, :, :], ALU.mult).then_inc(am_sb, 1)
                    nc.vector.tensor_tensor(am[s][:, 2, :], pt1[:, S:S + P], upto[:, 0, :], ALU.mult).then_inc(am_sb, 1)
                    dve.wait_ge(z3_ps, q.n + 1)
                    nc.vector.tensor_tensor(zq[s][:, :, :], pm0[:, 0:2 * LD].rearrange("p (t d) -> p t d", t=2),
                                            tok[q.slot][:, :, 0, :], ALU.mult).then_inc(zq_sb, 1)
                    dve.wait_ge(zq_sb, q.n + 1)
                    nc.vector.tensor_reduce(den[s][:, :], zq[s][:, :, :], AX.X, ALU.add).then_inc(den_sb, 1)
                    dve.wait_ge(den_sb, q.n + 1)
                    nc.vector.tensor_scalar(den2[s][:, :], den[s][:, :], 1e-6, None, ALU.max).then_inc(den2_sb, 1)
                    dve.wait_ge(den2_sb, q.n + 1)
                    nc.vector.reciprocal(inv3[q.slot][:, :], den2[s][:, :]).then_inc(inv3_sb, 1)
                    dve.wait_ge(inv3_sb, q.n + 1)
                if (q := at(0)):
                    s = q.slot % 2
                    dve.wait_ge(t3_ps, q.n + 1)
                    wait(dve, el_sb, 2 * (q.back(1)))
                    nc.vector.tensor_scalar(lowt[s][:, :], p1[0:LD, 0:S], 0.0, None, ALU.min).then_inc(low_sb, 1)
                    dve.wait_ge(tok_ps, q.n + 1)
                    nc.vector.tensor_scalar(low[s][:, :], pt0[:, 0:S], 0.0, None, ALU.min).then_inc(low_sb, 1)
                    dve.wait_ge(el_sb, 2 * q.n + 1)
                    nc.vector.scalar_tensor_tensor(qt3[s][:, :], p1[0:LD, 0:S], 0.0, elt[s][:, :], ALU.max,
                                                   ALU.add).then_inc(qt3_sb, 1)
                    dve.wait_ge(el_sb, 2 * q.n + 2)
                    nc.vector.scalar_tensor_tensor(tok[q.slot][:, :, :, :].rearrange("p a b c -> p (a b c)"),
                                                   pt0[:, 0:S], 0.0, el[s][:, :], ALU.max, ALU.add).then_inc(tok_sb, 1)
                if (q := at(3)):
                    norm_apply(dve, q, n)
                if (q := at(2)):
                    dve.wait_ge(y3_ps, q.n + 1)
                    for t, bank in ((0, pm1), (1, po1)):
                        last = nc.vector.tensor_tensor(res[q.slot][:, t:t + 1, :],
                                                       bank[:, t * P:t * P + P].unsqueeze(1),
                                                       xg[:, bass.ds(2 * q.n + t, 1), :], ALU.add)
                    last.then_inc(res_sb, 1)
                    norm_stats(dve, q, n)
            sweep(dve, 5, step)

        def load_x_routed(sp, g, n, before, each):
            def step(at):
                if (q := at(0)):
                    wait_apart(sp, scattered[q.slot], before // SLOTS + each * q.turn, passed)
                    load_x(sp, q, g, n)
            sweep(sp, 3, step)

        def load_x_only(sp, lags, g, n):
            def step(at):
                if (q := at(0)):
                    load_x(sp, q, g, n)
            sweep(sp, lags, step)

        lg = [sb(f"lg{i}", [P, 2, EM]) for i in range(2)]
        top = [sb(f"top{i}", [P, 2, 8]) for i in range(2)]
        topi = [sb(f"topi{i}", [P, 2, 8], U32) for i in range(2)]
        topf = [sb(f"topf{i}", [P, 2, 8]) for i in range(2)]
        oh = [sb(f"oh{i}", [P, 2, 2, EM]) for i in range(2)]
        sel = [sb(f"sel{i}", [P, 2, EM], BF16) for i in range(SLOTS)]
        seen = [sb(f"seen{i}", [P, EM], BF16) for i in range(SLOTS)]
        rank = [sb(f"rank{i}", [P, 2, EM]) for i in range(2)]
        pick = [sb(f"pick{i}", [P, 2, 2, EM]) for i in range(2)]
        pl = [sb(f"pl{i}", [P, 4, 2]) for i in range(2)]
        gap = [sb(f"gap{i}", [P, 2, EM]) for i in range(2)]
        eg = [sb(f"eg{i}", [P, 2, EM]) for i in range(2)]
        place = [sb(f"place{i}", [P, 2, 2], U32) for i in range(SLOTS)]
        places = sb("places", [P, TILES, 2], U32)
        weight = sb("weight", [P, TILES, 2])
        xs0 = nc.dram_tensor("sorted0", (E0 * ROOM0 + 8 * S, D), F32).ap()
        ys0 = nc.dram_tensor("result0", (NG * S, D), F32).ap()
        xs3 = nc.dram_tensor("sorted3", (E3 * CAP3 + SEQS * S, D), F32).ap()
        ys3 = nc.dram_tensor("result3", (E3 * CAP3, D), F32).ap()
        DUMP = E3 * CAP3

        lg_ps, lg_sb, seen_sb, top_sb, topi_sb, topf_sb = (sem(s) for s in (
            "lg_ps", "lg_sb", "seen_sb", "top_sb", "topi_sb", "topf_sb"))
        oh_sb, sel_sb, rank_ps, rank_sb, pick_sb, pl_sb = (sem(s) for s in (
            "oh_sb", "sel_sb", "rank_ps", "rank_sb", "pick_sb", "pl_sb"))
        gap_sb, eg_sb, wt_sb, place_sb, zeroed = (sem(s) for s in (
            "gap_sb", "eg_sb", "wt_sb", "place_sb", "zeroed"))
        scattered = [sem(f"scattered{i}") for i in range(SLOTS)]

        def route_tensor(pe, a, g, E, rw):
            def step(at):
                if (q := at(0)):
                    wait(pe, xt_sb, g + q.n)
                    transpose_x(pe, q, g)
                if (q := at(1)):
                    pe.wait_ge(sel_sb, a + q.n + 1)
                    pe.wait_ge(seen_sb, a // SEQS + a + q.n + 1)
                    wait(pe, rank_sb, a + q.n)
                    s = sel[q.slot]
                    pe.matmul(pt0[:, 0:E], upto16[:, :], s[:, 0, 0:E], start=True, stop=False)
                    pe.matmul(pt0[:, 0:E], ones16[:, :], seen[q.slot][:, 0:E], start=False, stop=True)
                    pe.matmul(pt0[:, E:2 * E], upto16[:, :], s[:, 1, 0:E], start=True, stop=False)
                    pe.matmul(pt0[:, E:2 * E], ones16[:, :], s[:, 0, 0:E], start=False, stop=False)
                    pe.matmul(pt0[:, E:2 * E], ones16[:, :], seen[q.slot][:, 0:E], start=False,
                              stop=True).then_inc(rank_ps, 1)
                if (q := at(0)):
                    pe.wait_ge(xt_sb, g + q.n + 1)
                    wait(pe, lg_sb, a + q.n)
                    for t in range(2):
                        last = pe.matmul(p1[:, t * E:t * E + E], xt[q.slot][:, 1 + t * P:1 + t * P + P], rw[:, :],
                                         start=True, stop=True)
                    last.then_inc(lg_ps, 1)
            sweep(pe, 3, step)

        def route_scalar(act, a, g, E):
            def step(at):
                if (q := at(0)):
                    copy_xt(act, q, g)
                if (q := at(1)):
                    s = q.slot % 2
                    act.wait_ge(gap_sb, 2 * (a + q.n + 1))
                    nc.scalar.activation(eg[s][:, :, 0:E], gap[s][:, :, 0:E], ACT.Exp).then_inc(eg_sb, 1)
            sweep(act, 3, step)

        def route_vector(dve, a, E, choices, base):
            nc.vector.memset(seen[0][:, :], 0.0).then_inc(seen_sb, 1)

            def step(at):
                if (q := at(0)):
                    s, k = q.slot % 2, a + q.n
                    dve.wait_ge(lg_ps, k + 1)
                    nc.vector.tensor_copy(lg[s][:, :, 0:E], p1[:, 0:2 * E].rearrange("p (t e) -> p t e", t=2)
                                          ).then_inc(lg_sb, 1)
                    wait_apart(dve, lg_sb, k + 1, passed)
                    for t in range(2):
                        nc.vector.max(top[s][:, t, :], lg[s][:, t, 0:E]).then_inc(top_sb, 1)
                    for t in range(2):
                        wait_apart(dve, top_sb, 2 * k + 1 + t, passed)
                        nc.vector.max_index(topi[s][:, t, :], top[s][:, t, :], lg[s][:, t, 0:E]).then_inc(topi_sb, 1)
                    dve.wait_ge(topi_sb, 2 * (k + 1))
                    nc.vector.tensor_copy(topf[s][:, :, :], topi[s][:, :, :]).then_inc(topf_sb, 1)
                    dve.wait_ge(topf_sb, k + 1)
                    for i in range(2):
                        for t in range(2):
                            nc.vector.tensor_scalar(oh[s][:, i, t, 0:E], iota_e[:, 0:E], topf[s][:, t, i:i + 1],
                                                    None, ALU.is_equal).then_inc(oh_sb, 1)
                    dve.wait_ge(oh_sb, 4 * (k + 1))
                    if choices == 2:
                        nc.vector.tensor_tensor(sel[q.slot][:, :, 0:E], oh[s][:, 0, :, 0:E], oh[s][:, 1, :, 0:E],
                                                ALU.add).then_inc(sel_sb, 1)
                    else:
                        nc.vector.tensor_copy(sel[q.slot][:, :, 0:E], oh[s][:, 0, :, 0:E]).then_inc(sel_sb, 1)
                    wait(dve, eg_sb, k - 1)
                    for t in range(2):
                        nc.vector.tensor_scalar(gap[s][:, t, 0:E], lg[s][:, t, 0:E], top[s][:, t, 0:1], None,
                                                ALU.subtract).then_inc(gap_sb, 1)
                    dve.wait_ge(gap_sb, 2 * (k + 1))
                if (q := at(1)):
                    s, k = q.slot % 2, a + q.n
                    sd = a // SEQS + k
                    nxt = (q.slot + 1) % SLOTS
                    dve.wait_ge(seen_sb, sd + 1)
                    nc.vector.tensor_tensor(rank[s][:, 0, 0:E], seen[q.slot][:, 0:E], sel[q.slot][:, 0, 0:E],
                                            ALU.add).then_inc(sel2_sb, 1)
                    dve.wait_ge(sel2_sb, k + 1)
                    nc.vector.tensor_tensor(seen[nxt][:, 0:E], rank[s][:, 0, 0:E], sel[q.slot][:, 1, 0:E],
                                            ALU.add).then_inc(seen_sb, 1)
                    dve.wait_ge(seen_sb, sd + 2)
                    dve.wait_ge(rank_ps, k + 1)
                    r = pt0[:, 0:2 * E].rearrange("p (t e) -> p t e", t=2)
                    if choices == 2:
                        nc.vector.tensor_tensor(rank[s][:, :, 0:E], r, base[:, :, :], ALU.add).then_inc(rank_sb, 1)
                        dve.wait_ge(rank_sb, k + 1)
                        for i in range(2):
                            nc.vector.tensor_tensor(pick[s][:, i, :, 0:E], oh[s][:, i, :, 0:E], rank[s][:, :, 0:E],
                                                    ALU.mult).then_inc(pick_sb, 1)
                        dve.wait_ge(pick_sb, 2 * (k + 1))
                        nc.vector.tensor_reduce(pl[s][:, 0:2, :].rearrange("p a b -> p (a b)"),
                                                pick[s][:, :, :, 0:E], AX.X, ALU.add).then_inc(pl_sb, 1)
                        dve.wait_ge(pl_sb, k + 1)
                        wait(dve, scattered[q.slot], 64 * q.turn)
                        nc.vector.tensor_copy(place[q.slot][:, :, :], pl[s][:, 0:2, :]).then_inc(place_sb, 1)
                        nc.vector.tensor_copy(places[:, bass.ds(2 * q.n, 2), :].rearrange("p t c -> p c t"),
                                              pl[s][:, 0:2, :]).then_inc(places_sb, 1)
                        dve.wait_ge(eg_sb, k + 1)
                        e2 = sm[s][:, 0, :]
                        nc.vector.tensor_tensor(gs[s][:, :, 0:E], eg[s][:, :, 0:E], oh[s][:, 1, :, 0:E],
                                                ALU.mult).then_inc(wt_sb, 1)
                        dve.wait_ge(wt_sb, 5 * q.n + 1)
                        nc.vector.tensor_reduce(e2, gs[s][:, :, 0:E], AX.X, ALU.add).then_inc(wt_sb, 1)
                        dve.wait_ge(wt_sb, 5 * q.n + 2)
                        nc.vector.tensor_scalar(sm[s][:, 1, :], e2, 1.0, None, ALU.add).then_inc(wt_sb, 1)
                        dve.wait_ge(wt_sb, 5 * q.n + 3)
                        nc.vector.reciprocal(weight[:, bass.ds(2 * q.n, 2), 0:1],
                                             sm[s][:, 1, :].unsqueeze(2)).then_inc(wt_sb, 1)
                        dve.wait_ge(wt_sb, 5 * q.n + 4)
                        nc.vector.tensor_tensor(weight[:, bass.ds(2 * q.n, 2), 1:2], e2.unsqueeze(2),
                                                weight[:, bass.ds(2 * q.n, 2), 0:1], ALU.mult).then_inc(wt_sb, 1)
                    else:
                        w0 = 5 * SEQS + 7 * q.n
                        nc.vector.tensor_tensor(pick[s][:, 0, :, 0:E], oh[s][:, 0, :, 0:E], r,
                                                ALU.mult).then_inc(rank_sb, 1)
                        nc.vector.tensor_tensor(pick[s][:, 1, :, 0:E], oh[s][:, 0, :, 0:E], base[:, :, :],
                                                ALU.mult).then_inc(pick_sb, 1)
                        dve.wait_ge(rank_sb, k + 1)
                        dve.wait_ge(pick_sb, 2 * SEQS + q.n + 1)
                        nc.vector.tensor_reduce(pl[s][:, 0:2, :].rearrange("p a b -> p (a b)"),
                                                pick[s][:, :, :, 0:E], AX.X, ALU.add).then_inc(pl_sb, 1)
                        dve.wait_ge(pl_sb, k + 1)
                        keep, lost = sm[s][:, 0, :], sm[s][:, 1, :]
                        nc.vector.tensor_scalar(keep, pl[s][:, 0, :], float(CAP3), None, ALU.is_le).then_inc(wt_sb, 1)
                        nc.vector.scalar_tensor_tensor(pl[s][:, 2, :], pl[s][:, 0, :], float(CAP3), pl[s][:, 1, :],
                                                       ALU.min, ALU.add).then_inc(wt_sb, 1)
                        dve.wait_ge(wt_sb, w0 + 2)
                        nc.vector.tensor_copy(places[:, bass.ds(2 * q.n, 2), 0:1],
                                              pl[s][:, 2, :].unsqueeze(2)).then_inc(places_sb, 1)
                        nc.vector.tensor_tensor(lost, pl[s][:, 2, :], dump[:, bass.ds(2 * q.n, 2)],
                                                ALU.subtract).then_inc(wt_sb, 1)
                        dve.wait_ge(wt_sb, w0 + 3)
                        nc.vector.tensor_tensor(pl[s][:, 3, :], lost, keep, ALU.mult).then_inc(wt_sb, 1)
                        dve.wait_ge(wt_sb, w0 + 4)
                        dve.wait_ge(scattered[q.slot], 64 * (SEQS // SLOTS) + 32 * q.turn)
                        nc.vector.tensor_tensor(place[q.slot][:, 0, :], pl[s][:, 3, :], dump[:, bass.ds(2 * q.n, 2)],
                                                ALU.add).then_inc(place_sb, 1)
                        dve.wait_ge(eg_sb, k + 1)
                        nc.vector.tensor_reduce(sm[s][:, 2, :], eg[s][:, :, 0:E], AX.X, ALU.add).then_inc(wt_sb, 1)
                        dve.wait_ge(wt_sb, w0 + 5)
                        nc.vector.reciprocal(sm[s][:, 3, :], sm[s][:, 2, :]).then_inc(wt_sb, 1)
                        dve.wait_ge(wt_sb, w0 + 6)
                        nc.vector.tensor_tensor(weight[:, bass.ds(2 * q.n, 2), 0:1], sm[s][:, 3, :].unsqueeze(2),
                                                keep.unsqueeze(2), ALU.mult).then_inc(wt_sb, 1)
            sweep(dve, 3, step)

        sm = [sb(f"sm{i}", [P, 4, 2]) for i in range(2)]
        gs = [sb(f"gs{i}", [P, 2, EM]) for i in range(2)]
        sel2_sb, places_sb = sem("sel2_sb"), sem("places_sb")

        def route_pool(pool, a, choices, rows):
            def step(at):
                if (q := at(2)):
                    wait_apart(pool, place_sb, a + q.n + 1, passed)
                    for i in range(choices):
                        for t in range(2):
                            pool.indirect_dma_start(
                                out=rows, out_offset=bass.IndirectOffsetOnAxis(ap=place[q.slot][:, i, t:t + 1], axis=0),
                                in_=xs[q.slot][:, t, :], in_offset=None).then_inc(scattered[q.slot], 16)
            sweep(pool, 3, step)

        count_f = sb("count_f", [P, E0])
        count_i = sb("count_i", [P, E0], I32)
        up_i = sb("up_i", [P, E0], I32)
        grp_i = sb("grp_i", [P, E0], I32)
        grp = sb("grp", [P, E0])
        cum = sb("cum", [P, E0])
        past = sb("past", [P, NG, E0])
        spent = sb("spent", [P, NG, E0])
        g_e = sb("g_e", [P, NG])
        g_b = sb("g_b", [P, NG])
        g_j = sb("g_j", [P, NG])
        g_o = sb("g_o", [P, NG])
        g_exp = sb("g_exp", [P, NG], I32)
        g_off = sb("g_off", [P, NG], I32)
        delta = sb("delta", [P, E0])
        ends = sb("ends", [P, E0])
        place_f = sb("place_f", [P, 2 * TILES])
        shift = sb("shift", [P, 2 * TILES, E0])
        moved = sb("moved", [P, 2 * TILES])
        count_ps, list_sb = sem("count_ps"), sem("list_sb")
        tails = sem("tails")
        LIST = 16

        def list_tensor(pe):
            pe.wait_ge(seen_sb, SEQS + 1)
            pe.wait_ge(lg_sb, SEQS)
            pe.matmul(p1[:, 0:E0], ones16[:, :], seen[0][:, 0:E0], start=True, stop=True).then_inc(count_ps, 1)

        def list_vector(dve):
            done = [0]

            def chain(ins):
                done[0] += 1
                ins.then_inc(list_sb, 1)
                dve.wait_ge(list_sb, done[0])

            v = nc.vector
            dve.wait_ge(count_ps, 1)
            chain(v.tensor_copy(count_i[:, :], p1[:, 0:E0]))
            chain(v.tensor_scalar(count_f[:, :], p1[:, 0:E0], float(S - 1), None, ALU.add))
            chain(v.tensor_copy(up_i[:, :], count_f[:, :]))
            chain(v.tensor_scalar(grp_i[:, :], up_i[:, :], S.bit_length() - 1, None, ALU.logical_shift_right))
            chain(v.tensor_copy(grp[:, :], grp_i[:, :]))
            chain(v.tensor_tensor_scan(cum[:, :], ones[:, 0:E0], grp[:, :], 0.0, ALU.mult, ALU.add))
            chain(v.tensor_tensor(past[:, :, :], cum[:, :].unsqueeze(1).to_broadcast([P, NG, E0]),
                                  iota_g[:, :].unsqueeze(2).to_broadcast([P, NG, E0]), ALU.is_le))
            chain(v.tensor_reduce(g_e[:, :], past[:, :, :], AX.X, ALU.add))
            chain(v.tensor_tensor(spent[:, :, :], past[:, :, :], grp[:, :].unsqueeze(1).to_broadcast([P, NG, E0]),
                                  ALU.mult))
            chain(v.tensor_reduce(g_b[:, :], spent[:, :, :], AX.X, ALU.add))
            chain(v.tensor_tensor(g_j[:, :], iota_g[:, :], g_b[:, :], ALU.subtract))
            chain(v.tensor_scalar(g_o[:, :], g_j[:, :], float(S), None, ALU.mult))
            chain(v.scalar_tensor_tensor(g_b[:, :], g_e[:, :], float(ROOM0), g_o[:, :], ALU.mult, ALU.add))
            chain(v.tensor_copy(g_off[:, :], g_b[:, :]))
            chain(v.tensor_scalar(g_j[:, :], g_e[:, :], float(E0 - 1), None, ALU.min))
            chain(v.tensor_copy(g_exp[:, :], g_j[:, :]))
            assert done[0] == LIST
            chain(v.tensor_scalar(delta[:, :], grp[:, :], float(S), -float(ROOM0), ALU.mult, ALU.add))
            chain(v.tensor_scalar(ends[:, :], iota_e[:, 0:E0], float(ROOM0), float(ROOM0), ALU.mult, ALU.add))
            flat = places[:, :, :].rearrange("p t c -> p (t c)")
            wide = [P, 2 * TILES, E0]
            chain(v.tensor_copy(place_f[:, :], flat))
            chain(v.tensor_tensor(shift[:, :, :], ends[:, :].unsqueeze(1).to_broadcast(wide),
                                  place_f[:, :].unsqueeze(2).to_broadcast(wide), ALU.is_le))
            chain(v.tensor_tensor(shift[:, :, :], shift[:, :, :], delta[:, :].unsqueeze(1).to_broadcast(wide), ALU.mult))
            chain(v.tensor_reduce(moved[:, :], shift[:, :, :], AX.X, ALU.add))
            chain(v.tensor_tensor(flat, place_f[:, :], moved[:, :], ALU.add))

        def list_sync(sp):
            sp.wait_ge(list_sb, LIST)
            for s in scattered:
                sp.wait_ge(s, 64 * SEQS // SLOTS)
            for e in range(E0):
                c = sp.value_load(count_i[0:1, e:e + 1], min_val=0, max_val=CAP0)
                sp.dma_start(xs0[bass.ds(c + e * ROOM0, S), :].rearrange("(p r) d -> p (r d)", p=P),
                             zt[:, 0:2 * D]).then_inc(tails, 16)

        W2_AT, B1_AT, B2_AT = F, F + FC * D, F + FC * D + FC
        we = [sb(f"we{i}", [P, B2_AT + 1]) for i in range(SLOTS)]
        xe = [sb(f"xe{i}", [P, 4, D]) for i in range(SLOTS)]
        xet = [sb(f"xet{i}", [P, CAP3]) for i in range(2)]
        he = [sb(f"he{i}", [P, FC, CAP3]) for i in range(2)]
        yt = [sb(f"yt{i}", [P, CAP3]) for i in range(2)]
        ye = [sb(f"ye{i}", [P, 4, D]) for i in range(SLOTS)]
        xet_ps, xet_sb, he_ps, he_sb, yt_ps, yt_sb, ye_ps, ye_sb = (sem(s) for s in (
            "xet_ps", "xet_sb", "he_ps", "he_sb", "yt_ps", "yt_sb", "ye_ps", "ye_sb"))
        grp_in = [sem(f"grp_in{i}") for i in range(SLOTS)]
        grp_out = [sem(f"grp_out{i}") for i in range(SLOTS)]
        IN = 16 * 2

        def pieces(T):
            k = next(k for k in range(1, T) if T % k == 0 and T // k <= P)
            return k, T // k

        def experts_sync(sp, a, first):
            if first:
                sp.wait_ge(tails, 16 * E0)
            else:
                for s in scattered:
                    sp.wait_ge(s, (64 + 32) * SEQS // SLOTS)
            sp.wait_ge(zeroed, 32)
            T = S if first else CAP3
            k, m = pieces(T)
            rows_in, rows_out = (xs0, ys0) if first else (xs3, ys3)
            packed, width = (pack0, B2_AT + 1) if first else (pack3, B1_AT)

            def step(at):
                if (q := at(0)):
                    if first:
                        e = sp.value_load(g_exp[0:1, bass.ds(q.n, 1)], min_val=0, max_val=E0 - 1)
                        r = sp.value_load(g_off[0:1, bass.ds(q.n, 1)], min_val=0, max_val=E0 * ROOM0 + 7 * S)
                    else:
                        e, r = q.n, q.n * CAP3
                    wait_apart(sp, yt_sb, a + q.back(3), passed)
                    sp.dma_start(xe[q.slot][0:m, 0:k, :], rows_in[bass.ds(r, T), :].rearrange("(p t) d -> p t d", t=k)
                                 ).then_inc(grp_in[q.slot], 16)
                    sp.dma_start(we[q.slot][:, 0:width], packed[bass.ds(e, 1)].rearrange("e p w -> p (e w)")
                                 ).then_inc(grp_in[q.slot], 16)
                if (q := at(5)):
                    wait_apart(sp, ye_sb, a + q.n + 1, passed)
                    sp.dma_start(rows_out[bass.ds(q.n * T, T), :].rearrange("(p t) d -> p t d", t=k),
                                 ye[q.slot][0:m, 0:k, :]).then_inc(grp_out[q.slot], 16)
            sweep(sp, 6, step, NG if first else E3)

        def experts_tensor(pe, a, T, n):
            hb = [pt0, pt1, pm0, pm1]
            k, m = pieces(T)

            def step(at):
                if (q := at(0)):
                    wait(pe, xet_sb, a + q.n)
                    pe.wait_ge(grp_in[q.slot], IN * (a // SLOTS + q.turn + 1))
                    for i in range(k):
                        last = pe.transpose(p0[:, i * m:i * m + m], xe[q.slot][0:m, i, :], ident[0:m, 0:m])
                    last.then_inc(xet_ps, 1)
                if (q := at(1)):
                    pe.wait_ge(xet_sb, a + q.n + 1)
                    for c in range(FC):
                        wait(pe, he_sb, 4 * (a + q.back(1)) + c + 1)
                        pe.matmul(hb[c][:, 0:T], we[q.slot][:, c * P:c * P + P], xet[q.slot % 2][:, 0:T],
                                  start=True, stop=True).then_inc(he_ps, 1)
                if (q := at(2)):
                    wait(pe, yt_sb, a + q.n)
                    pe.wait_ge(he_sb, 4 * (a + q.n + 1))
                    for c in range(FC):
                        last = pe.matmul(po0[:, 0:T], we[q.slot][:, W2_AT + c * D:W2_AT + c * D + D],
                                         he[q.slot % 2][:, c, 0:T], start=(c == 0), stop=(c == FC - 1))
                    last.then_inc(yt_ps, 1)
                if (q := at(3)):
                    pe.wait_ge(yt_sb, a + q.n + 1)
                    wait(pe, ye_sb, a + q.n)
                    for i in range(k):
                        last = pe.transpose(po1[0:m, i * D:i * D + D], yt[q.slot % 2][:, i * m:i * m + m], ident[:, :])
                    last.then_inc(ye_ps, 1)
            sweep(pe, 4, step, n)

        def experts_scalar(act, a, T, n, biased):
            hb = [pt0, pt1, pm0, pm1]

            def step(at):
                if (q := at(1)):
                    wait(act, yt_ps, a + q.back(1))
                    for c in range(FC):
                        act.wait_ge(he_ps, 4 * (a + q.n) + c + 1)
                        nc.scalar.activation(he[q.slot % 2][:, c, 0:T], hb[c][:, 0:T], ACT.Gelu_apprx_tanh,
                                             bias=we[q.slot][:, B1_AT + c:B1_AT + c + 1] if biased else zero_col[:, :]
                                             ).then_inc(he_sb, 1)
            sweep(act, 4, step, n)

        def experts_vector(dve, a, T, n, biased):
            k, m = pieces(T)

            def step(at):
                if (q := at(0)):
                    dve.wait_ge(xet_ps, a + q.n + 1)
                    wait(dve, he_ps, 4 * (a + q.back(1)))
                    nc.vector.tensor_copy(xet[q.slot % 2][:, 0:T], p0[:, 0:T]).then_inc(xet_sb, 1)
                if (q := at(2)):
                    dve.wait_ge(yt_ps, a + q.n + 1)
                    wait(dve, ye_ps, a + q.back(1))
                    if biased:
                        nc.vector.tensor_scalar(yt[q.slot % 2][:, 0:T], po0[:, 0:T], we[q.slot][:, B2_AT:B2_AT + 1],
                                                None, ALU.add).then_inc(yt_sb, 1)
                    else:
                        nc.vector.tensor_copy(yt[q.slot % 2][:, 0:T], po0[:, 0:T]).then_inc(yt_sb, 1)
                if (q := at(3)):
                    dve.wait_ge(ye_ps, a + q.n + 1)
                    wait(dve, grp_out[q.slot], 16 * (a // SLOTS + q.turn))
                    nc.vector.tensor_copy(ye[q.slot][0:m, 0:k, :],
                                          po1[0:m, 0:k * D].rearrange("p (t d) -> p t d", t=k)).then_inc(ye_sb, 1)
            sweep(dve, 4, step, n)

        at_row = [sb(f"at_row{i}", [P, 2, 2], U32) for i in range(SLOTS)]
        wrow = [sb(f"wrow{i}", [P, 2, 2]) for i in range(SLOTS)]
        yr = [sb(f"yr{i}", [P, 2, 2, D]) for i in range(SLOTS)]
        part = [sb(f"part{i}", [P, 2, D]) for i in range(2)]
        row_at, wrow_sb, part_sb = (sem(s) for s in ("row_at", "wrow_sb", "part_sb"))
        gathered = [sem(f"gathered{i}") for i in range(SLOTS)]

        def gather_pool(pool, a, n, choices, rows, outs_done, got):
            for s in grp_out:
                pool.wait_ge(s, outs_done // SLOTS)

            def step(at):
                if (q := at(3)):
                    norm_rstd(pool, q, n)
                if (q := at(1)):
                    pool.wait_ge(row_at, a + q.n + 1)
                    wait_apart(pool, res_sb, n + q.back(3), passed)
                    for t in range(2):
                        for i in range(choices):
                            pool.indirect_dma_start(
                                out=yr[q.slot][:, t, i, :], out_offset=None, in_=rows,
                                in_offset=bass.IndirectOffsetOnAxis(ap=at_row[q.slot][:, t, i:i + 1], axis=0)
                            ).then_inc(gathered[q.slot], 16)
            sweep(pool, 5, step)

        def gather_vector(dve, a, n, choices, got):
            def step(at):
                if (q := at(4)):
                    norm_apply(dve, q, n)
                if (q := at(0)):
                    wait(dve, gathered[q.slot], got // SLOTS + 32 * choices * q.turn)
                    nc.vector.tensor_copy(at_row[q.slot][:, :, 0:choices],
                                          places[:, bass.ds(2 * q.n, 2), 0:choices]).then_inc(row_at, 1)
                    nc.vector.tensor_copy(wrow[q.slot][:, :, 0:choices],
                                          weight[:, bass.ds(2 * q.n, 2), 0:choices]).then_inc(wrow_sb, 1)
                if (q := at(2)):
                    dve.wait_ge(wrow_sb, a + q.n + 1)
                    dve.wait_ge(gathered[q.slot], got // SLOTS + 32 * choices * (q.turn + 1))
                    src = xg[:, bass.ds(2 * q.n, 2), :]
                    if choices == 2:
                        for t in range(2):
                            nc.vector.scalar_tensor_tensor(part[q.slot % 2][:, t:t + 1, :], yr[q.slot][:, t, 0:1, :],
                                                           wrow[q.slot][:, t, 0:1], src[:, t:t + 1, :],
                                                           ALU.mult, ALU.add).then_inc(part_sb, 1)
                        dve.wait_ge(part_sb, 2 * (q.n + 1))
                        src = part[q.slot % 2][:, :, :]
                    for t in range(2):
                        last = nc.vector.scalar_tensor_tensor(res[q.slot][:, t:t + 1, :],
                                                              yr[q.slot][:, t, choices - 1:choices, :],
                                                              wrow[q.slot][:, t, choices - 1:choices],
                                                              src[:, t:t + 1, :], ALU.mult, ALU.add)
                    last.then_inc(res_sb, 1)
                    norm_stats(dve, q, n)
            sweep(dve, 5, step)

        def store_out(sp, n):
            def step(at):
                if (q := at(4)):
                    sp.wait_ge(ln_x, 2 * (n + q.n + 1))
                    sp.dma_start(out[bass.ds(2 * q.n, 2)].rearrange("t p d -> p t d"),
                                 xg[:, bass.ds(2 * q.n, 2), :]).then_inc(out_done, 16)
            sweep(sp, 5, step)
            sp.wait_ge(out_done, 16 * SEQS)

        N = SEQS
        CONSTS_V = 4 * SLOTS + 1
        block = ctx.enter_context(nc.Block())

        @block.sync
        def _(sp):
            sp.dma_start(xg[:, :, :], x.rearrange("t p d -> p t d")).then_inc(x_in, 16)
            sp.dma_start(wm[:, :, :], mats.rearrange("p (m d) -> p m d", d=D)).then_inc(w_in, 16)
            sp.dma_start(cv[:, :], cols).then_inc(w_in, 16)
            sp.dma_start(row1[:, :], rows).then_inc(w_in, 16)
            sp.dma_start(rw0[:, :], router0).then_inc(w_in, 16)
            sp.dma_start(rw3[:, :], gate).then_inc(w_in, 16)
            sp.dma_start(wl[:, :, :], w_l3.rearrange("p (m d) -> p m d", d=LD)).then_inc(w_in, 16)
            for t in range(2):
                sp.dma_start(wo[t * LD:t * LD + LD, :], wo_l3).then_inc(w_in, 16)
            sp.wait_ge(consts, CONSTS)
            sp.dma_start(xs3[0:E3 * CAP3, :].rearrange("n d -> (n d)").rearrange("(e p k) -> p e k", p=P, e=E3),
                         zt[:, :].unsqueeze(1).to_broadcast([P, E3, CAP3])).then_inc(zeroed, 16)
            sp.dma_start(xs0[E0 * ROOM0:E0 * ROOM0 + 8 * S, :].rearrange("(e p r) d -> p e (r d)", p=P, e=8),
                         zt[:, 0:2 * D].unsqueeze(1).to_broadcast([P, 8, 2 * D])).then_inc(zeroed, 16)
            heads_sync(sp, 0, 0, 0)
            load_x_routed(sp, N, N, 0, 64)
            list_sync(sp)
            experts_sync(sp, 0, True)
            load_x_only(sp, 4, 2 * N, 2 * N)
            load_x_only(sp, 4, 3 * N, 3 * N)
            heads_sync(sp, N, 4 * N, 4 * N)
            load_x_only(sp, 4, 5 * N, 5 * N)
            load_x_only(sp, 4, 6 * N, 6 * N)
            load_x_routed(sp, 7 * N, 7 * N, 64 * N, 32)
            experts_sync(sp, NG, False)
            store_out(sp, 7 * N)

        @block.tensor
        def _(pe):
            pe.wait_ge(w_in, W_IN)
            pe.wait_ge(consts, CONSTS)
            pe.wait_ge(consts_v, CONSTS_V)
            pe.matmul(po0[:, 0:3 * D], ones[0:1, :], row1[:, :], start=True, stop=True).then_inc(rows_ps, 1)
            pe.wait_ge(rows_sb, len(ROWS))
            heads_tensor(pe, 0, 0, False, 0)
            route_tensor(pe, 0, N, E0, rw0)
            list_tensor(pe)
            experts_tensor(pe, 0, S, NG)
            single_tensor(pe, 2 * N, 2 * N)
            mixing_tensor(pe, 0, 3 * N, 1)
            heads_tensor(pe, N, 4 * N, True, 2)
            mixing_tensor(pe, N, 5 * N, 2)
            linear_tensor(pe, 6 * N, 6 * N)
            route_tensor(pe, N, 7 * N, E3, rw3)
            experts_tensor(pe, NG, CAP3, E3)

        @block.scalar
        def _(act):
            heads_scalar(act, 0, 0, False)
            route_scalar(act, 0, N, E0)
            experts_scalar(act, 0, S, NG, True)
            single_scalar(act, 2 * N)
            mixing_scalar(act, 0, 3 * N, 1)
            heads_scalar(act, N, 4 * N, True)
            mixing_scalar(act, N, 5 * N, 2)
            linear_scalar(act, 6 * N)
            route_scalar(act, N, 7 * N, E3)
            experts_scalar(act, NG, CAP3, E3, False)

        @block.vector
        def _(dve):
            for i in range(SLOTS):
                nc.vector.memset(va[i][:, :, :, DH:DH + 1], 1.0).then_inc(consts_v, 1)
                nc.vector.memset(va[i][:, :, :, DH + 1:], 0.0).then_inc(consts_v, 1)
                nc.vector.memset(xt[i][:, 0:1], 0.0).then_inc(consts_v, 1)
                nc.vector.memset(ks[i][MAX_AT:MAX_AT + 3, :, :], 1.0).then_inc(consts_v, 1)
            dve.wait_ge(w_in, W_IN)
            nc.vector.tensor_scalar(omu[:, :], cv[:, COLS.index("mr1"):COLS.index("mr1") + 4], -1.0, 1.0,
                                    ALU.mult, ALU.add).then_inc(consts_v, 1)
            dve.wait_ge(rows_ps, 1)
            for i in range(len(ROWS)):
                nc.vector.tensor_copy(rowb[:, i, :], po0[:, i * D:i * D + D]).then_inc(rows_sb, 1)
            dve.wait_ge(rows_sb, len(ROWS))
            dve.wait_ge(consts_v, CONSTS_V)
            dve.wait_ge(x_in, 16)
            heads_vector(dve, 0, 0, False, 0)
            route_vector(dve, 0, E0, 2, base0)
            list_vector(dve)
            experts_vector(dve, 0, S, NG, True)
            gather_vector(dve, 0, N, 2, 0)
            single_vector(dve, 2 * N)
            mixing_vector(dve, 0, 3 * N, 3 * N, 1)
            heads_vector(dve, N, 4 * N, True, 2)
            mixing_vector(dve, N, 5 * N, 5 * N, 2)
            linear_vector(dve, 6 * N)
            dve.wait_ge(wt_sb, 5 * N)
            route_vector(dve, N, E3, 1, base3)
            experts_vector(dve, NG, CAP3, E3, False)
            gather_vector(dve, N, 7 * N, 1, 64 * N)

        @block.gpsimd
        def _(pool):
            g = nc.gpsimd
            for t, v in ((ident, 0.0), (ones, 1.0), (upto, 1.0), (hide_k, 0.0), (hide_q, 0.0), (half, -0.5),
                         (zt, 0.0), (zero_col, 0.0), (ones16, 1.0), (upto16, 1.0), (ident16, 0.0)):
                g.memset(t[tuple([slice(None)] * len(t.shape))], v).then_inc(cleared, 1)
            for i in range(SLOTS):
                g.memset(ks[i][0:MAX_AT, :, :], 0.0).then_inc(cleared, 1)
            pool.wait_ge(cleared, 11 + SLOTS)
            for t in (ident, ident16):
                g.affine_select(out=t[:, :], in_=t[:, :], compare_op=ALU.not_equal, fill=1.0, base=0,
                                pattern=[[-1, P]], channel_multiplier=1).then_inc(consts, 1)
            for t in (upto[:, 0, :], upto16[:, :]):
                g.affine_select(out=t, in_=t, compare_op=ALU.is_ge, fill=0.0, base=0,
                                pattern=[[1, P]], channel_multiplier=-1).then_inc(consts, 1)
            g.affine_select(out=hide_k[:, :], in_=hide_k[:, :], compare_op=ALU.is_ge, fill=HIDE, base=0,
                            pattern=[[1, P]], channel_multiplier=-1).then_inc(consts, 1)
            g.affine_select(out=hide_q[:, :], in_=hide_q[:, :], compare_op=ALU.is_ge, fill=HIDE, base=0,
                            pattern=[[-1, P]], channel_multiplier=1).then_inc(consts, 1)
            ig = {"allow_small_or_imprecise_dtypes": True}
            g.iota(iota_e[:, :], [[1, EM]], base=0, channel_multiplier=0, **ig).then_inc(consts, 1)
            g.iota(iota_g[:, :], [[1, NG]], base=0, channel_multiplier=0, **ig).then_inc(consts, 1)
            g.iota(dump[:, :], [[P, TILES]], base=DUMP, channel_multiplier=1, **ig).then_inc(consts, 1)
            g.iota(base0[:, :, :], [[0, 2], [ROOM0, E0]], base=-1, channel_multiplier=0, **ig).then_inc(consts, 1)
            g.iota(base3[:, :, :], [[0, 2], [CAP3, E3]], base=-1, channel_multiplier=0, **ig).then_inc(consts, 1)
            heads_pool(pool, 0, 0, 0)
            route_pool(pool, 0, 2, xs0)
            gather_pool(pool, 0, N, 2, ys0, 16 * NG, 0)
            norm_pool(pool, 2 * N, 6, 4)
            mixing_pool(pool, 0, 3 * N)
            heads_pool(pool, N, 4 * N, 2)
            mixing_pool(pool, N, 5 * N)
            norm_pool(pool, 6 * N, 5, 3)
            route_pool(pool, N, 1, xs3)
            gather_pool(pool, N, 7 * N, 1, ys3, 16 * (NG + E3), 64 * N)


_INS = ["x", "mats", "cols", "rows", "router0", "pack0", "w_l3", "wo_l3", "gate", "pack3"]


def kernel(**inputs):
    import numpy as _np
    import concourse.bacc as _bacc
    from concourse import mybir as _mybir
    from concourse.bass_utils import run_bass_kernel_spmd as _run

    a = {k: _np.asarray(v) for k, v in inputs.items()}

    def turned(w):
        return w.T

    def by_dim(w):
        return w.reshape(HEADS, DH, D).transpose(1, 0, 2).reshape(D, D).T

    def col_by_dim(b):
        return b.reshape(HEADS, DH).T.reshape(D)

    def by_chunk(w):
        return w.reshape(-1, FC, P, D).transpose(0, 2, 1, 3).reshape(-1, P, FC * D)

    w1 = a["L1_attn_W"]
    b1 = a["L1_attn_b"]
    mats = [by_dim(a["L0_attn_Wq"]), by_dim(a["L0_attn_Wk"]), turned(a["L0_attn_Wv"]), turned(a["L0_attn_Wo"]),
            turned(w1[0:D]), turned(w1[D:2 * D]), turned(w1[2 * D:3 * D]),
            turned(a["L1_ffn_W_r"]), turned(a["L1_ffn_W_k"]), turned(a["L1_ffn_W_v"]),
            by_dim(a["L2_attn_Wq"]), by_dim(a["L2_attn_Wk"]), turned(a["L2_attn_Wv"]), turned(a["L2_attn_Wo"]),
            turned(a["L2_ffn_W_r"]), turned(a["L2_ffn_W_k"]), turned(a["L2_ffn_W_v"])]
    cols = [col_by_dim(a["L0_attn_bq"]), col_by_dim(a["L0_attn_bk"]), b1[0:D], b1[D:2 * D],
            a["L1_ffn_mu_r"], a["L1_ffn_mu_k"], a["L2_ffn_mu_r"], a["L2_ffn_mu_k"]]
    laid = {
        "x": a["L0_attn_x"].reshape(TILES, P, D),
        "mats": _np.concatenate(mats, axis=1),
        "cols": _np.stack(cols, axis=1),
        "rows": _np.concatenate([a["L0_attn_bv"], a["L0_attn_bo"], b1[2 * D:3 * D]]).reshape(1, 3 * D),
        "router0": a["L0_ffn_router_w"],
        "pack0": _np.concatenate([a["L0_ffn_w1"], by_chunk(a["L0_ffn_w2"]),
                                  a["L0_ffn_b1"].reshape(E0, FC, P).transpose(0, 2, 1),
                                  a["L0_ffn_b2"].reshape(E0, D, 1)], axis=2),
        "w_l3": _np.concatenate([a["L3_attn_W_q"], a["L3_attn_W_k"], a["L3_attn_W_v"]], axis=1),
        "wo_l3": a["L3_attn_W_o"],
        "gate": a["L3_ffn_gate_w"].T,
        "pack3": _np.concatenate([a["L3_ffn_w1"], by_chunk(a["L3_ffn_w2"])], axis=2),
    }
    nc = _bacc.Bacc("TRN2", target_bir_lowering=False, num_devices=1)
    arrays, args = {}, []
    for name in _INS:
        v = _np.ascontiguousarray(laid[name])
        arrays[f"in_{name}"] = v
        args.append(nc.dram_tensor(f"in_{name}", v.shape, _mybir.dt.from_np(v.dtype), kind="ExternalInput").ap())
    args.append(nc.dram_tensor("out_x", (TILES, P, D), F32, kind="ExternalOutput").ap())
    post_norm_stack(nc, *args)
    r = _run(nc, [arrays], core_ids=[0])
    return r.results[0]["out_x"].reshape(SEQS, S, D)
```

```python
from contextlib import ExitStack

import numpy as np

import concourse.bass as bass
from concourse import mybir

P = 128
D = 128
SEQS = 16
S = 256
TILES = SEQS * S // P
HEADS = 16
DH = D // HEADS
SLOTS = 4
EPS = 1e-5

E0 = 8
F = 512
FC = F // P
CAP0 = SEQS * S
ROOM0 = CAP0 + S
GROUPS0 = 2 * SEQS + E0 - 1
E3 = 16
CAP3 = 320
HIDE = -1e30

F32 = mybir.dt.float32
BF16 = mybir.dt.bfloat16
I32 = mybir.dt.int32
U32 = mybir.dt.uint32
ALU = mybir.AluOpType
ACT = mybir.ActivationFunctionType
AX = mybir.AxisListType

MATS = ["q0", "k0", "v0", "o0", "q1", "k1", "v1", "r1", "m1", "w1", "q2", "k2", "v2", "o2",
        "r2", "m2", "w2"]
COLS = ["bq0", "bk0", "bq1", "bk1", "mr1", "mk1", "mr2", "mk2"]
ROWS = ["bv0", "bo0", "bv1"]


class Seq:

    def __init__(self, n, slot, least, turn):
        self.n, self.slot, self.least, self.turn = n, slot, least, turn

    def back(self, k):
        return self.n - (k if isinstance(self.n, int) else min(k, self.least))


def sweep(eng, lags, step, n=SEQS, lead=0):
    def peeled(s):
        step(lambda k: Seq(s - k, (s - k) % SLOTS, s - k, (s - k) // SLOTS) if 0 <= s - k < n else None)

    first = lags - 1 + lead
    full = n - first
    for s in range(first):
        peeled(s)
    with eng.Fori(0, full // SLOTS) as i:
        for c in range(SLOTS):
            s0 = first + c
            step(lambda k: Seq(SLOTS * i + (s0 - k), (s0 - k) % SLOTS, s0 - k,
                               i + (s0 - k) // SLOTS))
    for s in range(first + full // SLOTS * SLOTS, n + lags - 1):
        peeled(s)


class Norm:

    def __init__(self, sb, sem, name):
        def slots(what, shape):
            return [sb(f"{what}{name}{i}", shape) for i in range(SLOTS)]

        self.res, self.res_sb = slots("res", [P, 2, D]), sem("res_sb" + name)
        self.st, self.ln_st = slots("st", [P, 2, 6]), sem("ln_st" + name)
        self.mv, self.ln_mv = slots("mv", [P, 2, 2]), sem("ln_mv" + name)
        self.ve, self.ln_ve = slots("ve", [P, 2, 1]), sem("ln_ve" + name)
        self.rstd, self.ln_rs = slots("rstd", [P, 2, 1]), sem("ln_rs" + name)
        self.ln_x = sem("ln_x" + name)


def behind(at, k):
    return lambda i: at(i + k)


def wait(eng, sem, n):
    if isinstance(n, int) and n <= 0:
        return
    eng.wait_ge(sem, n)


def wait_apart(eng, sem, n, passed):
    wait(eng, sem, n)
    eng.sem_inc(passed, 1)


def post_norm_stack(nc, x, mats, cols, rows, router0, pack0,
                    w_l3, wo_l3, gate, pack3, out):
    with ExitStack() as ctx:
        def sb(name, shape, dt=F32, at=ctx):
            return at.enter_context(nc.sbuf_tensor(name, shape, dt))

        def sem(name):
            return ctx.enter_context(nc.semaphore(name))

        xg = sb("xg", [P, TILES, D])
        wm = sb("wm", [P, len(MATS), D])
        cv = sb("cv", [P, len(COLS)])
        row1 = sb("row1", [1, len(ROWS) * D])
        rowb = sb("rowb", [P, len(ROWS), D])
        ident = sb("ident", [P, P])
        ident16 = sb("ident16", [P, P], BF16)
        ones = sb("ones", [P, P])
        upto = sb("upto", [P, 2, P])
        hide_k = sb("hide_k", [P, P], BF16)
        hide_q = sb("hide_q", [P, P], BF16)
        half = sb("half", [P, 2])
        omu = sb("omu", [P, 4])
        xs = [sb(f"xs{i}", [P, 2, D]) for i in range(SLOTS)]
        xt = [sb(f"xt{i}", [P, 1 + S]) for i in range(SLOTS)]
        every = Norm(sb, sem, "")
        mixed = Norm(sb, sem, "_m")
        res, res_sb, ln_x = every.res, every.res_sb, every.ln_x
        zero_col = sb("zero_col", [P, 1])
        xr = [sb(f"xr{i}", [P, 2, D]) for i in range(SLOTS)]
        xrt = [sb(f"xrt{i}", [P, S]) for i in range(2)]

        EM = max(E0, E3)
        NG = GROUPS0 + 1
        LD = 64
        rw0 = sb("rw0", [P, E0])
        rw3 = sb("rw3", [P, E3])
        wl = sb("wl", [P, 3, LD])
        wo = sb("wo", [P, D])
        iota_e = sb("iota_e", [P, EM])
        iota_g = sb("iota_g", [P, NG])
        base0 = sb("base0", [P, 2, E0])
        base3 = sb("base3", [P, 2, E3])
        dump = sb("dump", [P, TILES])
        upto16 = sb("upto16", [P, P], BF16)
        ones16 = sb("ones16", [P, P], BF16)
        zt = sb("zt", [P, CAP3])
        STACK, MAX_AT = 48, 96
        ks = [sb(f"ks{i}", [MAX_AT + 3, HEADS, S], BF16) for i in range(SLOTS)]
        va = [sb(f"va{i}", [P, 2, HEADS, 32]) for i in range(SLOTS)]

        lg = [sb(f"lg{i}", [P, 2, EM]) for i in range(2)]
        top = [sb(f"top{i}", [P, 2, 8]) for i in range(2)]
        topi = [sb(f"topi{i}", [P, 2, 8], U32) for i in range(2)]
        topf = [sb(f"topf{i}", [P, 2, 8]) for i in range(2)]
        oh = [sb(f"oh{i}", [P, 2, 2, EM]) for i in range(2)]
        sel = [sb(f"sel{i}", [P, 2, EM], BF16) for i in range(SLOTS)]
        seen = [sb(f"seen{i}", [P, EM], BF16) for i in range(SLOTS)]
        rank = [sb(f"rank{i}", [P, 2, EM]) for i in range(2)]
        pick = [sb(f"pick{i}", [P, 2, 2, EM]) for i in range(2)]
        pl = [sb(f"pl{i}", [P, 4, 2]) for i in range(2)]
        gap = [sb(f"gap{i}", [P, 2, EM]) for i in range(2)]
        eg = [sb(f"eg{i}", [P, 2, EM]) for i in range(2)]
        place = [sb(f"place{i}", [P, 2, 2], U32) for i in range(SLOTS)]
        places = sb("places", [P, TILES, 2], U32)
        weight = sb("weight", [P, TILES, 2])
        sm = [sb(f"sm{i}", [P, 4, 2]) for i in range(2)]
        gs = [sb(f"gs{i}", [P, 2, EM]) for i in range(2)]
        run = [sb(f"run{i}", [P, EM]) for i in range(2)]

        with ExitStack() as mem:
            qs = [sb(f"qs{i}", [MAX_AT + 3, HEADS, S], BF16, mem) for i in range(SLOTS)]
            ex = [sb(f"ex{i}", [P, 4, S], F32, mem) for i in range(2)]
            qk = [sb(f"qk{i}", [P, 2, S], F32, mem) for i in range(2)]
            rem = [sb(f"rem{i}", [P, 2, S], F32, mem) for i in range(2)]
            parts = [sb(f"parts{i}", [P, 3, 2, S], BF16, mem) for i in range(2)]
            mx = [sb(f"mx{i}", [P, 2, HEADS], F32, mem) for i in range(2)]
            mr = [sb(f"mr{i}", [P, 2, HEADS], F32, mem) for i in range(2)]
            mp = [sb(f"mp{i}", [P, 2, 3, HEADS], BF16, mem) for i in range(2)]
            mt = [sb(f"mt{i}", [96, P], BF16, mem) for i in range(2)]
            ob = sb("ob", [P, 4, S], F32, mem)
            rc = [sb(f"rc{i}", [P, 2, HEADS], F32, mem) for i in range(2)]
            on = [sb(f"on{i}", [P, 2, D], F32, mem) for i in range(2)]
            ont = [sb(f"ont{i}", [P, S], F32, mem) for i in range(2)]
            xb = [sb(f"xb{i}", [P, 2, D], F32, mem) for i in range(SLOTS)]

        scr = nc.dram_tensor("scr", (SLOTS, 3, 2, P, S), BF16).ap()

        def psum(name, shape, dt=F32):
            return ctx.enter_context(nc.psum_tensor(name, shape, dt))

        p0 = psum("p0", [P, 512])
        p1 = psum("p1", [P, 512])
        pt = psum("pt", [P, 2, 512])
        pm = psum("pm", [P, 2, 512])
        po = psum("po", [P, 2, 512])

        passed = sem("passed")
        consts = sem("consts")
        consts_v = sem("consts_v")
        w_in = sem("w_in")
        x_first = sem("x_first")
        x_in = sem("x_in")
        rows_ps = sem("rows_ps")
        rows_sb = sem("rows_sb")
        x_loaded = [sem(f"x_loaded{i}") for i in range(SLOTS)]
        xt_ps = sem("xt_ps")
        xt_sb = sem("xt_sb")
        out_done = sem("out_done")
        qk_ps = sem("qk_ps")
        v_ps = sem("v_ps")
        qk_sb = sem("qk_sb")
        v_sb = sem("v_sb")
        part1 = sem("part1")
        rest1 = sem("rest1")
        part2 = sem("part2")
        part3 = sem("part3")
        to_scr = sem("to_scr")
        stacked = [sem(f"stacked{i}") for i in range(SLOTS)]
        ms_ps = sem("ms_ps")
        ms_max = sem("ms_max")
        m_parts = sem("m_parts")
        mt_ps = sem("mt_ps")
        mt_sb = sem("mt_sb")
        mrows = [sem(f"mrows{i}") for i in range(SLOTS)]
        ts_ps = sem("ts_ps")
        e_sb = sem("e_sb")
        pv_ps = sem("pv_ps")
        o_sb = sem("o_sb")
        ot_ps = sem("ot_ps")
        o_rc = sem("o_rc")
        o_rc2 = sem("o_rc2")
        o_nrm = sem("o_nrm")
        ont_ps = sem("ont_ps")
        ont_sb = sem("ont_sb")
        y_ps = sem("y_ps")
        xb_sb = sem("xb_sb")

        W_IN = 16 * 8
        FIRST = 2
        CONSTS = 11
        cleared = sem("cleared")
        xr_loaded = [sem(f"xr_loaded{i}") for i in range(SLOTS)]
        xrt_ps, xrt_sb = sem("xrt_ps"), sem("xrt_sb")
        stack_zero = sem("stack_zero")
        SPLITS = 16 * 6

        def mat(name):
            return wm[:, MATS.index(name), :]

        def col(name):
            return cv[:, COLS.index(name):COLS.index(name) + 1]

        def row(name):
            return rowb[:, ROWS.index(name), :]

        def load_x(sp, q, done, normed):
            if normed == "mixed":
                wait_apart(sp, mixed.ln_x, 2 * (q.n + 1), passed)
            else:
                if normed:
                    wait_apart(sp, ln_x, 2 * (normed - SEQS + q.n + 1), passed)
                else:
                    sp.wait_ge(x_first, 16)
                    if not (isinstance(q.n, int) and q.n < FIRST):
                        sp.wait_ge(x_in, 16)
            wait_apart(sp, xt_ps, done + q.back(3), passed)
            sp.dma_start(xs[q.slot][:, :, :], xg[:, bass.ds(2 * q.n, 2), :]).then_inc(x_loaded[q.slot], 16)

        def transpose_x(pe, q, done):
            pe.wait_ge(x_loaded[q.slot], 16 * (done // SLOTS + q.turn + 1))
            pe.transpose(p0[:, 0:P], xs[q.slot][:, 0, :], ident[:, :])
            pe.transpose(p0[:, P:S], xs[q.slot][:, 1, :], ident[:, :]).then_inc(xt_ps, 1)

        def copy_xt(act, q, done):
            act.wait_ge(xt_ps, done + q.n + 1)
            nc.scalar.copy(xt[q.slot][:, 1:1 + S], p0[:, 0:S]).then_inc(xt_sb, 1)

        def norm_stats(dve, q, done, of=None):
            of = of or every
            dve.wait_ge(of.res_sb, done + q.n + 1)
            for t in range(2):
                nc.vector.bn_stats(of.st[q.slot][:, t, :], of.res[q.slot][:, t, :]).then_inc(of.ln_st, 1)
            for t in range(2):
                wait_apart(dve, of.ln_st, 2 * (done + q.n) + 1 + t, passed)
                nc.vector.bn_aggr(of.mv[q.slot][:, t, :], of.st[q.slot][:, t, :]).then_inc(of.ln_mv, 1)

        def norm_rstd(pool, q, done, of=None):
            of = of or every
            wait_apart(pool, of.ln_mv, 2 * (done + q.n + 1), passed)
            nc.gpsimd.tensor_scalar(of.ve[q.slot][:, :, :], of.mv[q.slot][:, :, 1:2], EPS, None,
                                    ALU.add).then_inc(of.ln_ve, 1)
            pool.wait_ge(of.ln_ve, done + q.n + 1)
            nc.gpsimd.tensor_tensor(of.rstd[q.slot][:, :, :], of.ve[q.slot][:, :, :],
                                    half[:, :].unsqueeze(2), ALU.pow).then_inc(of.ln_rs, 1)

        def norm_apply(dve, q, done, of=None):
            of = of or every
            dve.wait_ge(of.ln_rs, done + q.n + 1)
            for t in range(2):
                nc.vector.tensor_scalar(xg[:, bass.ds(2 * q.n + t, 1), :], of.res[q.slot][:, t:t + 1, :],
                                        of.mv[q.slot][:, t, 0:1], of.rstd[q.slot][:, t, :],
                                        ALU.subtract, ALU.mult).then_inc(of.ln_x, 1)

        M0 = 1
        T0 = 4
        V0 = T0 + 1

        def heads_sync(sp, a, g, n, routed):
            def step(at):
                if (q := at(0)):
                    load_x(sp, q, g, n)
                if (q := at(3)):
                    sp.wait_ge(mt_sb, a + q.n + 1)
                    for t in range(2):
                        sp.dma_start(qs[q.slot][MAX_AT:MAX_AT + 3, :, t * P:t * P + P],
                                     mt[q.slot % 2][STACK * t:STACK * t + STACK, :]).then_inc(mrows[q.slot], 16)
                if (q := at(1)):
                    sp.wait_ge(part3, a + q.n + 1)
                    sp.dma_start(scr[q.slot].rearrange("t i p k -> p (t i) k"),
                                 parts[q.slot % 2][:, :, :, :].rearrange("p t i k -> p (t i) k")).then_inc(to_scr, 16)
                    wait_apart(sp, to_scr, 16 * (a + q.n + 1), passed)
                    wait_apart(sp, ts_ps, 16 * (a + q.back(3)), passed)
                    sp.wait_ge(stack_zero, SLOTS * (2 if a == 0 else 3))
                    for first, n_rows in ((0, 24), (24, 16), (40, 8)):
                        src = scr[q.slot, 0:n_rows // DH, 0].rearrange("t (d h) k -> t d (h k)", h=HEADS)
                        sp.dma_start(qs[q.slot][first:first + n_rows, :, :].rearrange("r h k -> r (h k)"), src).then_inc(stacked[q.slot], 16)
                        src = scr[q.slot, 3 - n_rows // DH, 1].rearrange("(d h) k -> d (h k)", h=HEADS)
                        sp.dma_start(ks[q.slot][first:first + n_rows, :, :].rearrange("r h k -> r (h k)"),
                                     src.unsqueeze(0).to_broadcast([n_rows // DH, DH, HEADS * S])
                                     ).then_inc(stacked[q.slot], 16)
                if routed and (q := at(5)):
                    wait_apart(sp, ln_x, 2 * (n + q.n + 1), passed)
                    wait_apart(sp, scattered[q.slot], 64 * q.turn, passed)
                    sp.dma_start(xr[q.slot][:, :, :], xg[:, bass.ds(2 * q.n, 2), :]).then_inc(xr_loaded[q.slot], 16)
            sweep(sp, 6, step, lead=SLOTS if routed else 0)

        def heads_tensor(pe, a, g, causal, layer, routed):
            def scores_t(q, j, u):
                b, kt = j // 2, j % 2
                pe.wait_ge(stacked[q.slot], SPLITS * (a // SLOTS + q.turn + 1))
                pe.wait_ge(mrows[q.slot], 32 * (a // SLOTS + q.turn + 1))
                wait(pe, e_sb, 16 * (a + q.n) + 2 * j + u - 1)
                for i in (2 * u, 2 * u + 1):
                    h = 4 * b + i
                    dst = pt[:, i // 2, (i % 2) * S:(i % 2) * S + S]
                    lhs = ks[q.slot][:, h, kt * P:kt * P + P]
                    rhs = qs[q.slot][:, h, :]
                    if not causal:
                        last = pe.matmul(dst, lhs, rhs, start=True, stop=True)
                        continue
                    d0 = kt * P
                    pe.matmul(dst[:, d0:d0 + P], ident16[:, :], hide_k[:, :], start=True, stop=False)
                    last = pe.matmul(dst[:, d0:d0 + P], lhs, rhs[:, d0:d0 + P], start=False, stop=True)
                    if kt == 0:
                        last = pe.matmul(dst[:, P:S], lhs, rhs[:, P:S], start=True, stop=True)
                last.then_inc(ts_ps, 1)

            def scores_m(q, j, u):
                b, qt = j // 2, j % 2
                if j == 0:
                    pe.wait_ge(stacked[q.slot], SPLITS * (a // SLOTS + q.turn + 1))
                wait(pe, ms_max, 16 * (a + q.n) + 2 * j + u - 1)
                for i in (2 * u, 2 * u + 1):
                    h = 4 * b + i
                    dst = pm[:, i // 2, (i % 2) * S:(i % 2) * S + S]
                    lhs = qs[q.slot][0:MAX_AT, h, qt * P:qt * P + P]
                    rhs = ks[q.slot][0:MAX_AT, h, :]
                    if not causal:
                        last = pe.matmul(dst, lhs, rhs, start=True, stop=True)
                        continue
                    d0 = qt * P
                    if qt == 1:
                        pe.matmul(dst[:, 0:P], lhs, rhs[:, 0:P], start=True, stop=True)
                    pe.matmul(dst[:, d0:d0 + P], ident16[:, :], hide_q[:, :], start=True, stop=False)
                    last = pe.matmul(dst[:, d0:d0 + P], lhs, rhs[:, d0:d0 + P], start=False, stop=True)
                last.then_inc(ms_ps, 1)

            def times_v(q, j):
                b, kt = j // 2, j % 2
                pe.wait_ge(e_sb, 16 * (a + q.n) + 2 * j + 2)
                pe.wait_ge(v_sb, 2 * (a + q.n + 1))
                if j == 0:
                    wait(pe, o_sb, a + q.n)
                lo = kt * P if causal else 0
                for i in range(4):
                    c0 = (b % 2) * S
                    last = pe.matmul(po[32 * i:32 * i + 32, b // 2, c0 + lo:c0 + S],
                                     va[q.slot][:, kt, 4 * b + i, :], ex[j % 2][:, i, lo:S],
                                     start=(kt == 0), stop=(kt == 1))
                last.then_inc(pv_ps, 1)

            def between(at, j, u):
                if (j, u) == (0, 0) and (q := at(0)):
                    wait(pe, v_sb, 2 * (a + q.n))
                    wait(pe, ont_sb, a + q.back(3))
                    transpose_x(pe, q, g)
                if (j, u) == (0, 1) and (q := at(4)):
                    pe.wait_ge(ont_sb, a + q.n + 1)
                    for t in range(2):
                        last = pe.matmul(p1[:, t * P:t * P + P], ont[q.slot % 2][:, t * P:t * P + P],
                                         mat(f"o{layer}"), start=True, stop=True)
                    last.then_inc(y_ps, 1)
                if j == 1 and (q := at(0)):
                    xq = xt[q.slot][:, 1:1 + S]
                    if u == 0:
                        pe.wait_ge(xt_sb, g + q.n + 1)
                        wait(pe, qk_sb, 2 * (a + q.n))
                        wait(pe, res_sb, n_of(layer) + q.back(3))
                        pe.matmul(p1[:, 0:S], mat(f"q{layer}"), xq, start=True, stop=True)
                    else:
                        pe.matmul(p1[:, S:2 * S], mat(f"k{layer}"), xq, start=True, stop=True).then_inc(qk_ps, 1)
                if (j, u) == (1, 1) and (q := at(2)):
                    if at(0):
                        pe.wait_ge(xt_sb, g + at(0).n + 1)
                    elif at(1):
                        pe.wait_ge(v_sb, 2 * (a + at(1).n + 1))
                    wait_apart(pe, m_parts, 4 * (a + q.n + 1), passed)
                    pe.transpose(p0[0:96, S:2 * S].bitcast(BF16)[:, 0:P],
                                 mp[q.slot % 2][:, :, :, :].rearrange("p t c h -> p (t c h)"),
                                 ident16[:, :]).then_inc(mt_ps, 1)
                if (j, u) == (2, 0) and (q := at(0)):
                    if at(2):
                        pe.wait_ge(mt_sb, a + at(2).n + 1)
                    for t in range(2):
                        last = pe.matmul(p0[:, t * P:t * P + P], xt[q.slot][:, 1 + t * P:1 + t * P + P],
                                         mat(f"v{layer}"), start=True, stop=True)
                    last.then_inc(v_ps, 1)
                if routed and (j, u) == (3, 0) and (q := at(5)):
                    if at(0):
                        pe.wait_ge(v_sb, 2 * (a + at(0).n + 1))
                    elif at(2):
                        pe.wait_ge(mt_sb, a + at(2).n + 1)
                    if at(4):
                        pe.wait_ge(ont_sb, a + at(4).n + 1)
                    if at(7):
                        pe.wait_ge(rank_sb, at(7).n + 1)
                    pe.wait_ge(xr_loaded[q.slot], 16 * (q.turn + 1))
                    for t in range(2):
                        last = pe.transpose(p0[:, t * P:t * P + P], xr[q.slot][:, t, :], ident[:, :])
                    last.then_inc(xrt_ps, 1)
                if routed and (j, u) == (4, 1):
                    if (q := at(6)):
                        if at(5):
                            pe.wait_ge(xrt_sb, at(5).n + 1)
                        ranks_tensor(pe, q, 0, E0, p0[:, S:S + 2 * E0])
                    if (q := at(5)):
                        pe.wait_ge(xrt_sb, q.n + 1)
                        wait(pe, lg_sb, q.n)
                        if at(0):
                            pe.wait_ge(qk_sb, 2 * (a + at(0).n + 1))
                        if at(4):
                            pe.wait_ge(res_sb, n_of(layer) + at(4).n + 1)
                        for t in range(2):
                            last = pe.matmul(p1[:, t * E0:t * E0 + E0], xrt[q.slot % 2][:, t * P:t * P + P],
                                             rw0[:, :], start=True, stop=True)
                        last.then_inc(lg_ps, 1)
                if j == 6 and (q := at(3)):
                    if u == 0:
                        if routed and at(6):
                            pe.wait_ge(rank_sb, at(6).n + 1)
                        if routed and at(5):
                            pe.wait_ge(xrt_sb, at(5).n + 1)
                            pe.wait_ge(lg_sb, at(5).n + 1)
                        pe.wait_ge(o_sb, a + q.n + 1)
                        if at(2):
                            pe.wait_ge(mt_sb, a + at(2).n + 1)
                        if at(4):
                            pe.wait_ge(res_sb, n_of(layer) + at(4).n + 1)
                        if at(0):
                            pe.wait_ge(v_sb, 2 * (a + at(0).n + 1))
                            pe.wait_ge(qk_sb, 2 * (a + at(0).n + 1))
                    for b in range(4):
                        last = pe.transpose((p0, p1)[u][:, b * P:b * P + P], ob[:, b, u * P:u * P + P], ident[:, :])
                    if u == 1:
                        last.then_inc(ot_ps, 1)
                if (j, u) == (7, 1) and (q := at(3)):
                    pe.wait_ge(o_nrm, 2 * (a + q.n + 1))
                    for t in range(2):
                        last = pe.transpose(p0[:, t * P:t * P + P], on[q.slot % 2][:, t, :], ident[:, :])
                    last.then_inc(ont_ps, 1)

            def step(at):
                for j in range(8):
                    for u in range(2):
                        if (q := at(2) if j >= T0 else at(3)):
                            scores_t(q, (j - T0) % 8, u)
                        if (q := at(1) if j >= M0 else at(2)):
                            scores_m(q, (j - M0) % 8, u)
                        between(at, j, u)
                    if (q := at(2) if j >= V0 else at(3)):
                        times_v(q, (j - V0) % 8)
            sweep(pe, 8 if routed else 5, step)

        def n_of(layer):
            return 0 if layer == 0 else 3 * SEQS

        def heads_scalar(act, a, g, causal, routed):
            def exps(q, j):
                wait(act, pv_ps, 8 * (a + q.n) + j - 1)
                lo = P if causal and j % 2 else 0
                for u in range(2):
                    act.wait_ge(ts_ps, 16 * (a + q.n) + 2 * j + u + 1)
                    nc.scalar.activation(ex[j % 2][:, 2 * u:2 * u + 2, lo:S],
                                         pt[:, u, :].rearrange("p (b k) -> p b k", k=S)[:, :, lo:S],
                                         ACT.Exp).then_inc(e_sb, 1)

            def step(at):
                for j in range(8):
                    if j == V0 and (q := at(3)):
                        act.wait_ge(pv_ps, 8 * (a + q.n + 1))
                        wait(act, ot_ps, a + q.n)
                        nc.scalar.copy(ob[:, :, :], po[:, :, :].rearrange("p a (b k) -> p (a b) k", k=S)
                                       ).then_inc(o_sb, 1)
                    if (q := at(2) if j >= T0 else at(3)):
                        exps(q, (j - T0) % 8)
                    if j == 0 and (q := at(0)):
                        copy_xt(act, q, g)
                    if j == 1 and (q := at(2)):
                        act.wait_ge(mt_ps, a + q.n + 1)
                        wait(act, ts_ps, 16 * (a + q.back(1)))
                        nc.scalar.copy(mt[q.slot % 2][:, :], p0[0:96, S:2 * S].bitcast(BF16)[:, 0:P]
                                       ).then_inc(mt_sb, 1)
                    if j == 2 and (q := at(0)):
                        act.wait_ge(qk_sb, 2 * (a + q.n + 1))
                        wait(act, to_scr, 16 * (a + q.back(1)))
                        nc.scalar.copy(parts[q.slot % 2][:, 0, :, :], qk[q.slot % 2][:, :, :]).then_inc(part1, 1)
                    if j == 3 and (q := at(0)):
                        act.wait_ge(rest1, a + q.n + 1)
                        nc.scalar.copy(parts[q.slot % 2][:, 1, :, :], rem[q.slot % 2][:, :, :]).then_inc(part2, 1)
                    if j == 7 and (q := at(3)):
                        act.wait_ge(ont_ps, a + q.n + 1)
                        wait(act, y_ps, a + q.back(1))
                        nc.scalar.copy(ont[q.slot % 2][:, :], p0[:, 0:S]).then_inc(ont_sb, 1)
                    if routed and j == 3 and (q := at(5)):
                        act.wait_ge(xrt_ps, q.n + 1)
                        wait(act, lg_ps, q.back(1))
                        nc.scalar.copy(xrt[q.slot % 2][:, :], p0[:, 0:S]).then_inc(xrt_sb, 1)
                    if routed and j == 4 and (q := at(6)):
                        exp_gaps(act, q, 0, E0)
            sweep(act, 7 if routed else 5, step, lead=1 if routed else 0)

        def heads_vector(dve, a, n, causal, layer, routed):
            def row_max(q, j):
                b, qt = j // 2, j % 2
                if j == 0:
                    wait(dve, m_parts, 4 * (a + q.back(1)))
                hi = P if causal and qt == 0 else S
                for u in range(2):
                    dve.wait_ge(ms_ps, 16 * (a + q.n) + 2 * j + u + 1)
                    nc.vector.tensor_reduce(mx[q.slot % 2][:, qt, 4 * b + 2 * u:4 * b + 2 * u + 2],
                                            pm[:, u, :].rearrange("p (b k) -> p b k", k=S)[:, :, 0:hi],
                                            AX.X, ALU.max).then_inc(ms_max, 1)

            def split_max(q):
                s = q.slot % 2
                k = 4 * (a + q.n)
                dve.wait_ge(ms_max, 16 * (a + q.n + 1))
                wait(dve, mt_ps, a + q.back(1))
                nc.vector.tensor_scalar(mp[s][:, :, 0, :], mx[s][:, :, :], -1.0, None,
                                        ALU.mult).then_inc(m_parts, 1)
                dve.wait_ge(m_parts, k + 1)
                nc.vector.scalar_tensor_tensor(mr[s][:, :, :], mx[s][:, :, :], -1.0, mp[s][:, :, 0, :],
                                               ALU.mult, ALU.subtract).then_inc(m_parts, 1)
                dve.wait_ge(m_parts, k + 2)
                nc.vector.tensor_copy(mp[s][:, :, 1, :], mr[s][:, :, :]).then_inc(m_parts, 1)
                dve.wait_ge(m_parts, k + 3)
                nc.vector.tensor_tensor(mp[s][:, :, 2, :], mr[s][:, :, :], mp[s][:, :, 1, :],
                                        ALU.subtract).then_inc(m_parts, 1)

            def step(at):
                for j in range(8):
                    if (q := at(1) if j >= M0 else at(2)):
                        row_max(q, (j - M0) % 8)
                    if j == 0 and (q := at(4)):
                        dve.wait_ge(y_ps, a + q.n + 1)
                        wait(dve, ln_x, 2 * (n + q.back(3)))
                        y = p1[:, 0:S].rearrange("p (t d) -> p t d", t=2)
                        if layer == 0:
                            dve.wait_ge(xb_sb, q.n + 1)
                            nc.vector.tensor_tensor(res[q.slot][:, :, :], y, xb[q.slot][:, :, :],
                                                    ALU.add).then_inc(res_sb, 1)
                        else:
                            nc.vector.tensor_tensor(res[q.slot][:, :, :], y,
                                                    xg[:, bass.ds(2 * q.n, 2), :], ALU.add).then_inc(res_sb, 1)
                    if j == M0 - 1 and (q := at(2)):
                        split_max(q)
                    if j == 0 and (q := at(4)):
                        norm_stats(dve, q, n)
                    if j == 1 and (q := at(0)):
                        dve.wait_ge(qk_ps, a + q.n + 1)
                        wait(dve, part3, a + q.back(1))
                        c = float(DH) ** -0.5
                        if layer == 0:
                            nc.vector.tensor_scalar(qk[q.slot % 2][:, 0, :], p1[:, 0:S], col("bq0"), c,
                                                    ALU.add, ALU.mult).then_inc(qk_sb, 1)
                            nc.vector.tensor_scalar(qk[q.slot % 2][:, 1, :], p1[:, S:2 * S], col("bk0"), None,
                                                    ALU.add).then_inc(qk_sb, 1)
                        else:
                            nc.vector.tensor_scalar(qk[q.slot % 2][:, 0, :], p1[:, 0:S], c, None,
                                                    ALU.mult).then_inc(qk_sb, 1)
                            nc.vector.tensor_copy(qk[q.slot % 2][:, 1, :], p1[:, S:2 * S]).then_inc(qk_sb, 1)
                    if j == 2 and (q := at(0)):
                        dve.wait_ge(v_ps, a + q.n + 1)
                        for t in range(2):
                            v = p0[:, t * P:t * P + P].rearrange("p (h d) -> p h d", h=HEADS)
                            dst = va[q.slot][:, t, :, 0:DH]
                            if layer == 0:
                                nc.vector.tensor_tensor(dst, v, row("bv0").rearrange("p (h d) -> p h d", h=HEADS),
                                                        ALU.add).then_inc(v_sb, 1)
                            else:
                                nc.vector.tensor_copy(dst, v).then_inc(v_sb, 1)
                    if j == 2 and (q := at(4)):
                        norm_apply(dve, q, n)
                    if j == 6 and (q := at(3)):
                        dve.wait_ge(ot_ps, a + q.n + 1)
                        for t, bank in ((0, p0), (1, p1)):
                            o = bank[:, :].rearrange("p (h d) -> p h d", d=32)
                            r = rc[q.slot % 2][:, t, :]
                            if layer == 2:
                                nc.vector.tensor_scalar(r.unsqueeze(2), o[:, :, DH:DH + 1], 1e-12, None,
                                                        ALU.max).then_inc(o_rc, 1)
                                dve.wait_ge(o_rc, 2 * q.n + t + 1)
                                nc.vector.reciprocal(r, r).then_inc(o_rc2, 1)
                            else:
                                nc.vector.reciprocal(r.unsqueeze(2), o[:, :, DH:DH + 1]).then_inc(o_rc2, 1)
                        for t, bank in ((0, p0), (1, p1)):
                            dve.wait_ge(o_rc2, 2 * (a + q.n) + t + 1)
                            o = bank[:, :].rearrange("p (h d) -> p h d", d=32)
                            nc.vector.tensor_tensor(on[q.slot % 2][:, t, :].rearrange("p (h d) -> p h d", h=HEADS),
                                                    o[:, :, 0:DH],
                                                    rc[q.slot % 2][:, t, :].unsqueeze(2).to_broadcast([P, HEADS, DH]),
                                                    ALU.mult).then_inc(o_nrm, 1)
                    if routed:
                        if j >= 5 and (q := at(5)):
                            choose(dve, q, 0, E0, 2, j - 5)
                        if j < 3 and (q := at(6)):
                            choose(dve, q, 0, E0, 2, j + 3)
                        if j >= 3 and (q := at(6)):
                            put(dve, q, 0, E0, 2, base0, p0[:, S:S + 2 * E0], j - 3)
                        if j < 2 and (q := at(7)):
                            put(dve, q, 0, E0, 2, base0, p0[:, S:S + 2 * E0], j + 5)
            sweep(dve, 8 if routed else 5, step, lead=SLOTS if routed else 0)

        def heads_pool(pool, a, n, layer, routed):
            for i in range(SLOTS):
                stacks = (qs, ks) if a == 0 else (qs,)
                for stack in stacks:
                    nc.gpsimd.memset(stack[i][0:MAX_AT, :, :].rearrange("p h k -> p (h k)").bitcast(F32),
                                     0.0).then_inc(stack_zero, 1)

            def step(at):
                if (q := at(4)):
                    norm_rstd(pool, q, n)
                if routed and (q := at(7)):
                    wait_apart(pool, place_sb, q.n + 1, passed)
                    scatter(pool, q, 0, xr, xs0)
                if (q := at(0)):
                    s = q.slot % 2
                    pool.wait_ge(part1, a + q.n + 1)
                    nc.gpsimd.tensor_tensor(rem[s][:, :, :], qk[s][:, :, :], parts[s][:, 0, :, :],
                                            ALU.subtract).then_inc(rest1, 1)
                    pool.wait_ge(part2, a + q.n + 1)
                    nc.gpsimd.tensor_tensor(parts[s][:, 2, :, :], rem[s][:, :, :], parts[s][:, 1, :, :],
                                            ALU.subtract).then_inc(part3, 1)
                if layer == 0 and (q := at(3)):
                    pool.wait_ge(x_first, 16)
                    pool.wait_ge(x_in, 16)
                    pool.wait_ge(rows_sb, len(ROWS))
                    wait(pool, res_sb, q.back(3))
                    for t in range(2):
                        ins = nc.gpsimd.tensor_tensor(xb[q.slot][:, t:t + 1, :], xg[:, bass.ds(2 * q.n + t, 1), :],
                                                      row("bo0").unsqueeze(1), ALU.add)
                    ins.then_inc(xb_sb, 1)
                if routed and (q := at(7)):
                    scatter(pool, q, 1, xr, xs0)
            sweep(pool, 8 if routed else 5, step)

        pt0, pt1, pm0, pm1, po0, po1 = (b[:, i, :] for b in (pt, pm, po) for i in range(2))
        with ExitStack() as mem:
            kq = [sb(f"kq{i}", [P, 2, S], F32, mem) for i in range(2)]
            v1 = [sb(f"v1_{i}", [P, 2, D], F32, mem) for i in range(2)]
            vn = [sb(f"vn{i}", [P, 2, D], F32, mem) for i in range(2)]
            e1 = [sb(f"e1_{i}", [P, 2, S], F32, mem) for i in range(2)]
            m1 = [sb(f"m1_{i}", [P, 2], F32, mem) for i in range(2)]
            nb1 = [sb(f"nb1_{i}", [P, 2], F32, mem) for i in range(2)]
            sum1 = [sb(f"sum1_{i}", [P, 2], F32, mem) for i in range(2)]
            inv1 = [sb(f"inv1_{i}", [P, 2], F32, mem) for i in range(2)]
        kq_ps, kq_sb, v1_ps, v1_sb = sem("kq_ps"), sem("kq_sb"), sem("v1_ps"), sem("v1_sb")
        s1_ps, s1_max, s1_nb, e1_sb = sem("s1_ps"), sem("s1_max"), sem("s1_nb"), sem("e1_sb")
        inv1_sb, vn_sb, y1_ps = sem("inv1_sb"), sem("vn_sb"), sem("y1_ps")

        def single_tensor(pe, g, n):
            def step(at):
                if (q := at(0)):
                    wait(pe, xt_sb, g + q.n)
                    transpose_x(pe, q, g)
                at = behind(at, 1)
                if (q := at(3)):
                    s = q.slot % 2
                    pe.wait_ge(vn_sb, 2 * (q.n + 1))
                    wait(pe, res_sb, n + q.back(1))
                    for i in range(2):
                        for t in range(2):
                            last = pe.matmul((po0, po1)[s][:, i * P:i * P + P], e1[s][:, t, i * P:i * P + P],
                                             vn[s][:, t, :], start=(t == 0), stop=(t == 1))
                    last.then_inc(y1_ps, 1)
                if (q := at(1)):
                    s = q.slot % 2
                    pe.wait_ge(kq_sb, 2 * (q.n + 1))
                    wait(pe, e1_sb, 2 * q.back(1))
                    for t in range(2):
                        last = pe.matmul((pt1, pm1)[s][:, t * S:t * S + S], kq[s][:, 1, t * P:t * P + P], kq[s][:, 0, :],
                                         start=True, stop=True)
                    last.then_inc(s1_ps, 1)
                if (q := at(0)):
                    pe.wait_ge(xt_sb, g + q.n + 1)
                    wait(pe, kq_sb, 2 * q.n)
                    xq = xt[q.slot][:, 1:1 + S]
                    pe.matmul(p1[:, 0:S], mat("q1"), xq, start=True, stop=True)
                    pe.matmul(p1[:, S:2 * S], mat("k1"), xq, start=True, stop=True).then_inc(kq_ps, 1)
                    wait(pe, v1_sb, q.n)
                    for t in range(2):
                        last = pe.matmul(pt0[:, t * P:t * P + P], xq[:, t * P:t * P + P], mat("v1"),
                                         start=True, stop=True)
                    last.then_inc(v1_ps, 1)
            sweep(pe, 6, step)

        def single_scalar(act, g):
            def step(at):
                if (q := at(0)):
                    copy_xt(act, q, g)
                at = behind(at, 1)
                if (q := at(1)):
                    s = q.slot % 2
                    act.wait_ge(s1_nb, q.n + 1)
                    wait(act, y1_ps, q.back(1))
                    for t in range(2):
                        nc.scalar.activation(e1[s][:, t, :], (pt1, pm1)[s][:, t * S:t * S + S], ACT.Exp,
                                             bias=nb1[s][:, t:t + 1], scale=1.0 / D,
                                             accum_out=sum1[s][:, t:t + 1]).then_inc(e1_sb, 1)
                if (q := at(0)):
                    act.wait_ge(kq_ps, q.n + 1)
                    wait(act, s1_ps, q.back(1))
                    for i, b in enumerate(("bq1", "bk1")):
                        nc.scalar.activation(kq[q.slot % 2][:, i, :], p1[:, i * S:i * S + S], ACT.Identity,
                                             bias=col(b)).then_inc(kq_sb, 1)
            sweep(act, 6, step)

        def single_vector(dve, n):
            def step(at):
                at = behind(at, 1)
                if (q := at(2)):
                    s = q.slot % 2
                    dve.wait_ge(e1_sb, 2 * (q.n + 1))
                    nc.vector.reciprocal(inv1[s][:, :], sum1[s][:, :]).then_inc(inv1_sb, 1)
                    dve.wait_ge(inv1_sb, q.n + 1)
                    dve.wait_ge(v1_sb, q.n + 1)
                    for t in range(2):
                        nc.vector.tensor_scalar(vn[s][:, t, :], v1[s][:, t, :], inv1[s][:, t:t + 1], None,
                                                ALU.mult).then_inc(vn_sb, 1)
                if (q := at(1)):
                    s = q.slot % 2
                    dve.wait_ge(s1_ps, q.n + 1)
                    nc.vector.tensor_reduce(m1[s][:, :], (pt1, pm1)[s][:, :].rearrange("p (t k) -> p t k", t=2), AX.X,
                                            ALU.max).then_inc(s1_max, 1)
                    dve.wait_ge(s1_max, q.n + 1)
                    nc.vector.tensor_scalar(nb1[s][:, :], m1[s][:, :], -1.0 / D, None,
                                            ALU.mult).then_inc(s1_nb, 1)
                if (q := at(0)):
                    s = q.slot % 2
                    dve.wait_ge(v1_ps, q.n + 1)
                    wait(dve, vn_sb, 2 * (q.back(1)))
                    nc.vector.tensor_tensor(v1[s][:, :, :], pt0[:, 0:S].rearrange("p (t d) -> p t d", t=2),
                                            row("bv1").unsqueeze(1).to_broadcast([P, 2, D]), ALU.add).then_inc(v1_sb, 1)
                if (q := at(4)):
                    norm_apply(dve, q, n)
                if (q := at(3)):
                    dve.wait_ge(y1_ps, q.n + 1)
                    add_x(dve, q, (po0, po1)[q.slot % 2])
                    norm_stats(dve, q, n)
            return step

        def add_x(dve, q, bank):
            nc.vector.tensor_tensor(res[q.slot][:, :, :], bank[:, 0:S].rearrange("p (t d) -> p t d", t=2),
                                    xg[:, bass.ds(2 * q.n, 2), :], ALU.add).then_inc(res_sb, 1)

        with ExitStack() as mem:
            mix = [sb(f"mix{i}", [P, 2, S], F32, mem) for i in range(2)]
            before = [sb(f"before{i}", [P, 2, S], F32, mem) for i in range(2)]
            rs = [sb(f"rs{i}", [P, 2, D], F32, mem) for i in range(SLOTS)]
            kr = [sb(f"kr{i}", [P, S], F32, mem) for i in range(2)]
            ka = [sb(f"ka{i}", [P, S], F32, mem) for i in range(2)]
            gv = [sb(f"gv{i}", [P, 2, D], F32, mem) for i in range(2)]
        before_sb, mix_sb, r_ps, k_ps = sem("before_sb"), sem("mix_sb"), sem("r_ps"), sem("k_ps")
        r_sb, kr_sb, ka_sb, vf_ps, gv_sb = sem("r_sb"), sem("kr_sb"), sem("ka_sb"), sem("vf_ps"), sem("gv_sb")

        def mixing_tensor(pe, a, g, layer):
            def step(at):
                if (q := at(0)):
                    wait(pe, xt_sb, g + q.n)
                    transpose_x(pe, q, g)
                at = behind(at, 1)
                if (q := at(1)):
                    s = q.slot % 2
                    pe.wait_ge(mix_sb, 2 * (a + q.n + 1))
                    wait(pe, r_sb, a + q.n)
                    for t in range(2):
                        last = pe.matmul(p1[:, t * P:t * P + P], mix[s][:, 0, t * P:t * P + P], mat(f"r{layer}"),
                                         start=True, stop=True)
                    last.then_inc(r_ps, 1)
                    wait(pe, kr_sb, a + q.n)
                    pe.matmul(pt0[:, 0:S], mat(f"m{layer}"), mix[s][:, 1, :], start=True, stop=True).then_inc(k_ps, 1)
                if (q := at(2)):
                    pe.wait_ge(ka_sb, a + q.n + 1)
                    wait(pe, gv_sb, a + q.n)
                    for t in range(2):
                        last = pe.matmul(pt1[:, t * P:t * P + P], ka[q.slot % 2][:, t * P:t * P + P],
                                         mat(f"w{layer}"), start=True, stop=True)
                    last.then_inc(vf_ps, 1)
            sweep(pe, 5, step)

        def mixing_scalar(act, a, g, layer):
            def step(at):
                if (q := at(0)):
                    copy_xt(act, q, g)
                    act.wait_ge(xt_sb, g + q.n + 1)
                    wait(act, mix_sb, 2 * (a + q.back(1)))
                    for c in range(2):
                        nc.scalar.mul(before[q.slot % 2][:, c, :], xt[q.slot][:, 0:S],
                                      omu[:, 2 * layer - 2 + c:2 * layer - 1 + c]).then_inc(before_sb, 1)
                at = behind(at, 1)
                if (q := at(1)):
                    act.wait_ge(r_ps, a + q.n + 1)
                    nc.scalar.activation(rs[q.slot][:, :, :], p1[:, 0:S].rearrange("p (t d) -> p t d", t=2),
                                         ACT.Sigmoid).then_inc(r_sb, 1)
                    act.wait_ge(k_ps, a + q.n + 1)
                    wait(act, ka_sb, a + q.back(1))
                    nc.scalar.activation(kr[q.slot % 2][:, :], pt0[:, 0:S], ACT.Relu).then_inc(kr_sb, 1)
            sweep(act, 5, step)

        def mixing_vector(dve, a, g, n, layer):
            def step(at):
                at = behind(at, 1)
                if (q := at(0)):
                    s = q.slot % 2
                    wait(dve, k_ps, a + q.back(1))
                    for c, mu in ((0, "mr"), (1, "mk")):
                        dve.wait_ge(before_sb, 2 * (a + q.n) + 1 + c)
                        nc.vector.scalar_tensor_tensor(mix[s][:, c, :], xt[q.slot][:, 1:1 + S],
                                                       col(f"{mu}{layer}"), before[s][:, c, :],
                                                       ALU.mult, ALU.add).then_inc(mix_sb, 1)
                if (q := at(3)):
                    norm_apply(dve, q, n)
                if (q := at(2)):
                    s = q.slot % 2
                    dve.wait_ge(vf_ps, a + q.n + 1)
                    nc.vector.tensor_tensor(gv[s][:, :, :], pt1[:, 0:S].rearrange("p (t d) -> p t d", t=2),
                                            rs[q.slot][:, :, :], ALU.mult).then_inc(gv_sb, 1)
                    dve.wait_ge(gv_sb, a + q.n + 1)
                    nc.vector.tensor_tensor(res[q.slot][:, :, :], gv[s][:, :, :], xg[:, bass.ds(2 * q.n, 2), :],
                                            ALU.add).then_inc(res_sb, 1)
                    norm_stats(dve, q, n)
            sweep(dve, 5, step)

        def mixing_pool(pool, a, n):
            def step(at):
                at = behind(at, 1)
                if (q := at(1)):
                    s = q.slot % 2
                    pool.wait_ge(kr_sb, a + q.n + 1)
                    wait(pool, vf_ps, a + q.back(1))
                    nc.gpsimd.tensor_tensor(ka[s][:, :], kr[s][:, :], kr[s][:, :], ALU.mult).then_inc(ka_sb, 1)
                if (q := at(2)):
                    norm_rstd(pool, q, n)
            sweep(pool, 5, step)

        def norm_pool(pool, n, lags, lag):
            def step(at):
                if (q := at(lag)):
                    norm_rstd(pool, q, n)
            sweep(pool, lags, step)

        with ExitStack() as mem:
            qt3 = [sb(f"qt3_{i}", [LD, S], F32, mem) for i in range(2)]
            vt3 = [sb(f"vt3_{i}", [LD, S], F32, mem) for i in range(2)]
            lowt = [sb(f"lowt{i}", [LD, S], F32, mem) for i in range(2)]
            low = [sb(f"low{i}", [P, S], F32, mem) for i in range(2)]
            elt = [sb(f"elt{i}", [LD, S], F32, mem) for i in range(2)]
            el = [sb(f"el{i}", [P, S], F32, mem) for i in range(2)]
            tok = [sb(f"tok{i}", [P, 2, 2, LD], F32, mem) for i in range(SLOTS)]
            am = [sb(f"am{i}", [P, 3, P], F32, mem) for i in range(2)]
            zq = [sb(f"zq{i}", [P, 2, LD], F32, mem) for i in range(2)]
            den = [sb(f"den{i}", [P, 2], F32, mem) for i in range(2)]
            den2 = [sb(f"den2_{i}", [P, 2], F32, mem) for i in range(2)]
            inv3 = [sb(f"inv3_{i}", [P, 2], F32, mem) for i in range(SLOTS)]
            o3 = [sb(f"o3_{i}", [P, 2, LD], F32, mem) for i in range(2)]
            ot3 = [sb(f"ot3_{i}", [P, P], F32, mem) for i in range(2)]
        t3_ps, tok_ps, low_sb, el_sb, qt3_sb, vt3_sb, tok_sb = (sem(s) for s in (
            "t3_ps", "tok_ps", "low_sb", "el_sb", "qt3_sb", "vt3_sb", "tok_sb"))
        a3_ps, z3_ps, am_sb, zq_sb, den_sb, den2_sb, inv3_sb = (sem(s) for s in (
            "a3_ps", "z3_ps", "am_sb", "zq_sb", "den_sb", "den2_sb", "inv3_sb"))
        o3_ps, o3_sb, ot3_ps, ot3_sb, y3_ps = (sem(s) for s in ("o3_ps", "o3_sb", "ot3_ps", "ot3_sb", "y3_ps"))

        def linear_tensor(pe, g, n):
            def step(at):
                if (q := at(0)):
                    wait(pe, xt_sb, g + q.n)
                    wait(pe, vt3_sb, q.back(1))
                    transpose_x(pe, q, g)
                ahead = at(0)
                at = behind(at, 1)
                if (q := at(2)):
                    s = q.slot % 2
                    pe.wait_ge(am_sb, 2 * (q.n + 1))
                    wait(pe, o3_sb, q.n)
                    k0, k1 = tok[q.slot][:, 0, 1, :], tok[q.slot][:, 1, 1, :]
                    pe.matmul(po0[:, 0:LD], am[s][:, 0, :], k0, start=True, stop=True)
                    pe.matmul(po0[:, LD:2 * LD], am[s][:, 1, :], k0, start=True, stop=False)
                    pe.matmul(po0[:, LD:2 * LD], am[s][:, 2, :], k1, start=False, stop=True).then_inc(o3_ps, 1)
                if (q := at(1)):
                    s = q.slot % 2
                    pe.wait_ge(qt3_sb, q.n + 1)
                    pe.wait_ge(vt3_sb, q.n + 1)
                    wait(pe, am_sb, 2 * q.n)
                    pe.matmul(pt1[:, 0:S], vt3[s][:, 0:P], qt3[s][:, :], start=True, stop=True)
                    pe.matmul(pt1[:, S:S + P], vt3[s][:, P:S], qt3[s][:, P:S], start=True, stop=True).then_inc(a3_ps, 1)
                    pe.wait_ge(tok_sb, q.n + 1)
                    wait(pe, zq_sb, q.n)
                    k0, k1 = tok[q.slot][:, 0, 1, :], tok[q.slot][:, 1, 1, :]
                    pe.matmul(pm0[:, 0:LD], upto[:, 0, :], k0, start=True, stop=True)
                    pe.matmul(pm0[:, LD:2 * LD], upto[:, 1, :], k0, start=True, stop=False)
                    pe.matmul(pm0[:, LD:2 * LD], upto[:, 0, :], k1, start=False, stop=True).then_inc(z3_ps, 1)
                if (q := at(2)):
                    pe.wait_ge(o3_sb, q.n + 1)
                    wait(pe, ot3_sb, q.n)
                    wait(pe, res_sb, n + q.n)
                    pe.transpose(po1[:, 0:P], o3[q.slot % 2][:, :, :].rearrange("p t d -> p (t d)"),
                                 ident[:, :]).then_inc(ot3_ps, 1)
                if (q := at(0)):
                    xq = xt[q.slot][:, 1:1 + S]
                    pe.wait_ge(xt_sb, g + q.n + 1)
                    wait(pe, qt3_sb, q.n)
                    pe.matmul(p1[0:LD, 0:S], wl[:, 0, :], xq, start=True, stop=True)
                    if ahead:
                        pe.wait_ge(xt_sb, g + ahead.n + 1)
                    pe.matmul(p0[0:LD, S:2 * S], wl[:, 2, :], xq, start=True, stop=True).then_inc(t3_ps, 1)
                    wait(pe, tok_sb, q.n)
                    for t in range(2):
                        last = pe.matmul(pt0[:, t * P:t * P + P], xq[:, t * P:t * P + P],
                                         wl[:, 0:2, :].rearrange("p a b -> p (a b)"), start=True, stop=True)
                    last.then_inc(tok_ps, 1)
                if (q := at(2)):
                    pe.wait_ge(ot3_sb, q.n + 1)
                    wait(pe, res_sb, n + q.n)
                    for t in range(2):
                        last = pe.matmul((pm1, po1)[t][:, t * P:t * P + P], ot3[q.slot % 2][t * LD:t * LD + LD, :],
                                         wo[t * LD:t * LD + LD, :],
                                         start=True, stop=True)
                    last.then_inc(y3_ps, 1)
            sweep(pe, 5, step)

        def linear_scalar(act, g):
            def step(at):
                if (q := at(0)):
                    copy_xt(act, q, g)
                at = behind(at, 1)
                if (q := at(2)):
                    act.wait_ge(ot3_ps, q.n + 1)
                    wait(act, y3_ps, q.back(1))
                    nc.scalar.copy(ot3[q.slot % 2][:, :], po1[:, 0:P]).then_inc(ot3_sb, 1)
                if (q := at(0)):
                    s = q.slot % 2
                    act.wait_ge(t3_ps, q.n + 1)
                    wait(act, a3_ps, q.back(1))
                    nc.scalar.copy(vt3[s][:, :], p0[0:LD, S:2 * S]).then_inc(vt3_sb, 1)
                    act.wait_ge(low_sb, 2 * q.n + 1)
                    wait(act, tok_sb, q.back(1))
                    nc.scalar.activation(elt[s][:, :], lowt[s][:, :], ACT.Exp).then_inc(el_sb, 1)
                    act.wait_ge(low_sb, 2 * q.n + 2)
                    nc.scalar.activation(el[s][:, :], low[s][:, :], ACT.Exp).then_inc(el_sb, 1)
            sweep(act, 5, step, lead=1)

        def linear_vector(dve, n):
            def step(at):
                at = behind(at, 1)
                if (q := at(2)):
                    s = q.slot % 2
                    dve.wait_ge(o3_ps, q.n + 1)
                    nc.vector.tensor_tensor(o3[s][:, :, :], po0[:, 0:2 * LD].rearrange("p (t d) -> p t d", t=2),
                                            inv3[q.slot][:, :].unsqueeze(2).to_broadcast([P, 2, LD]),
                                            ALU.mult).then_inc(o3_sb, 1)
                if (q := at(1)):
                    s = q.slot % 2
                    dve.wait_ge(a3_ps, q.n + 1)
                    nc.vector.tensor_tensor(am[s][:, 0:2, :], pt1[:, 0:S].rearrange("p (a b) -> p a b", a=2),
                                            upto[:, :, :], ALU.mult).then_inc(am_sb, 1)
                    nc.vector.tensor_tensor(am[s][:, 2, :], pt1[:, S:S + P], upto[:, 0, :], ALU.mult).then_inc(am_sb, 1)
                    dve.wait_ge(z3_ps, q.n + 1)
                    nc.vector.tensor_tensor(zq[s][:, :, :], pm0[:, 0:2 * LD].rearrange("p (t d) -> p t d", t=2),
                                            tok[q.slot][:, :, 0, :], ALU.mult).then_inc(zq_sb, 1)
                    dve.wait_ge(zq_sb, q.n + 1)
                    nc.vector.tensor_reduce(den[s][:, :], zq[s][:, :, :], AX.X, ALU.add).then_inc(den_sb, 1)
                    dve.wait_ge(den_sb, q.n + 1)
                    nc.vector.tensor_scalar(den2[s][:, :], den[s][:, :], 1e-6, None, ALU.max).then_inc(den2_sb, 1)
                    dve.wait_ge(den2_sb, q.n + 1)
                    nc.vector.reciprocal(inv3[q.slot][:, :], den2[s][:, :]).then_inc(inv3_sb, 1)
                    dve.wait_ge(inv3_sb, q.n + 1)
                if (q := at(0)):
                    s = q.slot % 2
                    dve.wait_ge(t3_ps, q.n + 1)
                    wait(dve, el_sb, 2 * (q.back(1)))
                    nc.vector.tensor_scalar(lowt[s][:, :], p1[0:LD, 0:S], 0.0, None, ALU.min).then_inc(low_sb, 1)
                    dve.wait_ge(tok_ps, q.n + 1)
                    nc.vector.tensor_scalar(low[s][:, :], pt0[:, 0:S], 0.0, None, ALU.min).then_inc(low_sb, 1)
                    dve.wait_ge(el_sb, 2 * q.n + 1)
                    nc.vector.scalar_tensor_tensor(qt3[s][:, :], p1[0:LD, 0:S], 0.0, elt[s][:, :], ALU.max,
                                                   ALU.add).then_inc(qt3_sb, 1)
                    dve.wait_ge(el_sb, 2 * q.n + 2)
                    nc.vector.scalar_tensor_tensor(tok[q.slot][:, :, :, :].rearrange("p a b c -> p (a b c)"),
                                                   pt0[:, 0:S], 0.0, el[s][:, :], ALU.max, ALU.add).then_inc(tok_sb, 1)
                if (q := at(3)):
                    norm_apply(dve, q, n)
                if (q := at(2)):
                    dve.wait_ge(y3_ps, q.n + 1)
                    for t, bank in ((0, pm1), (1, po1)):
                        last = nc.vector.tensor_tensor(res[q.slot][:, t:t + 1, :],
                                                       bank[:, t * P:t * P + P].unsqueeze(1),
                                                       xg[:, bass.ds(2 * q.n + t, 1), :], ALU.add)
                    last.then_inc(res_sb, 1)
                    norm_stats(dve, q, n)
            sweep(dve, 5, step)

        def load_x_routed(sp, g, n, before, each):
            def step(at):
                if (q := at(0)):
                    wait_apart(sp, scattered[q.slot], before // SLOTS + each * q.turn, passed)
                    load_x(sp, q, g, n)
            sweep(sp, 3, step)

        def load_x_only(sp, lags, g, n):
            def step(at):
                if (q := at(0)):
                    load_x(sp, q, g, n)
            sweep(sp, lags, step)

        xs0 = nc.dram_tensor("sorted0", (E0 * ROOM0 + 8 * S, D), F32).ap()
        ys0 = nc.dram_tensor("result0", (NG * S, D), F32).ap()
        xs3 = nc.dram_tensor("sorted3", (E3 * CAP3 + SEQS * S, D), F32).ap()
        ys3 = nc.dram_tensor("result3", (E3 * CAP3, D), F32).ap()
        DUMP = E3 * CAP3

        lg_ps, lg_sb, seen_sb, top_sb, topi_sb, topf_sb = (sem(s) for s in (
            "lg_ps", "lg_sb", "seen_sb", "top_sb", "topi_sb", "topf_sb"))
        oh_sb, sel_sb, rank_ps, rank_sb, pick_sb, pl_sb = (sem(s) for s in (
            "oh_sb", "sel_sb", "rank_ps", "rank_sb", "pick_sb", "pl_sb"))
        gap_sb, eg_sb, wt_sb, place_sb = (sem(s) for s in (
            "gap_sb", "eg_sb", "wt_sb", "place_sb"))
        zeroed = sem("zeroed")
        scattered = [sem(f"scattered{i}") for i in range(SLOTS)]

        def route_tensor(pe, a, g, E, rw):
            def step(at):
                if (q := at(0)):
                    wait(pe, xt_sb, g + q.n)
                    transpose_x(pe, q, g)
                if (q := at(1)):
                    ranks_tensor(pe, q, a, E, pt0)
                if (q := at(0)):
                    pe.wait_ge(xt_sb, g + q.n + 1)
                    wait(pe, lg_sb, a + q.n)
                    for t in range(2):
                        last = pe.matmul(p1[:, t * E:t * E + E], xt[q.slot][:, 1 + t * P:1 + t * P + P], rw[:, :],
                                         start=True, stop=True)
                    last.then_inc(lg_ps, 1)
            sweep(pe, 3, step)

        def route_scalar(act, a, g, E):
            def step(at):
                if (q := at(0)):
                    copy_xt(act, q, g)
                if (q := at(1)):
                    exp_gaps(act, q, a, E)
            sweep(act, 3, step)

        def choose(dve, q, a, E, choices, part):
            s, k = q.slot % 2, a + q.n
            if part == 0:
                dve.wait_ge(lg_ps, k + 1)
                nc.vector.tensor_copy(lg[s][:, :, 0:E], p1[:, 0:2 * E].rearrange("p (t e) -> p t e", t=2)
                                      ).then_inc(lg_sb, 1)
            elif part == 1:
                wait_apart(dve, lg_sb, k + 1, passed)
                for t in range(2):
                    nc.vector.max(top[s][:, t, :], lg[s][:, t, 0:E]).then_inc(top_sb, 1)
            elif part == 2:
                for t in range(2):
                    wait_apart(dve, top_sb, 2 * k + 1 + t, passed)
                    nc.vector.max_index(topi[s][:, t, :], top[s][:, t, :], lg[s][:, t, 0:E]).then_inc(topi_sb, 1)
            elif part == 3:
                dve.wait_ge(topi_sb, 2 * (k + 1))
                nc.vector.tensor_copy(topf[s][:, :, :], topi[s][:, :, :]).then_inc(topf_sb, 1)
            elif part == 4:
                dve.wait_ge(topf_sb, k + 1)
                for i in range(2):
                    for t in range(2):
                        nc.vector.tensor_scalar(oh[s][:, i, t, 0:E], iota_e[:, 0:E], topf[s][:, t, i:i + 1],
                                                None, ALU.is_equal).then_inc(oh_sb, 1)
            elif part == 5:
                dve.wait_ge(oh_sb, 4 * (k + 1))
                if choices == 2:
                    nc.vector.tensor_tensor(sel[q.slot][:, :, 0:E], oh[s][:, 0, :, 0:E], oh[s][:, 1, :, 0:E],
                                            ALU.add).then_inc(sel_sb, 1)
                else:
                    nc.vector.tensor_copy(sel[q.slot][:, :, 0:E], oh[s][:, 0, :, 0:E]).then_inc(sel_sb, 1)
                wait(dve, eg_sb, k - 1)
                for t in range(2):
                    nc.vector.tensor_scalar(gap[s][:, t, 0:E], lg[s][:, t, 0:E], top[s][:, t, 0:1], None,
                                            ALU.subtract).then_inc(gap_sb, 1)

        def put(dve, q, a, E, choices, base, bank, part):
            s, k = q.slot % 2, a + q.n
            sd = a // SEQS + k
            r = bank.rearrange("p (t e) -> p t e", t=2)
            both = pl[s][:, 0:2, :].rearrange("p a b -> p (a b)")
            w0 = 5 * k if choices == 2 else 5 * SEQS + 7 * q.n
            of_seq = bass.ds(2 * q.n, 2)
            if part == 0:
                dve.wait_ge(seen_sb, sd + 1)
                dve.wait_ge(sel_sb, k + 1)
                nc.vector.tensor_tensor(run[s][:, 0:E], seen[q.slot][:, 0:E], sel[q.slot][:, 0, 0:E],
                                        ALU.add).then_inc(sel2_sb, 1)
            elif part == 1:
                dve.wait_ge(sel2_sb, k + 1)
                nc.vector.tensor_tensor(seen[(q.slot + 1) % SLOTS][:, 0:E], run[s][:, 0:E],
                                        sel[q.slot][:, 1, 0:E], ALU.add).then_inc(seen_sb, 1)
            elif choices == 2:
                e2 = sm[s][:, 0, :]
                if part == 2:
                    dve.wait_ge(rank_ps, k + 1)
                    nc.vector.tensor_tensor(rank[s][:, :, 0:E], r, base[:, :, :], ALU.add).then_inc(rank_sb, 1)
                    dve.wait_ge(eg_sb, k + 1)
                    nc.vector.tensor_tensor(gs[s][:, :, 0:E], eg[s][:, :, 0:E], oh[s][:, 1, :, 0:E],
                                            ALU.mult).then_inc(wt_sb, 1)
                elif part == 3:
                    dve.wait_ge(rank_sb, k + 1)
                    for i in range(2):
                        nc.vector.tensor_tensor(pick[s][:, i, :, 0:E], oh[s][:, i, :, 0:E], rank[s][:, :, 0:E],
                                                ALU.mult).then_inc(pick_sb, 1)
                    dve.wait_ge(wt_sb, w0 + 1)
                    nc.vector.tensor_reduce(e2, gs[s][:, :, 0:E], AX.X, ALU.add).then_inc(wt_sb, 1)
                elif part == 4:
                    dve.wait_ge(pick_sb, 2 * (k + 1))
                    nc.vector.tensor_reduce(both, pick[s][:, :, :, 0:E], AX.X, ALU.add).then_inc(pl_sb, 1)
                    dve.wait_ge(wt_sb, w0 + 2)
                    nc.vector.tensor_scalar(sm[s][:, 1, :], e2, 1.0, None, ALU.add).then_inc(wt_sb, 1)
                elif part == 5:
                    dve.wait_ge(pl_sb, k + 1)
                    wait(dve, scattered[q.slot], 64 * q.turn)
                    nc.vector.tensor_copy(place[q.slot][:, :, :], pl[s][:, 0:2, :]).then_inc(place_sb, 1)
                    nc.vector.tensor_copy(places[:, of_seq, :].rearrange("p t c -> p c t"),
                                          pl[s][:, 0:2, :]).then_inc(places_sb, 1)
                    dve.wait_ge(wt_sb, w0 + 3)
                    nc.vector.reciprocal(weight[:, of_seq, 0:1], sm[s][:, 1, :].unsqueeze(2)).then_inc(wt_sb, 1)
                elif part == 6:
                    dve.wait_ge(wt_sb, w0 + 4)
                    nc.vector.tensor_tensor(weight[:, of_seq, 1:2], e2.unsqueeze(2), weight[:, of_seq, 0:1],
                                            ALU.mult).then_inc(wt_sb, 1)
            else:
                keep, lost, all_e, inv_e = (sm[s][:, i, :] for i in range(4))
                if part == 2:
                    dve.wait_ge(rank_ps, k + 1)
                    nc.vector.tensor_tensor(pick[s][:, 0, :, 0:E], oh[s][:, 0, :, 0:E], r,
                                            ALU.mult).then_inc(rank_sb, 1)
                    nc.vector.tensor_tensor(pick[s][:, 1, :, 0:E], oh[s][:, 0, :, 0:E], base[:, :, :],
                                            ALU.mult).then_inc(pick_sb, 1)
                    dve.wait_ge(eg_sb, k + 1)
                    nc.vector.tensor_reduce(all_e, eg[s][:, :, 0:E], AX.X, ALU.add).then_inc(wt_sb, 1)
                elif part == 3:
                    dve.wait_ge(rank_sb, k + 1)
                    dve.wait_ge(pick_sb, 2 * SEQS + q.n + 1)
                    nc.vector.tensor_reduce(both, pick[s][:, :, :, 0:E], AX.X, ALU.add).then_inc(pl_sb, 1)
                    dve.wait_ge(wt_sb, w0 + 1)
                    nc.vector.reciprocal(inv_e, all_e).then_inc(wt_sb, 1)
                elif part == 4:
                    dve.wait_ge(pl_sb, k + 1)
                    nc.vector.tensor_scalar(keep, pl[s][:, 0, :], float(CAP3), None, ALU.is_le).then_inc(wt_sb, 1)
                    nc.vector.scalar_tensor_tensor(pl[s][:, 2, :], pl[s][:, 0, :], float(CAP3), pl[s][:, 1, :],
                                                   ALU.min, ALU.add).then_inc(wt_sb, 1)
                elif part == 5:
                    dve.wait_ge(wt_sb, w0 + 4)
                    nc.vector.tensor_tensor(lost, pl[s][:, 2, :], dump[:, of_seq], ALU.subtract).then_inc(wt_sb, 1)
                    nc.vector.tensor_copy(places[:, of_seq, 0:1], pl[s][:, 2, :].unsqueeze(2)).then_inc(places_sb, 1)
                    nc.vector.tensor_tensor(weight[:, of_seq, 0:1], inv_e.unsqueeze(2), keep.unsqueeze(2),
                                            ALU.mult).then_inc(wt_sb, 1)
                elif part == 6:
                    dve.wait_ge(wt_sb, w0 + 6)
                    nc.vector.tensor_tensor(pl[s][:, 3, :], lost, keep, ALU.mult).then_inc(wt_sb, 1)
                elif part == 7:
                    dve.wait_ge(wt_sb, w0 + 7)
                    wait(dve, scattered[q.slot], 64 * (SEQS // SLOTS) + 32 * q.turn)
                    nc.vector.tensor_tensor(place[q.slot][:, 0, :], pl[s][:, 3, :], dump[:, of_seq],
                                            ALU.add).then_inc(place_sb, 1)

        def count_from_zero():
            nc.vector.memset(seen[0][:, :], 0.0).then_inc(seen_sb, 1)

        def route_vector(dve, a, E, choices, base):
            count_from_zero()

            def step(at):
                for part in range(8):
                    if (q := at(0)):
                        choose(dve, q, a, E, choices, part)
                    if (q := at(1)):
                        put(dve, q, a, E, choices, base, pt0[:, 0:2 * E], part)
            sweep(dve, 3, step)

        def ranks_tensor(pe, q, a, E, bank):
            pe.wait_ge(sel_sb, a + q.n + 1)
            pe.wait_ge(seen_sb, a // SEQS + a + q.n + 1)
            wait(pe, rank_sb, a + q.n)
            s, before = sel[q.slot], seen[q.slot][:, 0:E]
            pe.matmul(bank[:, 0:E], upto16[:, :], s[:, 0, 0:E], start=True, stop=False)
            pe.matmul(bank[:, 0:E], ones16[:, :], before, start=False, stop=True)
            pe.matmul(bank[:, E:2 * E], upto16[:, :], s[:, 1, 0:E], start=True, stop=False)
            pe.matmul(bank[:, E:2 * E], ones16[:, :], s[:, 0, 0:E], start=False, stop=False)
            pe.matmul(bank[:, E:2 * E], ones16[:, :], before, start=False, stop=True).then_inc(rank_ps, 1)

        def exp_gaps(act, q, a, E):
            s = q.slot % 2
            act.wait_ge(gap_sb, 2 * (a + q.n + 1))
            nc.scalar.activation(eg[s][:, :, 0:E], gap[s][:, :, 0:E], ACT.Exp).then_inc(eg_sb, 1)

        def scatter(pool, q, i, rows_of, rows):
            for t in range(2):
                pool.indirect_dma_start(
                    out=rows, out_offset=bass.IndirectOffsetOnAxis(ap=place[q.slot][:, i, t:t + 1], axis=0),
                    in_=rows_of[q.slot][:, t, :], in_offset=None).then_inc(scattered[q.slot], 16)

        sel2_sb, places_sb = sem("sel2_sb"), sem("places_sb")

        def route_pool(pool, a, choices, rows):
            def step(at):
                if (q := at(2)):
                    wait_apart(pool, place_sb, a + q.n + 1, passed)
                    for i in range(choices):
                        scatter(pool, q, i, xs, rows)
            sweep(pool, 3, step)

        count_f = sb("count_f", [P, E0])
        count_i = sb("count_i", [P, E0], I32)
        up_i = sb("up_i", [P, E0], I32)
        grp_i = sb("grp_i", [P, E0], I32)
        grp = sb("grp", [P, E0])
        cum = sb("cum", [P, E0])
        past = sb("past", [P, NG, E0])
        spent = sb("spent", [P, NG, E0])
        g_e = sb("g_e", [P, NG])
        g_b = sb("g_b", [P, NG])
        g_j = sb("g_j", [P, NG])
        g_o = sb("g_o", [P, NG])
        g_exp = sb("g_exp", [P, NG], I32)
        g_off = sb("g_off", [P, NG], I32)
        delta = sb("delta", [P, E0])
        ends = sb("ends", [P, E0])
        place_f = sb("place_f", [P, 2 * TILES])
        shift = sb("shift", [P, 2 * TILES, E0])
        moved = sb("moved", [P, 2 * TILES])
        count_ps, list_sb = sem("count_ps"), sem("list_sb")
        tails = sem("tails")
        LIST = 16

        def list_tensor(pe):
            pe.wait_ge(seen_sb, SEQS + 1)
            pe.wait_ge(lg_sb, SEQS)
            pe.matmul(p1[:, 0:E0], ones16[:, :], seen[0][:, 0:E0], start=True, stop=True).then_inc(count_ps, 1)

        def list_vector(dve):
            done = [0]

            def chain(ins):
                done[0] += 1
                ins.then_inc(list_sb, 1)
                dve.wait_ge(list_sb, done[0])

            v = nc.vector
            dve.wait_ge(count_ps, 1)
            chain(v.tensor_copy(count_i[:, :], p1[:, 0:E0]))
            chain(v.tensor_scalar(count_f[:, :], p1[:, 0:E0], float(S - 1), None, ALU.add))
            chain(v.tensor_copy(up_i[:, :], count_f[:, :]))
            chain(v.tensor_scalar(grp_i[:, :], up_i[:, :], S.bit_length() - 1, None, ALU.logical_shift_right))
            chain(v.tensor_copy(grp[:, :], grp_i[:, :]))
            chain(v.tensor_tensor_scan(cum[:, :], ones[:, 0:E0], grp[:, :], 0.0, ALU.mult, ALU.add))
            chain(v.tensor_tensor(past[:, :, :], cum[:, :].unsqueeze(1).to_broadcast([P, NG, E0]),
                                  iota_g[:, :].unsqueeze(2).to_broadcast([P, NG, E0]), ALU.is_le))
            chain(v.tensor_reduce(g_e[:, :], past[:, :, :], AX.X, ALU.add))
            chain(v.tensor_tensor(spent[:, :, :], past[:, :, :], grp[:, :].unsqueeze(1).to_broadcast([P, NG, E0]),
                                  ALU.mult))
            chain(v.tensor_reduce(g_b[:, :], spent[:, :, :], AX.X, ALU.add))
            chain(v.tensor_tensor(g_j[:, :], iota_g[:, :], g_b[:, :], ALU.subtract))
            chain(v.tensor_scalar(g_o[:, :], g_j[:, :], float(S), None, ALU.mult))
            chain(v.scalar_tensor_tensor(g_b[:, :], g_e[:, :], float(ROOM0), g_o[:, :], ALU.mult, ALU.add))
            chain(v.tensor_copy(g_off[:, :], g_b[:, :]))
            chain(v.tensor_scalar(g_j[:, :], g_e[:, :], float(E0 - 1), None, ALU.min))
            chain(v.tensor_copy(g_exp[:, :], g_j[:, :]))
            assert done[0] == LIST
            chain(v.tensor_scalar(delta[:, :], grp[:, :], float(S), -float(ROOM0), ALU.mult, ALU.add))
            chain(v.tensor_scalar(ends[:, :], iota_e[:, 0:E0], float(ROOM0), float(ROOM0), ALU.mult, ALU.add))
            flat = places[:, :, :].rearrange("p t c -> p (t c)")
            wide = [P, 2 * TILES, E0]
            chain(v.tensor_copy(place_f[:, :], flat))
            chain(v.tensor_tensor(shift[:, :, :], ends[:, :].unsqueeze(1).to_broadcast(wide),
                                  place_f[:, :].unsqueeze(2).to_broadcast(wide), ALU.is_le))
            chain(v.tensor_tensor(shift[:, :, :], shift[:, :, :], delta[:, :].unsqueeze(1).to_broadcast(wide), ALU.mult))
            chain(v.tensor_reduce(moved[:, :], shift[:, :, :], AX.X, ALU.add))
            chain(v.tensor_tensor(flat, place_f[:, :], moved[:, :], ALU.add))

        def list_sync(sp):
            sp.wait_ge(list_sb, 1)
            for e in range(E0):
                c = sp.value_load(count_i[0:1, e:e + 1], min_val=0, max_val=CAP0)
                sp.dma_start(xs0[bass.ds(c + e * ROOM0, S), :].rearrange("(p r) d -> p (r d)", p=P),
                             zt[:, 0:2 * D]).then_inc(tails, 16)

        W2_AT, B1_AT, B2_AT = F, F + FC * D, F + FC * D + FC
        we = [sb(f"we{i}", [P, B2_AT + 1]) for i in range(SLOTS)]
        xe = [sb(f"xe{i}", [P, 4, D]) for i in range(SLOTS)]
        xet = [sb(f"xet{i}", [P, CAP3]) for i in range(2)]
        he = [sb(f"he{i}", [P, FC, CAP3]) for i in range(2)]
        yt = [sb(f"yt{i}", [P, CAP3]) for i in range(2)]
        ye = [sb(f"ye{i}", [P, 4, D]) for i in range(SLOTS)]
        xet_ps, xet_sb, he_ps, he_sb, yt_ps, yt_sb, ye_ps, ye_sb = (sem(s) for s in (
            "xet_ps", "xet_sb", "he_ps", "he_sb", "yt_ps", "yt_sb", "ye_ps", "ye_sb"))
        grp_in = [sem(f"grp_in{i}") for i in range(SLOTS)]
        grp_out = [sem(f"grp_out{i}") for i in range(SLOTS)]
        IN = 16 * 2

        def pieces(T):
            k = next(k for k in range(1, T) if T % k == 0 and T // k <= P)
            return k, T // k

        def experts_sync(sp, a, first):
            if first:
                sp.wait_ge(tails, 16 * E0)
                sp.wait_ge(zeroed, 16)
                sp.wait_ge(list_sb, LIST)
                for s in scattered:
                    sp.wait_ge(s, 64 * SEQS // SLOTS)
            else:
                for s in scattered:
                    sp.wait_ge(s, (64 + 32) * SEQS // SLOTS)
                sp.wait_ge(zeroed, 32)
            T = S if first else CAP3
            k, m = pieces(T)
            rows_in, rows_out = (xs0, ys0) if first else (xs3, ys3)
            packed, width = (pack0, B2_AT + 1) if first else (pack3, B1_AT)

            def step(at):
                if (q := at(0)):
                    if first:
                        e = sp.value_load(g_exp[0:1, bass.ds(q.n, 1)], min_val=0, max_val=E0 - 1)
                        r = sp.value_load(g_off[0:1, bass.ds(q.n, 1)], min_val=0, max_val=E0 * ROOM0 + 7 * S)
                    else:
                        e, r = q.n, q.n * CAP3
                    wait_apart(sp, yt_sb, a + q.back(3), passed)
                    sp.dma_start(xe[q.slot][0:m, 0:k, :], rows_in[bass.ds(r, T), :].rearrange("(p t) d -> p t d", t=k)
                                 ).then_inc(grp_in[q.slot], 16)
                    sp.dma_start(we[q.slot][:, 0:width], packed[bass.ds(e, 1)].rearrange("e p w -> p (e w)")
                                 ).then_inc(grp_in[q.slot], 16)
                if (q := at(5)):
                    wait_apart(sp, ye_sb, a + q.n + 1, passed)
                    sp.dma_start(rows_out[bass.ds(q.n * T, T), :].rearrange("(p t) d -> p t d", t=k),
                                 ye[q.slot][0:m, 0:k, :]).then_inc(grp_out[q.slot], 16)
            sweep(sp, 6, step, NG if first else E3)

        def experts_tensor(pe, a, T, n):
            hb = [pt0, pt1, pm0, pm1]
            k, m = pieces(T)

            def step(at):
                if (q := at(0)):
                    wait(pe, xet_sb, a + q.n)
                    pe.wait_ge(grp_in[q.slot], IN * (a // SLOTS + q.turn + 1))
                    for i in range(k):
                        last = pe.transpose(p0[:, i * m:i * m + m], xe[q.slot][0:m, i, :], ident[0:m, 0:m])
                    last.then_inc(xet_ps, 1)
                if (q := at(1)):
                    pe.wait_ge(xet_sb, a + q.n + 1)
                    for c in range(FC):
                        wait(pe, he_sb, 4 * (a + q.back(1)) + c + 1)
                        pe.matmul(hb[c][:, 0:T], we[q.slot][:, c * P:c * P + P], xet[q.slot % 2][:, 0:T],
                                  start=True, stop=True).then_inc(he_ps, 1)
                if (q := at(2)):
                    wait(pe, yt_sb, a + q.n)
                    pe.wait_ge(he_sb, 4 * (a + q.n + 1))
                    for c in range(FC):
                        last = pe.matmul(po0[:, 0:T], we[q.slot][:, W2_AT + c * D:W2_AT + c * D + D],
                                         he[q.slot % 2][:, c, 0:T], start=(c == 0), stop=(c == FC - 1))
                    last.then_inc(yt_ps, 1)
                if (q := at(3)):
                    pe.wait_ge(yt_sb, a + q.n + 1)
                    wait(pe, ye_sb, a + q.n)
                    for i in range(k):
                        last = pe.transpose(po1[0:m, i * D:i * D + D], yt[q.slot % 2][:, i * m:i * m + m], ident[:, :])
                    last.then_inc(ye_ps, 1)
            sweep(pe, 4, step, n, lead=0 if a else 1)

        def experts_scalar(act, a, T, n, biased):
            hb = [pt0, pt1, pm0, pm1]

            def step(at):
                if (q := at(1)):
                    wait(act, yt_ps, a + q.back(1))
                    for c in range(FC):
                        act.wait_ge(he_ps, 4 * (a + q.n) + c + 1)
                        nc.scalar.activation(he[q.slot % 2][:, c, 0:T], hb[c][:, 0:T], ACT.Gelu_apprx_tanh,
                                             bias=we[q.slot][:, B1_AT + c:B1_AT + c + 1] if biased else zero_col[:, :]
                                             ).then_inc(he_sb, 1)
            sweep(act, 4, step, n)

        def experts_vector(dve, a, T, n, biased):
            k, m = pieces(T)

            def step(at):
                if (q := at(0)):
                    dve.wait_ge(xet_ps, a + q.n + 1)
                    wait(dve, he_ps, 4 * (a + q.back(1)))
                    nc.vector.tensor_copy(xet[q.slot % 2][:, 0:T], p0[:, 0:T]).then_inc(xet_sb, 1)
                if (q := at(2)):
                    dve.wait_ge(yt_ps, a + q.n + 1)
                    wait(dve, ye_ps, a + q.back(1))
                    if biased:
                        nc.vector.tensor_scalar(yt[q.slot % 2][:, 0:T], po0[:, 0:T], we[q.slot][:, B2_AT:B2_AT + 1],
                                                None, ALU.add).then_inc(yt_sb, 1)
                    else:
                        nc.vector.tensor_copy(yt[q.slot % 2][:, 0:T], po0[:, 0:T]).then_inc(yt_sb, 1)
                if (q := at(3)):
                    dve.wait_ge(ye_ps, a + q.n + 1)
                    wait(dve, grp_out[q.slot], 16 * (a // SLOTS + q.turn))
                    nc.vector.tensor_copy(ye[q.slot][0:m, 0:k, :],
                                          po1[0:m, 0:k * D].rearrange("p (t d) -> p t d", t=k)).then_inc(ye_sb, 1)
            sweep(dve, 4, step, n, lead=0 if a else SLOTS)

        at_row = [sb(f"at_row{i}", [P, 2, 2], U32) for i in range(SLOTS)]
        wrow = [sb(f"wrow{i}", [P, 2, 2]) for i in range(SLOTS)]
        yr = [sb(f"yr{i}", [P, 2, 2, D]) for i in range(SLOTS)]
        part = [sb(f"part{i}", [P, 2, D]) for i in range(2)]
        row_at, wrow_sb, part_sb = (sem(s) for s in ("row_at", "wrow_sb", "part_sb"))
        gathered = [sem(f"gathered{i}") for i in range(SLOTS)]

        def gather_pool(pool, a, choices, rows, outs_done, then=None):
            for s in grp_out:
                pool.wait_ge(s, outs_done // SLOTS)

            def step(at):
                if then:
                    then(behind(at, 6))
                if (q := at(3)):
                    norm_rstd(pool, q, a, mixed)
                if (q := at(1)):
                    pool.wait_ge(row_at, a + q.n + 1)
                    wait_apart(pool, mixed.res_sb, a + q.back(3), passed)
                    for t in range(2):
                        for i in range(choices):
                            pool.indirect_dma_start(
                                out=yr[q.slot][:, t, i, :], out_offset=None, in_=rows,
                                in_offset=bass.IndirectOffsetOnAxis(ap=at_row[q.slot][:, t, i:i + 1], axis=0)
                            ).then_inc(gathered[q.slot], 16)
            sweep(pool, 12 if then else 5, step)

        def gather_vector(dve, a, choices, got, then=None):
            def step(at):
                if then:
                    then(behind(at, 6))
                if (q := at(4)):
                    norm_apply(dve, q, a, mixed)
                if (q := at(0)):
                    wait(dve, gathered[q.slot], got // SLOTS + 32 * choices * q.turn)
                    nc.vector.tensor_copy(at_row[q.slot][:, :, 0:choices],
                                          places[:, bass.ds(2 * q.n, 2), 0:choices]).then_inc(row_at, 1)
                    nc.vector.tensor_copy(wrow[q.slot][:, :, 0:choices],
                                          weight[:, bass.ds(2 * q.n, 2), 0:choices]).then_inc(wrow_sb, 1)
                if (q := at(2)):
                    dve.wait_ge(wrow_sb, a + q.n + 1)
                    dve.wait_ge(gathered[q.slot], got // SLOTS + 32 * choices * (q.turn + 1))
                    src = xg[:, bass.ds(2 * q.n, 2), :]
                    if choices == 2:
                        for t in range(2):
                            nc.vector.scalar_tensor_tensor(part[q.slot % 2][:, t:t + 1, :], yr[q.slot][:, t, 0:1, :],
                                                           wrow[q.slot][:, t, 0:1], src[:, t:t + 1, :],
                                                           ALU.mult, ALU.add).then_inc(part_sb, 1)
                        dve.wait_ge(part_sb, 2 * (q.n + 1))
                        src = part[q.slot % 2][:, :, :]
                    for t in range(2):
                        last = nc.vector.scalar_tensor_tensor(mixed.res[q.slot][:, t:t + 1, :],
                                                              yr[q.slot][:, t, choices - 1:choices, :],
                                                              wrow[q.slot][:, t, choices - 1:choices],
                                                              src[:, t:t + 1, :], ALU.mult, ALU.add)
                    last.then_inc(mixed.res_sb, 1)
                    norm_stats(dve, q, a, mixed)
            sweep(dve, 12 if then else 5, step)

        def store_out(sp, n):
            def step(at):
                if (q := at(4)):
                    sp.wait_ge(mixed.ln_x, 2 * (n + q.n + 1))
                    sp.dma_start(out[bass.ds(2 * q.n, 2)].rearrange("t p d -> p t d"),
                                 xg[:, bass.ds(2 * q.n, 2), :]).then_inc(out_done, 16)
            sweep(sp, 5, step)
            sp.wait_ge(out_done, 16 * SEQS)

        N = SEQS
        CONSTS_V = 4 * SLOTS + 1
        block = ctx.enter_context(nc.Block())

        @block.sync
        def _(sp):
            sp.dma_start(xg[:, 0:2 * FIRST, :], x[0:2 * FIRST].rearrange("t p d -> p t d")).then_inc(x_first, 16)
            sp.dma_start(wm[:, :, :], mats.rearrange("p (m d) -> p m d", d=D)).then_inc(w_in, 16)
            sp.dma_start(cv[:, :], cols).then_inc(w_in, 16)
            sp.dma_start(row1[:, :], rows).then_inc(w_in, 16)
            sp.dma_start(rw0[:, :], router0).then_inc(w_in, 16)
            sp.dma_start(rw3[:, :], gate).then_inc(w_in, 16)
            sp.dma_start(wl[:, :, :], w_l3.rearrange("p (m d) -> p m d", d=LD)).then_inc(w_in, 16)
            for t in range(2):
                sp.dma_start(wo[t * LD:t * LD + LD, :], wo_l3).then_inc(w_in, 16)
            sp.dma_start(xg[:, 2 * FIRST:, :], x[2 * FIRST:].rearrange("t p d -> p t d")).then_inc(x_in, 16)
            heads_sync(sp, 0, 0, 0, True)
            sp.wait_ge(consts, CONSTS)
            sp.dma_start(xs0[E0 * ROOM0:E0 * ROOM0 + 8 * S, :].rearrange("(e p r) d -> p e (r d)", p=P, e=8),
                         zt[:, 0:2 * D].unsqueeze(1).to_broadcast([P, 8, 2 * D])).then_inc(zeroed, 16)
            list_sync(sp)
            experts_sync(sp, 0, True)
            sp.dma_start(xs3[0:E3 * CAP3, :].rearrange("n d -> (n d)").rearrange("(e p k) -> p e k", p=P, e=E3),
                         zt[:, :].unsqueeze(1).to_broadcast([P, E3, CAP3])).then_inc(zeroed, 16)
            load_x_only(sp, 4, N, "mixed")
            load_x_only(sp, 4, 2 * N, 2 * N)
            heads_sync(sp, N, 3 * N, 3 * N, False)
            load_x_only(sp, 4, 4 * N, 4 * N)
            load_x_only(sp, 4, 5 * N, 5 * N)
            load_x_routed(sp, 6 * N, 6 * N, 64 * N, 32)
            experts_sync(sp, NG, False)
            store_out(sp, N)

        @block.tensor
        def _(pe):
            pe.wait_ge(w_in, W_IN)
            pe.wait_ge(consts, CONSTS)
            pe.wait_ge(consts_v, CONSTS_V)
            pe.matmul(po0[:, 0:3 * D], ones[0:1, :], row1[:, :], start=True, stop=True).then_inc(rows_ps, 1)
            pe.wait_ge(rows_sb, len(ROWS))
            heads_tensor(pe, 0, 0, False, 0, True)
            list_tensor(pe)
            experts_tensor(pe, 0, S, NG)
            single_tensor(pe, N, N)
            mixing_tensor(pe, 0, 2 * N, 1)
            heads_tensor(pe, N, 3 * N, True, 2, False)
            mixing_tensor(pe, N, 4 * N, 2)
            linear_tensor(pe, 5 * N, 5 * N)
            route_tensor(pe, N, 6 * N, E3, rw3)
            experts_tensor(pe, NG, CAP3, E3)

        @block.scalar
        def _(act):
            heads_scalar(act, 0, 0, False, True)
            experts_scalar(act, 0, S, NG, True)
            single_scalar(act, N)
            mixing_scalar(act, 0, 2 * N, 1)
            heads_scalar(act, N, 3 * N, True, False)
            mixing_scalar(act, N, 4 * N, 2)
            linear_scalar(act, 5 * N)
            route_scalar(act, N, 6 * N, E3)
            experts_scalar(act, NG, CAP3, E3, False)

        @block.vector
        def _(dve):
            for i in range(SLOTS):
                nc.vector.memset(va[i][:, :, :, DH:DH + 1], 1.0).then_inc(consts_v, 1)
                nc.vector.memset(va[i][:, :, :, DH + 1:], 0.0).then_inc(consts_v, 1)
                nc.vector.memset(xt[i][:, 0:1], 0.0).then_inc(consts_v, 1)
                nc.vector.memset(ks[i][MAX_AT:MAX_AT + 3, :, :].rearrange("p h k -> p (h k)").bitcast(F32),
                                 float(np.uint32(0x3F803F80).view(np.float32))).then_inc(consts_v, 1)
            dve.wait_ge(w_in, W_IN)
            nc.vector.tensor_scalar(omu[:, :], cv[:, COLS.index("mr1"):COLS.index("mr1") + 4], -1.0, 1.0,
                                    ALU.mult, ALU.add).then_inc(consts_v, 1)
            dve.wait_ge(rows_ps, 1)
            for i in range(len(ROWS)):
                nc.vector.tensor_copy(rowb[:, i, :], po0[:, i * D:i * D + D]).then_inc(rows_sb, 1)
            dve.wait_ge(rows_sb, len(ROWS))
            dve.wait_ge(consts_v, CONSTS_V)
            dve.wait_ge(x_first, 16)
            dve.wait_ge(x_in, 16)
            count_from_zero()
            heads_vector(dve, 0, 0, False, 0, True)
            list_vector(dve)
            experts_vector(dve, 0, S, NG, True)
            gather_vector(dve, 0, 2, 0, then=single_vector(dve, N))
            mixing_vector(dve, 0, 2 * N, 2 * N, 1)
            heads_vector(dve, N, 3 * N, True, 2, False)
            mixing_vector(dve, N, 4 * N, 4 * N, 2)
            linear_vector(dve, 5 * N)
            dve.wait_ge(wt_sb, 5 * N)
            route_vector(dve, N, E3, 1, base3)
            experts_vector(dve, NG, CAP3, E3, False)
            gather_vector(dve, N, 1, 64 * N)

        @block.gpsimd
        def _(pool):
            g = nc.gpsimd
            for t, v in ((ident, 0.0), (ones, 1.0), (upto, 1.0), (hide_k, 0.0), (hide_q, 0.0), (half, -0.5),
                         (zt, 0.0), (zero_col, 0.0), (ones16, 1.0), (upto16, 1.0), (ident16, 0.0)):
                g.memset(t[tuple([slice(None)] * len(t.shape))], v).then_inc(cleared, 1)
            pool.wait_ge(cleared, 11)
            for t in (ident, ident16):
                g.affine_select(out=t[:, :], in_=t[:, :], compare_op=ALU.not_equal, fill=1.0, base=0,
                                pattern=[[-1, P]], channel_multiplier=1).then_inc(consts, 1)
            for t in (upto[:, 0, :], upto16[:, :]):
                g.affine_select(out=t, in_=t, compare_op=ALU.is_ge, fill=0.0, base=0,
                                pattern=[[1, P]], channel_multiplier=-1).then_inc(consts, 1)
            g.affine_select(out=hide_k[:, :], in_=hide_k[:, :], compare_op=ALU.is_ge, fill=HIDE, base=0,
                            pattern=[[1, P]], channel_multiplier=-1).then_inc(consts, 1)
            g.affine_select(out=hide_q[:, :], in_=hide_q[:, :], compare_op=ALU.is_ge, fill=HIDE, base=0,
                            pattern=[[-1, P]], channel_multiplier=1).then_inc(consts, 1)
            ig = {"allow_small_or_imprecise_dtypes": True}
            g.iota(iota_e[:, :], [[1, EM]], base=0, channel_multiplier=0, **ig).then_inc(consts, 1)
            g.iota(iota_g[:, :], [[1, NG]], base=0, channel_multiplier=0, **ig).then_inc(consts, 1)
            g.iota(dump[:, :], [[P, TILES]], base=DUMP, channel_multiplier=1, **ig).then_inc(consts, 1)
            g.iota(base0[:, :, :], [[0, 2], [ROOM0, E0]], base=-1, channel_multiplier=0, **ig).then_inc(consts, 1)
            g.iota(base3[:, :, :], [[0, 2], [CAP3, E3]], base=-1, channel_multiplier=0, **ig).then_inc(consts, 1)
            heads_pool(pool, 0, 0, 0, True)
            gather_pool(pool, 0, 2, ys0, 16 * NG, then=lambda at: (q := at(4)) and norm_rstd(pool, q, N))
            mixing_pool(pool, 0, 2 * N)
            heads_pool(pool, N, 3 * N, 2, False)
            mixing_pool(pool, N, 4 * N)
            norm_pool(pool, 5 * N, 5, 3)
            route_pool(pool, N, 1, xs3)
            gather_pool(pool, N, 1, ys3, 16 * (NG + E3))


_INS = ["x", "mats", "cols", "rows", "router0", "pack0", "w_l3", "wo_l3", "gate", "pack3"]


def kernel(**inputs):
    import numpy as _np
    import concourse.bacc as _bacc
    from concourse import mybir as _mybir
    from concourse.bass_utils import run_bass_kernel_spmd as _run

    a = {k: _np.asarray(v) for k, v in inputs.items()}

    def turned(w):
        return w.T

    def by_dim(w):
        return w.reshape(HEADS, DH, D).transpose(1, 0, 2).reshape(D, D).T

    def col_by_dim(b):
        return b.reshape(HEADS, DH).T.reshape(D)

    def by_chunk(w):
        return w.reshape(-1, FC, P, D).transpose(0, 2, 1, 3).reshape(-1, P, FC * D)

    w1 = a["L1_attn_W"]
    b1 = a["L1_attn_b"]
    mats = [by_dim(a["L0_attn_Wq"]), by_dim(a["L0_attn_Wk"]), turned(a["L0_attn_Wv"]), turned(a["L0_attn_Wo"]),
            turned(w1[0:D]), turned(w1[D:2 * D]), turned(w1[2 * D:3 * D]),
            turned(a["L1_ffn_W_r"]), turned(a["L1_ffn_W_k"]), turned(a["L1_ffn_W_v"]),
            by_dim(a["L2_attn_Wq"]), by_dim(a["L2_attn_Wk"]), turned(a["L2_attn_Wv"]), turned(a["L2_attn_Wo"]),
            turned(a["L2_ffn_W_r"]), turned(a["L2_ffn_W_k"]), turned(a["L2_ffn_W_v"])]
    cols = [col_by_dim(a["L0_attn_bq"]), col_by_dim(a["L0_attn_bk"]), b1[0:D], b1[D:2 * D],
            a["L1_ffn_mu_r"], a["L1_ffn_mu_k"], a["L2_ffn_mu_r"], a["L2_ffn_mu_k"]]
    laid = {
        "x": a["L0_attn_x"].reshape(TILES, P, D),
        "mats": _np.concatenate(mats, axis=1),
        "cols": _np.stack(cols, axis=1),
        "rows": _np.concatenate([a["L0_attn_bv"], a["L0_attn_bo"], b1[2 * D:3 * D]]).reshape(1, 3 * D),
        "router0": a["L0_ffn_router_w"],
        "pack0": _np.concatenate([a["L0_ffn_w1"], by_chunk(a["L0_ffn_w2"]),
                                  a["L0_ffn_b1"].reshape(E0, FC, P).transpose(0, 2, 1),
                                  a["L0_ffn_b2"].reshape(E0, D, 1)], axis=2),
        "w_l3": _np.concatenate([a["L3_attn_W_q"], a["L3_attn_W_k"], a["L3_attn_W_v"]], axis=1),
        "wo_l3": a["L3_attn_W_o"],
        "gate": a["L3_ffn_gate_w"].T,
        "pack3": _np.concatenate([a["L3_ffn_w1"], by_chunk(a["L3_ffn_w2"])], axis=2),
    }
    nc = _bacc.Bacc("TRN2", target_bir_lowering=False, num_devices=1)
    arrays, args = {}, []
    for name in _INS:
        v = _np.ascontiguousarray(laid[name])
        arrays[f"in_{name}"] = v
        args.append(nc.dram_tensor(f"in_{name}", v.shape, _mybir.dt.from_np(v.dtype), kind="ExternalInput").ap())
    args.append(nc.dram_tensor("out_x", (TILES, P, D), F32, kind="ExternalOutput").ap())
    post_norm_stack(nc, *args)
    r = _run(nc, [arrays], core_ids=[0])
    return r.results[0]["out_x"].reshape(SEQS, S, D)
```
